# Optimizing a Trainium2 kernel written in Bass

```python
import numpy as np
import jax
import jax.numpy as jnp

def _softmax(x, axis=-1):
    return jax.nn.softmax(x, axis=axis)

def _gelu(x):
    return jax.nn.gelu(x, approximate=True)

def _silu(x):
    return jax.nn.silu(x)

def _sigmoid(x):
    return jax.nn.sigmoid(x)

def _layernorm(x, axis=-1, eps=1e-05):
    m = jnp.mean(x, axis=axis, keepdims=True)
    v = jnp.var(x, axis=axis, keepdims=True)
    return (x - m) / jnp.sqrt(v + eps)

def _scatter_add(tgt, idx, src, axis=0):
    return tgt.at[idx].add(src)

def _segment_sum(src, seg, n):
    return jax.ops.segment_sum(src, seg, n)
kernel_name = 'mk_decoder_postln_d1_seqx_r8_594264'

def setup_inputs(seed: int=0):
    np.random.seed(seed)
    _w = jnp.asarray

    def _rec_inputs():
        import jax
        import jax.numpy as jnp
        _rk = jax.random.key(seed)
        x = -0.0005146 + 1 * jax.random.normal(jax.random.fold_in(_rk, 1), (2, 256, 128), jnp.float32)
        _lenS = 256 - jax.random.randint(jax.random.fold_in(_rk, 7), (2,), 0, max(1, 256 // 4) + 1, jnp.int32)
        _lenS2 = 512 - jax.random.randint(jax.random.fold_in(_rk, 8), (2,), 0, max(1, 512 // 4) + 1, jnp.int32)
        _ctx_1024P = jax.random.normal(jax.random.fold_in(_rk, 11), (2, 16, 128), jnp.float32)
        _ctx_1024c = jax.random.dirichlet(jax.random.fold_in(_rk, 511), 0.3 * jnp.ones((16,), jnp.float32), (2, 512))
        _ctx_1024t = jnp.einsum('bsk,bkd->bsd', _ctx_1024c, _ctx_1024P)
        _ctx_1024t = _ctx_1024t * jax.lax.rsqrt(jnp.mean(jnp.square(_ctx_1024t)) + 1e-12) * 0.953939
        ctx_1024 = -0.000125008 + 0.999885 * (_ctx_1024t + 0.3 * jax.random.normal(jax.random.fold_in(_rk, 611), (2, 512, 128), jnp.float32))
        return (x, ctx_1024)
    x, ctx_1024 = _rec_inputs()

    def _L0_attn_setup():
        import jax, jax.numpy as jnp
        import numpy as np
        HEAD_NUM = 16
        NEG_BIG = 1000000.0
        key = jax.random.key(seed)
        ks = jax.random.split(key, 5)
        E = 128
        B, S = (1, 512)
        x = jax.random.normal(ks[0], (B, S, E), dtype=jnp.float32)
        W1 = jax.random.normal(ks[1], (E, 3 * E), dtype=jnp.float32) * (1.0 / np.sqrt(E))
        b1 = jax.random.normal(ks[2], (3 * E,), dtype=jnp.float32) * 0.02
        Wp = jax.random.normal(ks[3], (E, E), dtype=jnp.float32) * (1.0 / np.sqrt(E))
        bp = jax.random.normal(ks[4], (E,), dtype=jnp.float32) * 0.02
        return {'x': x, 'W1': W1, 'b1': b1, 'Wp': Wp, 'bp': bp}
    _L0_attn_all = _L0_attn_setup()
    _L0_attn_in = {k: v for k, v in _L0_attn_all.items() if k in ('W1', 'b1', 'Wp', 'bp')}
    del _L0_attn_all

    def _L0_xattn_setup():
        import jax, jax.numpy as jnp
        import numpy as np
        DIM = 128
        HEADS = 16
        DIM_HEAD = 64
        INNER = HEADS * DIM_HEAD
        EPS = 1e-05

        def layer_norm(x, gamma, beta):
            mu = jnp.mean(x, axis=-1, keepdims=True)
            var = jnp.mean(jnp.square(x - mu), axis=-1, keepdims=True)
            return (x - mu) * jax.lax.rsqrt(var + EPS) * gamma + beta
        key = jax.random.key(seed)
        ks = jax.random.split(key, 6)
        b, n1, n2 = (8, 512, 32)
        x = jax.random.normal(ks[0], (b, n1, DIM), dtype=jnp.float32)
        latents = jax.random.normal(ks[1], (b, n2, DIM), dtype=jnp.float32)
        s = 1.0 / np.sqrt(DIM)
        Wq = jax.random.normal(ks[2], (DIM, INNER), dtype=jnp.float32) * s
        Wkv = jax.random.normal(ks[3], (DIM, 2 * INNER), dtype=jnp.float32) * s
        Wout = jax.random.normal(ks[4], (INNER, DIM), dtype=jnp.float32) * (1.0 / np.sqrt(INNER))
        g1 = jnp.ones((DIM,), jnp.float32)
        b1 = jnp.zeros((DIM,), jnp.float32)
        g2 = jnp.ones((DIM,), jnp.float32)
        b2 = jnp.zeros((DIM,), jnp.float32)
        return {'x': x, 'latents': latents, 'g1': g1, 'b1': b1, 'g2': g2, 'b2': b2, 'Wq': Wq, 'Wkv': Wkv, 'Wout': Wout}
    _L0_xattn_all = _L0_xattn_setup()
    _L0_xattn_in = {k: v for k, v in _L0_xattn_all.items() if k in ('g1', 'b1', 'g2', 'b2', 'Wq', 'Wkv', 'Wout')}
    del _L0_xattn_all

    def _L0_ffn_setup():
        import jax, jax.numpy as jnp
        import numpy as np
        DIM = 128
        NQ = 16
        NKV = 4
        HD = DIM // NQ
        HID = 256
        E = 8
        B, S = (1, 128)
        EPS = 1e-06

        def rmsnorm(x, w):
            ms = jnp.mean(x * x, axis=-1, keepdims=True)
            return w * (x * jax.lax.rsqrt(ms + EPS))

        def rope_tables(seq_len, head_dim):
            inv_freq = 1.0 / 10000.0 ** (jnp.arange(0, head_dim, 2, dtype=jnp.float32) / head_dim)
            t = jnp.arange(seq_len, dtype=jnp.float32)
            freqs = jnp.einsum('i,j->ij', t, inv_freq)
            return (jnp.cos(freqs), jnp.sin(freqs))

        def apply_rope(x, cos, sin):
            c = cos[None, :, None, :]
            s = sin[None, :, None, :]
            half = x.shape[-1] // 2
            x1, x2 = (x[..., :half], x[..., half:])
            return jnp.concatenate([x1 * c - x2 * s, x1 * s + x2 * c], axis=-1)

        def _forward(x, ln1_w, ln2_w, Wq, bq, Wk, bk, Wv, bv, qn_w, kn_w, Wg, bg, Wo, bo, Wr, br, W1, b1, W2, b2):
            batch, seq, _ = x.shape
            cos, sin = rope_tables(seq, HD)
            h = rmsnorm(x, ln1_w)
            q = (h @ Wq + bq).reshape(batch, seq, NQ, HD)
            k = (h @ Wk + bk).reshape(batch, seq, NKV, HD)
            v = (h @ Wv + bv).reshape(batch, seq, NKV, HD)
            q = rmsnorm(apply_rope(q, cos, sin), qn_w)
            k = rmsnorm(apply_rope(k, cos, sin), kn_w)
            rep = NQ // NKV
            k = jnp.repeat(k, rep, axis=2)
            v = jnp.repeat(v, rep, axis=2)
            scores = jnp.einsum('bthd,bshd->bhts', q, k) / np.sqrt(HD)
            causal = jnp.tril(jnp.ones((seq, seq), dtype=bool))
            scores = jnp.where(causal[None, None], scores, -jnp.inf)
            attn = jax.nn.softmax(scores, axis=-1)
            out = jnp.einsum('bhts,bshd->bthd', attn, v)
            gate = jax.nn.sigmoid(out @ Wg + bg)
            out = (out * gate).reshape(batch, seq, DIM)
            x = x + out @ Wo + bo
            h2 = rmsnorm(x, ln2_w)
            logits = h2 @ Wr + br
            top1 = jnp.argmax(logits, axis=-1).reshape(-1)
            xt = h2.reshape(-1, DIM)
            u = jnp.einsum('td,edf->tef', xt, W1) + b1
            u1, u2 = (u[..., :HID], u[..., HID:])
            act = u1 * jax.nn.sigmoid(u2)
            y_all = jnp.einsum('teh,ehd->ted', act, W2) + b2
            y = jnp.take_along_axis(y_all, top1[:, None, None], axis=1)[:, 0, :]
            return x + y.reshape(batch, seq, DIM)
        key = jax.random.key(seed)
        ks = jax.random.split(key, 20)
        sc = lambda fan_in: 1.0 / np.sqrt(fan_in)
        d = {}
        d['x'] = jax.random.normal(ks[0], (B, S, DIM), dtype=jnp.float32)
        d['ln1_w'] = jnp.ones((DIM,), jnp.float32)
        d['ln2_w'] = jnp.ones((DIM,), jnp.float32)
        d['Wq'] = jax.random.normal(ks[1], (DIM, DIM), jnp.float32) * sc(DIM)
        d['bq'] = jnp.zeros((DIM,), jnp.float32)
        d['Wk'] = jax.random.normal(ks[2], (DIM, HD * NKV), jnp.float32) * sc(DIM)
        d['bk'] = jnp.zeros((HD * NKV,), jnp.float32)
        d['Wv'] = jax.random.normal(ks[3], (DIM, HD * NKV), jnp.float32) * sc(DIM)
        d['bv'] = jnp.zeros((HD * NKV,), jnp.float32)
        d['qn_w'] = jnp.ones((HD,), jnp.float32)
        d['kn_w'] = jnp.ones((HD,), jnp.float32)
        d['Wg'] = jax.random.normal(ks[4], (HD, HD), jnp.float32) * sc(HD)
        d['bg'] = jnp.zeros((HD,), jnp.float32)
        d['Wo'] = jax.random.normal(ks[5], (DIM, DIM), jnp.float32) * sc(DIM)
        d['bo'] = jnp.zeros((DIM,), jnp.float32)
        d['Wr'] = jax.random.normal(ks[6], (DIM, E), jnp.float32) * sc(DIM)
        d['br'] = jnp.zeros((E,), jnp.float32)
        d['W1'] = jax.random.normal(ks[7], (E, DIM, 2 * HID), jnp.float32) * sc(DIM)
        d['b1'] = jnp.zeros((E, 2 * HID), jnp.float32)
        d['W2'] = jax.random.normal(ks[8], (E, HID, DIM), jnp.float32) * sc(HID)
        d['b2'] = jnp.zeros((E, DIM), jnp.float32)
        return d
    _L0_ffn_all = _L0_ffn_setup()
    _L0_ffn_in = {k: v for k, v in _L0_ffn_all.items() if k in ('ln1_w', 'ln2_w', 'Wq', 'bq', 'Wk', 'bk', 'Wv', 'bv', 'qn_w', 'kn_w', 'Wg', 'bg', 'Wo', 'bo', 'Wr', 'br', 'W1', 'b1', 'W2', 'b2')}
    del _L0_ffn_all
    return {'x': x, 'ctx_1024': ctx_1024, 'L0_attn_W1': _L0_attn_in['W1'], 'L0_attn_b1': _L0_attn_in['b1'], 'L0_attn_Wp': _L0_attn_in['Wp'], 'L0_attn_bp': _L0_attn_in['bp'], 'L0_xattn_g1': _L0_xattn_in['g1'], 'L0_xattn_b1': _L0_xattn_in['b1'], 'L0_xattn_g2': _L0_xattn_in['g2'], 'L0_xattn_b2': _L0_xattn_in['b2'], 'L0_xattn_Wq': _L0_xattn_in['Wq'], 'L0_xattn_Wkv': _L0_xattn_in['Wkv'], 'L0_xattn_Wout': _L0_xattn_in['Wout'], 'L0_ffn_ln1_w': _L0_ffn_in['ln1_w'], 'L0_ffn_ln2_w': _L0_ffn_in['ln2_w'], 'L0_ffn_Wq': _L0_ffn_in['Wq'], 'L0_ffn_bq': _L0_ffn_in['bq'], 'L0_ffn_Wk': _L0_ffn_in['Wk'], 'L0_ffn_bk': _L0_ffn_in['bk'], 'L0_ffn_Wv': _L0_ffn_in['Wv'], 'L0_ffn_bv': _L0_ffn_in['bv'], 'L0_ffn_qn_w': _L0_ffn_in['qn_w'], 'L0_ffn_kn_w': _L0_ffn_in['kn_w'], 'L0_ffn_Wg': _L0_ffn_in['Wg'], 'L0_ffn_bg': _L0_ffn_in['bg'], 'L0_ffn_Wo': _L0_ffn_in['Wo'], 'L0_ffn_bo': _L0_ffn_in['bo'], 'L0_ffn_Wr': _L0_ffn_in['Wr'], 'L0_ffn_br': _L0_ffn_in['br'], 'L0_ffn_W1': _L0_ffn_in['W1'], 'L0_ffn_b1': _L0_ffn_in['b1'], 'L0_ffn_W2': _L0_ffn_in['W2'], 'L0_ffn_b2': _L0_ffn_in['b2']}

def reference(x, ctx_1024, L0_attn_W1, L0_attn_b1, L0_attn_Wp, L0_attn_bp, L0_xattn_g1, L0_xattn_b1, L0_xattn_g2, L0_xattn_b2, L0_xattn_Wq, L0_xattn_Wkv, L0_xattn_Wout, L0_ffn_ln1_w, L0_ffn_ln2_w, L0_ffn_Wq, L0_ffn_bq, L0_ffn_Wk, L0_ffn_bk, L0_ffn_Wv, L0_ffn_bv, L0_ffn_qn_w, L0_ffn_kn_w, L0_ffn_Wg, L0_ffn_bg, L0_ffn_Wo, L0_ffn_bo, L0_ffn_Wr, L0_ffn_br, L0_ffn_W1, L0_ffn_b1, L0_ffn_W2, L0_ffn_b2):
    import jax
    import jax.numpy as jnp

    def _L0_attn_ref(x, W1, b1, Wp, bp):
        import jax, jax.numpy as jnp
        import numpy as np
        HEAD_NUM = 16
        NEG_BIG = 1000000.0
        B, S, E = x.shape
        H = HEAD_NUM
        d = E // H
        dk = jnp.asarray(d, x.dtype) ** 0.5
        h = x @ W1 + b1
        h = jnp.swapaxes(h.reshape(B, S, H, 3 * d), 1, 2)
        q, k, v = (h[..., :d], h[..., d:2 * d], h[..., 2 * d:])
        w = jnp.einsum('bhqd,bhkd->bhqk', q, k) / dk
        mask = jnp.tril(jnp.ones((S, S), dtype=x.dtype))
        w = jax.nn.softmax(w * mask - (1.0 - mask) * NEG_BIG, axis=-1)
        a = jnp.einsum('bhqk,bhkd->bhqd', w, v)
        a = jnp.swapaxes(a, 1, 2).reshape(B, S, E)
        return a @ Wp + bp

    def _L0_xattn_ref(x, latents, g1, b1, g2, b2, Wq, Wkv, Wout):
        import jax, jax.numpy as jnp
        import numpy as np
        DIM = 128
        HEADS = 16
        DIM_HEAD = 64
        INNER = HEADS * DIM_HEAD
        EPS = 1e-05

        def layer_norm(x, gamma, beta):
            mu = jnp.mean(x, axis=-1, keepdims=True)
            var = jnp.mean(jnp.square(x - mu), axis=-1, keepdims=True)
            return (x - mu) * jax.lax.rsqrt(var + EPS) * gamma + beta
        b, l, _ = latents.shape
        xn = layer_norm(x, g1, b1)
        ln = layer_norm(latents, g2, b2)
        q = ln @ Wq
        kv_input = jnp.concatenate([xn, ln], axis=1)
        kv = kv_input @ Wkv
        k, v = jnp.split(kv, 2, axis=-1)

        def heads(t):
            return t.reshape(t.shape[0], t.shape[1], HEADS, DIM_HEAD).transpose(0, 2, 1, 3)
        q, k, v = (heads(q), heads(k), heads(v))
        scale = 1.0 / np.sqrt(np.sqrt(DIM_HEAD))
        logits = jnp.einsum('bhqd,bhkd->bhqk', q * scale, k * scale)
        w = jax.nn.softmax(logits.astype(jnp.float32), axis=-1).astype(logits.dtype)
        out = jnp.einsum('bhqk,bhkd->bhqd', w, v)
        out = out.transpose(0, 2, 1, 3).reshape(b, l, INNER)
        return out @ Wout

    def _L0_ffn_ref(x, ln1_w, ln2_w, Wq, bq, Wk, bk, Wv, bv, qn_w, kn_w, Wg, bg, Wo, bo, Wr, br, W1, b1, W2, b2):
        import jax, jax.numpy as jnp
        import numpy as np
        DIM = 128
        NQ = 16
        NKV = 4
        HD = DIM // NQ
        HID = 256
        E = 8
        B, S = (1, 128)
        EPS = 1e-06

        def rmsnorm(x, w):
            ms = jnp.mean(x * x, axis=-1, keepdims=True)
            return w * (x * jax.lax.rsqrt(ms + EPS))

        def rope_tables(seq_len, head_dim):
            inv_freq = 1.0 / 10000.0 ** (jnp.arange(0, head_dim, 2, dtype=jnp.float32) / head_dim)
            t = jnp.arange(seq_len, dtype=jnp.float32)
            freqs = jnp.einsum('i,j->ij', t, inv_freq)
            return (jnp.cos(freqs), jnp.sin(freqs))

        def apply_rope(x, cos, sin):
            c = cos[None, :, None, :]
            s = sin[None, :, None, :]
            half = x.shape[-1] // 2
            x1, x2 = (x[..., :half], x[..., half:])
            return jnp.concatenate([x1 * c - x2 * s, x1 * s + x2 * c], axis=-1)

        def _forward(x, ln1_w, ln2_w, Wq, bq, Wk, bk, Wv, bv, qn_w, kn_w, Wg, bg, Wo, bo, Wr, br, W1, b1, W2, b2):
            batch, seq, _ = x.shape
            cos, sin = rope_tables(seq, HD)
            h = rmsnorm(x, ln1_w)
            q = (h @ Wq + bq).reshape(batch, seq, NQ, HD)
            k = (h @ Wk + bk).reshape(batch, seq, NKV, HD)
            v = (h @ Wv + bv).reshape(batch, seq, NKV, HD)
            q = rmsnorm(apply_rope(q, cos, sin), qn_w)
            k = rmsnorm(apply_rope(k, cos, sin), kn_w)
            rep = NQ // NKV
            k = jnp.repeat(k, rep, axis=2)
            v = jnp.repeat(v, rep, axis=2)
            scores = jnp.einsum('bthd,bshd->bhts', q, k) / np.sqrt(HD)
            causal = jnp.tril(jnp.ones((seq, seq), dtype=bool))
            scores = jnp.where(causal[None, None], scores, -jnp.inf)
            attn = jax.nn.softmax(scores, axis=-1)
            out = jnp.einsum('bhts,bshd->bthd', attn, v)
            gate = jax.nn.sigmoid(out @ Wg + bg)
            out = (out * gate).reshape(batch, seq, DIM)
            x = x + out @ Wo + bo
            h2 = rmsnorm(x, ln2_w)
            logits = h2 @ Wr + br
            top1 = jnp.argmax(logits, axis=-1).reshape(-1)
            xt = h2.reshape(-1, DIM)
            u = jnp.einsum('td,edf->tef', xt, W1) + b1
            u1, u2 = (u[..., :HID], u[..., HID:])
            act = u1 * jax.nn.sigmoid(u2)
            y_all = jnp.einsum('teh,ehd->ted', act, W2) + b2
            y = jnp.take_along_axis(y_all, top1[:, None, None], axis=1)[:, 0, :]
            return x + y.reshape(batch, seq, DIM)
        return _forward(x, ln1_w, ln2_w, Wq, bq, Wk, bk, Wv, bv, qn_w, kn_w, Wg, bg, Wo, bo, Wr, br, W1, b1, W2, b2)
    x = _layernorm(x + _L0_attn_ref(x, L0_attn_W1, L0_attn_b1, L0_attn_Wp, L0_attn_bp), axis=-1)
    x = _layernorm(x + _L0_xattn_ref(ctx_1024, x, L0_xattn_g1, L0_xattn_b1, L0_xattn_g2, L0_xattn_b2, L0_xattn_Wq, L0_xattn_Wkv, L0_xattn_Wout), axis=-1)
    x = _layernorm(x + _L0_ffn_ref(x, L0_ffn_ln1_w, L0_ffn_ln2_w, L0_ffn_Wq, L0_ffn_bq, L0_ffn_Wk, L0_ffn_bk, L0_ffn_Wv, L0_ffn_bv, L0_ffn_qn_w, L0_ffn_kn_w, L0_ffn_Wg, L0_ffn_bg, L0_ffn_Wo, L0_ffn_bo, L0_ffn_Wr, L0_ffn_br, L0_ffn_W1, L0_ffn_b1, L0_ffn_W2, L0_ffn_b2), axis=-1)
    return x

_drawn_inputs = setup_inputs


def setup_inputs(seed=0):
    import zlib

    import numpy as np

    out = dict(_drawn_inputs(seed))
    spreads = {'L0_xattn_g1': (1.0, 0.2),
     'L0_xattn_b1': (0.0, 0.1),
     'L0_xattn_g2': (1.0, 0.2),
     'L0_xattn_b2': (0.0, 0.1),
     'L0_ffn_ln1_w': (1.0, 0.2),
     'L0_ffn_ln2_w': (1.0, 0.2),
     'L0_ffn_bq': (0.0, 0.1),
     'L0_ffn_bk': (0.0, 0.1),
     'L0_ffn_bv': (0.0, 0.1),
     'L0_ffn_qn_w': (1.0, 0.2),
     'L0_ffn_kn_w': (1.0, 0.2),
     'L0_ffn_bg': (0.0, 0.1),
     'L0_ffn_bo': (0.0, 0.1),
     'L0_ffn_br': (0.0, 0.1),
     'L0_ffn_b1': (0.0, 0.283),
     'L0_ffn_b2': (0.0, 0.1)}
    factors = {}
    for name, (base, spread) in spreads.items():
        noise = np.random.default_rng([zlib.crc32(name.encode()), seed]).standard_normal(out[name].shape)
        drawn = base * np.exp(spread * noise) if base else spread * noise
        out[name] = jnp.asarray(drawn.astype(out[name].dtype))
    for name, factor in factors.items():
        out[name] = (out[name] * factor).astype(out[name].dtype)
    return out
```

```python
import concourse.bass as bass
from concourse import mybir
from contextlib import ExitStack

F = mybir.dt.float32
R = mybir.dt.float32r
ACT = mybir.ActivationFunctionType
ALU = mybir.AluOpType
X = mybir.AxisListType.X

P = 128
NEG = -2.0 ** 100
KB = 1024

B, S, D, SC = 2, 256, 128, 512
NT = B * S // P
H, HD = 16, 8
XH, XD = 16, 64
NP = XH // 2
CT = SC // P
KT = CT + S // P
NE, HID = 8, 256
KV = 4

A_XT, A_W1, A_B1, A_WP, A_BP, A_N = 0, 512, 896, 1280, 1408, 1536
G_QKV, G_BQKV, G_ROPE, G_QN, G_WG, G_BG, G_WO, G_BO, G_WR, G_BR, G_RK, G_N = (
    0, 192, 384, 416, 576, 704, 832, 960, 1088, 1096, 1104, 1112)
C_G1, C_B1, C_G2, C_B2, C_L1, C_L2, C_E5, C_E6 = range(8)


class Attn:
    pass


def decoder_layer(nc, d_a, d_x, d_ctx, d_cols, d_wkv, d_wq, d_wout, d_g, d_we1, d_we2, d_be, d_out):
    ctx = ExitStack()
    with ctx:
        def sem(name):
            return ctx.enter_context(nc.semaphore(name))

        base = 16512

        def at(name, cols, dt, off):
            return nc.alloc_sbuf_tensor_at(name, [P, cols], dt, offset=base + off)

        ident = at("ident", P, F, 0)
        cR = at("const_r", 3 * P, R, 512)
        xs = at("xs", NT * D, F, 2112)
        xq_w = at("xq_w", XH * XD, F, 4160)
        lnT = at("lnT", B * S, F, 8256)
        st = at("stats", 256, F, 10304)
        cols = at("cols", 8, F, 11328)
        bnst = at("bn_stats", 32, F, 11360)
        negmax = at("negmax", 8, F, 11488)
        rc = at("rc", 64, F, 11616)
        psums = st[:, 64:128]
        o_w = 11904
        o_ot = 16000
        o_q = 24192
        o_sc = 40576
        o_kch = 65152
        o_kcl = o_kch + 32 * KB
        o_vc = o_kcl + 32 * KB
        o_klh = o_vc + 32 * KB
        o_kll = o_klh + 16 * KB
        o_vl = o_kll + 16 * KB
        assert base + o_vl + 16 * KB <= 229344

        kch = at("kc_hi", B * NP * SC, R, o_kch)
        kcl = at("kc_lo", B * NP * SC, R, o_kcl)
        vc = at("vc", B * CT * XH * XD, F, o_vc)
        klh = at("kl_hi", B * NP * S, R, o_klh)
        kll = at("kl_lo", B * NP * S, R, o_kll)
        vl = at("vl", B * 2 * XH * XD, F, o_vl)
        qh = at("q_hi", NP * S, R, o_q)
        ql = at("q_lo", NP * S, R, o_q + 8 * KB)
        recT = at("recT", 2 * P, F, o_q)
        xout_w = at("xout_w", NP * D, F, o_w)
        ot = at("ot", NP * S, F, o_ot)
        pr = at("probs", 4 * 6 * P, F, o_sc)
        pT = at("probsT", 2 * 12 * P, F, o_sc + 12 * KB)
        wkvh = at("wkv_hi", 2048, R, o_sc)
        wkvl = at("wkv_lo", 2048, R, o_sc + 8 * KB)
        cTh = at("ctxT_hi", B * SC, R, o_sc + 16 * KB)
        cTl = at("ctxT_lo", B * SC, R, o_sc + 20 * KB)
        lnTh = at("lnT_hi", B * S, R, o_sc + 16 * KB)
        lnTl = at("lnT_lo", B * S, R, o_sc + 18 * KB)
        wkv = at("wkv_raw", 2048, F, o_q)
        wA = at("wA", A_N, F, o_q + 8 * KB)
        ln = at("ln_tok", NT * D, F, o_q + 14 * KB)
        cx = at("ctx_tok", B * SC, F, o_ot)
        cS = at("const_f", 2 * P, F, o_kcl)
        cX = at("ctxT_f", SC, F, o_kch)

        ps = ctx.enter_context(nc.psum_tensor("ps", [P, 8, 512], F))

        def bank(n, a=0, b=512):
            return ps[:, n, a:b]

        idR = cR[:, 0:P]
        up = cR[:, P:2 * P]
        low = cR[:, 2 * P:3 * P]

        def attn_buffers(tag, o_qst, o_kst, o_vp, o_pt, o_ots, o_otok, o_ott, kgroups):
            a = Attn()
            a.s_qsplit, a.s_ksplit = sem(tag + "q_split"), sem(tag + "k_split")
            a.s_T, a.s_q_ev, a.s_k_ev = sem(tag + "transposed"), sem(tag + "q_ready"), sem(tag + "k_ready")
            a.s_vp = sem(tag + "v_padded")
            a.s_S, a.s_max, a.s_nm = sem(tag + "scores"), sem(tag + "max_taken"), sem(tag + "negmax_split")
            a.s_q2T, a.s_q2 = sem(tag + "q_with_max_T"), sem(tag + "q_with_max_ready")
            a.s_ST, a.s_E, a.s_PV = sem(tag + "scores_t"), sem(tag + "exp_done"), sem(tag + "pv_done")
            a.s_ots, a.s_OT, a.s_O = sem(tag + "o_copied"), sem(tag + "o_untransposed"), sem(tag + "o_normed")
            a.kg = kgroups
            a.qst = at(tag + "qst", 4 * 512, R, o_qst)
            a.kst = at(tag + "kst", kgroups * 512, R, o_kst)
            a.vh = 4 * kgroups
            a.vp = at(tag + "vpad", NT * a.vh * 32, F, o_vp)
            a.pt = [at(f"{tag}pt{i}", 2048, F, o_pt[i]) for i in range(3)]
            a.ots = at(tag + "ots", 1024, F, o_ots)
            a.otok = at(tag + "otok", NT * P, F, o_otok)
            a.ott = at(tag + "ott", NT * P, F, o_ott)
            a.qs = at(tag + "qs", NT * 512, F, o_pt[0])
            a.ks = at(tag + "ks", NT * kgroups * P, F, o_pt[1])
            a.h = at(tag + "h", NT * 384, F, o_pt[2])
            return a

        LAT = o_klh
        a1 = attn_buffers("sa_", LAT + 24 * KB, LAT + 32 * KB, LAT + 40 * KB,
                          [LAT, LAT + 8 * KB, LAT + 16 * KB], o_ot + 4 * KB,
                          o_q, o_q + 2 * KB, 4)
        f0 = o_kch + 16 * KB
        f1 = o_kcl + 16 * KB
        f2 = o_vc + 16 * KB
        a2 = attn_buffers("ga_", f0, f0 + 8 * KB, f0 + 10 * KB, [f1, f1 + 8 * KB, f2],
                          f2 + 8 * KB, f2 + 12 * KB, f2 + 14 * KB, 1)
        wG = at("wG", G_N, F, o_klh + 8 * KB)
        wbe = at("wbe", 640, F, o_klh + 8 * KB + 4480)
        w1r = at("w1_raw", NE * 512, F, o_kch)
        w1h = at("w1_hi", NE * 512, R, o_kcl)
        w1l = at("w1_lo", NE * 512, R, o_vc)
        w2r = at("w2_raw", NE * 256, F, o_klh)
        w2h = at("w2_hi", NE * 256, R, o_kll)
        w2l = at("w2_lo", NE * 256, R, o_vl)
        beh = at("be_hi", 512, R, o_kll + 8 * KB)
        bel = at("be_lo", 512, R, o_kll + 10 * KB)
        x3 = at("x3", NT * D, F, o_kll + 12 * KB)
        x2T = at("x2T", NT * D, F, o_kll + 14 * KB)
        rp = at("rope_out", NT * 160, F, o_vl + 8 * KB)
        rq = at("rope_tmp", NT * 160, F, o_vl + 8 * KB + 2560)
        xmh = at("xm_hi", NE * 512, R, f1)
        xml = at("xm_lo", NE * 512, R, f2)
        sc = o_sc
        h2 = at("h2_tok", NT * D, F, sc)
        h2T = at("h2T", NT * D, F, sc + 2 * KB)
        gat = at("gate", NT * D, F, sc + 4 * KB)
        lg = at("logits", 3 * NT * NE, F, sc + 6 * KB)
        mk = at("mask", NT * NE, F, sc + 6 * KB + 512)
        mkT = at("maskT", NT * P, F, sc + 8 * KB)
        mkR = at("maskT_r", NT * P, R, sc + 10 * KB)
        sg = at("sig", NT * HID, F, sc + 12 * KB)
        actf = at("act", NT * HID, F, sc + 16 * KB)
        acTh = at("actT_hi", NT * HID, R, sc + 20 * KB)
        acTl = at("actT_lo", NT * HID, R, o_q)
        prod = at("prod", 2 * 1024, F, o_q + 4 * KB)
        yv = at("y", NT * D, F, o_q + 12 * KB)
        h2h = at("h2T_hi", NT * D, R, o_q + 14 * KB)
        fT = at("gatedT", NT * D, F, o_ot)

        s_ldA, s_ldx, s_ldc, s_ldv, s_ldk, s_ldq, s_ldo = (sem(n) for n in (
            "ld_self_attn", "ld_x", "ld_ctx", "ld_wv", "ld_wk", "ld_wq", "ld_wout"))
        s_ldg, s_ld1, s_ld2, s_store = (sem(n) for n in ("ld_ffn", "ld_w1", "ld_w2", "store"))
        s_c0, s_const, s_zero, s_constR = (sem(n) for n in ("const0", "const", "zeroed", "const_r_ready"))
        s_dv, s_ac, s_po = sem("dve_chain"), sem("act_chain"), sem("pool_chain")
        s_vhi, s_vlo, s_khi, s_klo = (sem(n) for n in ("wv_hi", "wv_lo", "wk_hi", "wk_lo"))
        s_cst, s_crs, s_cln, s_cT, s_cTh, s_cTl = (sem(n) for n in (
            "ctx_stats", "ctx_rstd", "ctx_ln", "ctx_T", "ctxT_hi_ready", "ctxT_ready"))
        s_qkv, s_h = sem("qkv"), sem("h")
        s_vch, s_vev, s_kch, s_kev, s_kdn = (sem(n) for n in (
            "v_chunk", "v_evacuated", "k_chunk", "k_hi_done", "k_done"))
        s_OtT, s_ott, s_pj, s_x1p = (sem(n) for n in ("o_T", "o_T_sb", "proj", "x_pre"))
        s_st, s_rs, s_xn = sem("ln_stats"), sem("ln_rstd"), sem("ln_done")
        s_lnT, s_lnTf, s_lnTs = sem("lat_T"), sem("lat_T_sb"), sem("lat_T_split")
        s_lch, s_lhi, s_llo = sem("lat_chunk"), sem("lat_hi"), sem("lat_done")
        s_S, s_mx, s_ex, s_tr, s_cpA, s_cpD, s_pv, s_oev = (sem(n) for n in (
            "x_scores", "x_max", "x_exp", "x_transposed", "x_copied_act", "x_copied_dve", "x_pv", "x_o_evacuated"))
        s_rc, s_rcT, s_rcS, s_R, s_on, s_xo, s_xov = (sem(n) for n in (
            "x_recip", "x_recip_T", "x_recip_sb", "x_recip_bcast", "x_normed", "x_out", "x_out_read"))
        s_q1, s_q1h, s_q1l = sem("q_chunk"), sem("q_hi_done"), sem("q_done")
        s_w1h, s_w1l, s_w2h, s_w2l = (sem(n) for n in ("w1_hi_done", "w1_lo_done", "w2_hi_done", "w2_lo_done"))
        s_g = {n: sem("g_" + n) for n in (
            "x2T", "x2Tsb", "ss", "rstd", "qkv", "h", "sq", "rms", "OtT", "ott", "gl", "gpre", "e", "gated", "gT",
            "gTs", "wo", "x3", "ss3", "rstd3", "h2", "h2T", "h2Ts", "h2h", "lg", "mk", "mkT", "mkTs", "bc", "xm",
            "be", "b2r", "u", "eu", "act", "actT", "acTh", "acTl", "y", "yr", "b2", "v")}

        block = ctx.enter_context(nc.Block())

        @block.sync
        def _(sp):
            sp.dma_start(wA[:, :], d_a).then_inc(s_ldA, 16)
            sp.dma_start(cx[:, :], d_ctx).then_inc(s_ldc, 16)
            sp.dma_start(wkv[:, 1024:2048], d_wkv[:, 1024:2048]).then_inc(s_ldv, 16)
            sp.dma_start(xq_w[:, :], d_wq).then_inc(s_ldq, 16)
            sp.dma_start(xout_w[:, :], d_wout).then_inc(s_ldo, 16)
            sp.wait_ge(s_pv, 16)
            sp.dma_start(w1r[:, :], d_we1).then_inc(s_ld1, 16)
            sp.dma_start(w2r[:, :], d_we2).then_inc(s_ld2, 16)
            sp.wait_ge(s_pv, 32)
            sp.dma_start(wG[:, :], d_g).then_inc(s_ldg, 16)
            sp.dma_start(wbe[0:NE, :], d_be).then_inc(s_ldg, 16)
            sp.wait_ge(s_g["v"], 4)
            sp.dma_start(d_out, xs[:, :]).then_inc(s_store, 16)
            sp.wait_ge(s_store, 16)

        @block.gpsimd
        def _(pool):
            def max_slots(a):
                pool.memset(a.qs[:, :].rearrange("p (n r d) -> p n r d", r=4, d=HD)[:, :, 3, :], 0.0).then_inc(s_zero, 1)
                pool.memset(a.ks[:, :].rearrange("p (n r d) -> p n r d", r=4, d=HD)[:, :, 3, :], 1.0).then_inc(s_zero, 1)

            pool.memset(ident[:, :], 0.0).then_inc(s_c0, 1)
            pool.memset(cS[:, :], 0.0).then_inc(s_c0, 1)
            pool.wait_ge(s_c0, 2)
            pool.affine_select(out=ident[:, :], in_=ident[:, :], compare_op=ALU.not_equal, fill=1.0,
                               base=0, pattern=[[-1, P]], channel_multiplier=1).then_inc(s_const, 1)
            pool.affine_select(out=cS[:, 0:P], in_=cS[:, 0:P], compare_op=ALU.is_ge, fill=NEG,
                               base=0, pattern=[[-1, P]], channel_multiplier=1).then_inc(s_const, 1)
            pool.affine_select(out=cS[:, P:2 * P], in_=cS[:, P:2 * P], compare_op=ALU.is_ge, fill=NEG,
                               base=0, pattern=[[1, P]], channel_multiplier=-1).then_inc(s_const, 1)
            max_slots(a1)
            pool.memset(a1.vp[:, :], 0.0).then_inc(s_po, 1)
            pool.wait_ge(s_po, 1)
            pool.memset(a1.vp[:, :].rearrange("p (n c) -> p n c", c=32)[:, :, HD:HD + 1], 1.0).then_inc(s_zero, 1)
            pool.wait_ge(s_ld1, 16)
            for e in range(NE):
                w = slice(512 * e, 512 * e + 512)
                pool.tensor_copy(w1h[:, w], w1r[:, w]).then_inc(s_w1h, 1)
                pool.wait_ge(s_w1h, e + 1)
                pool.tensor_tensor(w1l[:, w], w1r[:, w], w1h[:, w].bitcast(F), ALU.subtract).then_inc(s_w1l, 1)
            pool.wait_ge(s_ld2, 16)
            for e in range(4):
                w = slice(512 * e, 512 * e + 512)
                pool.tensor_copy(w2h[:, w], w2r[:, w]).then_inc(s_w2h, 1)
                pool.wait_ge(s_w2h, e + 1)
                pool.tensor_tensor(w2l[:, w], w2r[:, w], w2h[:, w].bitcast(F), ALU.subtract).then_inc(s_w2l, 1)
            pool.wait_ge(s_pv, 32)
            max_slots(a2)
            pool.memset(a2.vp[:, :], 0.0).then_inc(s_po, 1)
            pool.wait_ge(s_po, 2)
            pool.memset(a2.vp[:, :].rearrange("p (n c) -> p n c", c=32)[:, :, HD:HD + 1], 1.0).then_inc(s_zero, 1)

        ROUNDS = [(b, kind) for b in range(B) for kind in range(3)]

        def q_transposes(pe, a, b, bk, s_done):
            for g in range(4):
                for i in range(2):
                    pe.transpose(ps[:, bk + g // 2, 256 * (g % 2) + P * i:256 * (g % 2) + P * i + P],
                                 a.qs[:, (2 * b + i) * 512 + P * g:(2 * b + i) * 512 + P * g + P],
                                 ident[:, :]).then_inc(s_done, 1)

        def pe_stacks(pe, a):
            kg = a.kg
            pe.wait_ge(s_zero, 2 if a is a1 else 5)
            for b in range(B):
                pe.wait_ge(a.s_qsplit, b + 1)
                q_transposes(pe, a, b, 4 * b, a.s_T)
                pe.wait_ge(a.s_ksplit, b + 1)
                for g in range(kg):
                    for i in range(2):
                        pe.transpose(ps[:, 4 * b + 2 + g // 2, 256 * (g % 2) + P * i:256 * (g % 2) + P * i + P],
                                     a.ks[:, ((2 * b + i) * kg + g) * P:((2 * b + i) * kg + g + 1) * P],
                                     ident[:, :]).then_inc(a.s_T, 1)

        def pe_scores(pe, a, r):
            b, kind = ROUNDS[r]
            if r % 3 == 0:
                pe.wait_ge(a.s_q_ev, b + 1)
                pe.wait_ge(a.s_k_ev, b + 1)
            tok = 256 * b
            n = 4 if kind == 0 else 2
            w = 512 // n
            for hf in range(2):
                if r > 0:
                    pe.wait_ge(a.s_max, 2 * (r - 1) + hf + 1)
                quads = (2 * hf, 2 * hf + 1)
                for j in quads:
                    pe.matmul(ps[:, j, :].rearrange("p (n w) -> p n w", n=n)[:, :, w - P:w], idR,
                              up.unsqueeze(1).to_broadcast([P, n, P]), start=True, stop=False,
                              skip_group_check=True)
                for m in range(n):
                    g = m if kind == 0 else 2 * (kind - 1) + m
                    kg = g if a.kg > 1 else 0
                    q0 = 512 * g + tok + (0 if kind == 0 else P)
                    k0 = 512 * kg + tok
                    for j in quads:
                        s = slice(32 * j, 32 * j + 32)
                        last = pe.matmul(ps[:, j, w * m:w * m + w], a.qst[s, q0:q0 + P], a.kst[s, k0:k0 + w],
                                         start=False, stop=True, skip_group_check=True)
                last.then_inc(a.s_S, 1)

        def pe_maxrows(pe, a, b):
            pe.wait_ge(a.s_nm, b + 1)
            q_transposes(pe, a, b, 4 + 2 * b, a.s_q2T)

        def pe_scoresT(pe, a, r):
            b, kind = ROUNDS[r]
            if kind == 0:
                pe.wait_ge(a.s_q2, b + 1)
            tok = 256 * b
            n = 4 if kind == 0 else 2
            w = 512 // n
            q1 = tok + (P if kind == 0 else 0)
            for hf in range(2):
                if r == 0:
                    pe.wait_ge(a.s_max, 11 + hf)
                else:
                    pe.wait_ge(a.s_E, 2 * (r - 1) + hf + 1)
                quads = (2 * hf, 2 * hf + 1)
                for j in quads:
                    pe.matmul(ps[:, j, :].rearrange("p (n w) -> p n w", n=n)[:, :, 0:P], idR,
                              low.unsqueeze(1).to_broadcast([P, n, P]), start=True, stop=False,
                              skip_group_check=True)
                for m in range(n):
                    g = m if kind == 0 else 2 * (kind - 1) + m
                    kg = g if a.kg > 1 else 0
                    k0 = 512 * kg + tok + (P if kind == 0 else 0)
                    q0 = 512 * g + q1
                    for j in quads:
                        s = slice(32 * j, 32 * j + 32)
                        last = pe.matmul(ps[:, j, w * m:w * m + w], a.kst[s, k0:k0 + P], a.qst[s, q0:q0 + w],
                                         start=False, stop=True, skip_group_check=True)
                last.then_inc(a.s_ST, 1)

        def pe_values(pe, a, b, half):
            pe.wait_ge(a.s_E, 2 * (3 * b + 2 + half))
            if half == 0:
                pe.wait_ge(a.s_vp, 1)
                if b > 0:
                    pe.wait_ge(a.s_O, 2 * b)
            short = a.pt[(3 * b) % 3]
            long = a.pt[(3 * b + 1 + half) % 3]
            for m in range(2):
                g = 2 * half + m
                for t, (buf, c0, w) in enumerate(((long, 256 * m, 256), (short, P * g, P))):
                    for j in range(4):
                        head = (4 * g + j) if a.kg > 1 else j
                        v0 = ((2 * b + t) * a.vh + head) * 32
                        last = pe.matmul(ps[32 * j:32 * j + 32, 4 + half, 256 * m + 256 - w:256 * m + 256],
                                         a.vp[:, v0:v0 + 32], buf[:, 512 * j + c0:512 * j + c0 + w],
                                         start=(t == 0), stop=(t == 1), skip_group_check=True)
            last.then_inc(a.s_PV, 1)

        def pe_untranspose(pe, a, b):
            pe.wait_ge(a.s_ots, b + 1)
            for i in range(2):
                for g in range(4):
                    c = 512 * (g // 2) + 256 * (g % 2) + P * i
                    last = pe.transpose(ps[:, 4 + i, P * g:P * g + P], a.ots[:, c:c + P], ident[:, :])
                last.then_inc(a.s_OT, 1)

        def act_maxrows(act, a, b):
            act.wait_ge(a.s_q2T, 8 * (b + 1))
            act.wait_ge(a.s_S, 6 * (b + 1))
            nc.scalar.activation(a.qst[:, :].rearrange("p (g t) -> p g t", g=4)[:, :, 256 * b:256 * b + 256],
                                 ps[:, 4 + 2 * b:6 + 2 * b, :].rearrange("p a (g t) -> p (a g) t", g=2),
                                 ACT.Copy).then_inc(a.s_q2, 1)

        def act_exp(act, a, r):
            if r == 0:
                act.wait_ge(a.s_q2T, 16)
            if r == 1:
                act.wait_ge(a.s_T, 16 + 4 * a.kg)
            if r == 3:
                act.wait_ge(a.s_PV, 2)
            for hf in range(2):
                act.wait_ge(a.s_ST, 2 * r + hf + 1)
                nc.scalar.activation(a.pt[r % 3][:, 1024 * hf:1024 * hf + 1024],
                                     ps[:, 2 * hf:2 * hf + 2, :].rearrange("p a b -> p (a b)"),
                                     ACT.Exp).then_inc(a.s_E, 1)

        def dve_max(dve, a, r, v, need):
            b, kind = ROUNDS[r]
            t = 2 * b + (0 if kind == 0 else 1)
            nmf = st[:, 128:192].rearrange("p (t g j) -> p t g j", t=NT, g=4)
            for hf in range(2):
                dve.wait_ge(a.s_S, 2 * r + hf + 1)
                jj = slice(2 * hf, 2 * hf + 2)
                if kind == 0:
                    src = ps[:, jj, :].rearrange("p j (g w) -> p j g w", g=4)
                    dst = nmf[:, t, :, jj].rearrange("p g j -> p j g")
                else:
                    src = ps[:, jj, :].rearrange("p j (g w) -> p j g w", g=2)
                    dst = nmf[:, t, 2 * (kind - 1):2 * kind, jj].rearrange("p g j -> p j g")
                dve.tensor_reduce(dst, src, X, ALU.max, negate=True).then_inc(a.s_max, 1)
            if kind == 2:
                dve.wait_ge(a.s_max, 2 * r + 2)
                dve.wait_ge(a.s_T, (8 + 2 * a.kg) * (b + 1))
                src = st[:, 128:192].rearrange("p (t c) -> p t c", t=NT)[:, 2 * b:2 * b + 2, :]
                dst = a.qs[:, :].rearrange("p (t n r d) -> p t n r d", t=NT, n=16, r=4)[:, 2 * b:2 * b + 2, :, 3, :]
                n = v(dve.tensor_copy(dst[:, :, :, 0].bitcast(R), src))
                need(n)
                dve.tensor_tensor(dst[:, :, :, 1], src, dst[:, :, :, 0], ALU.subtract).then_inc(a.s_nm, 1)

        def dve_norm(dve, a, b, v, need):
            for i in range(2):
                t = 2 * b + i
                dve.wait_ge(a.s_OT, t + 1)
                src = ps[:, 4 + i, :].rearrange("p (h c) -> p h c", c=32)
                n = v(dve.reciprocal(st[:, 192 + 16 * t:208 + 16 * t], src[:, :, HD]))
                need(n)
                dve.tensor_tensor(a.otok[:, P * t:P * t + P].rearrange("p (h c) -> p h c", c=HD),
                                  src[:, :, 0:HD],
                                  st[:, 192 + 16 * t:208 + 16 * t].unsqueeze(2).to_broadcast([P, 16, HD]),
                                  ALU.mult).then_inc(a.s_O, 1)

        STEPS = [(b, c, i) for b in range(B) for c in range(NP) for i in range(2)]
        LCH = [x for c in range(NP) for x in (("q", c), ("k", c))] + [("v", n) for n in range(8)]

        @block.tensor
        def _(pe):
            def three(out, xh, xl, wh, wl, start=True):
                pe.matmul(out, xh, wh, start=start, stop=False)
                pe.matmul(out, xh, wl, start=False, stop=False)
                return pe.matmul(out, xl, wh, start=False, stop=True)

            pe.wait_ge(s_ldA, 16)
            for t in range(NT):
                pe.matmul(bank(4 + t, 0, 384), wA[:, A_XT + P * t:A_XT + P * t + P], wA[:, A_W1:A_W1 + 384],
                          start=True, stop=True).then_inc(s_qkv, 1)

            def ctx_transposes(b):
                pe.wait_ge(s_cln, 4 * (b + 1))
                for i in range(4):
                    t = 4 * b + i
                    last = pe.transpose(bank(b, P * i, P * i + P), cx[:, P * t:P * t + P], ident[:, :])
                last.then_inc(s_cT, 1)

            pe.wait_ge(s_const, 1)
            ctx_transposes(0)
            ctx_transposes(1)
            pe.wait_ge(s_cTl, 2)
            pe.wait_ge(s_h, 4)
            pe_stacks(pe, a1)
            pe.wait_ge(s_constR, 2)

            def v_chunk(n):
                t, half = n // 2, n % 2
                if n == 0:
                    pe.wait_ge(s_vlo, 1)
                    pe.wait_ge(a1.s_q_ev, 2)
                    pe.wait_ge(a1.s_k_ev, 2)
                if n >= 4:
                    pe.wait_ge(s_vev, n - 3)
                c = slice(1024 + 512 * half, 1536 + 512 * half)
                tt = slice(P * t, P * t + P)
                three(bank(4 + n % 4), cTh[:, tt], cTl[:, tt], wkvh[:, c], wkvl[:, c]).then_inc(s_vch, 1)

            vn = 0
            for r in range(6):
                pe_scores(pe, a1, r)
                for _ in range(3 if r < 4 else 2):
                    v_chunk(vn)
                    vn += 1
            pe.wait_ge(s_vev, 16)
            pe_maxrows(pe, a1, 0)
            pe_maxrows(pe, a1, 1)

            def k_chunk(n):
                c, b = n // 2, n % 2
                if n == 0:
                    pe.wait_ge(s_klo, 1)
                    pe.wait_ge(a1.s_q2, 2)
                if n >= 2:
                    pe.wait_ge(s_kdn, n - 1)
                cc = slice(P * c, P * c + P)
                tt = slice(SC * b, SC * b + SC)
                three(bank(6 + n % 2), wkvh[:, cc], wkvl[:, cc], cTh[:, tt], cTl[:, tt]).then_inc(s_kch, 1)

            kn = 0

            def k_chunks(m):
                nonlocal kn
                for _ in range(m):
                    k_chunk(kn)
                    kn += 1

            pe_scoresT(pe, a1, 0)
            k_chunks(2)
            pe_scoresT(pe, a1, 1)
            k_chunks(2)
            pe_scoresT(pe, a1, 2)
            pe_values(pe, a1, 0, 0)
            k_chunks(2)
            pe_scoresT(pe, a1, 3)
            pe_values(pe, a1, 0, 1)
            k_chunks(2)
            pe_scoresT(pe, a1, 4)
            pe_untranspose(pe, a1, 0)
            k_chunks(3)
            pe_scoresT(pe, a1, 5)
            pe_values(pe, a1, 1, 0)
            k_chunks(3)
            pe_values(pe, a1, 1, 1)
            k_chunks(1)
            pe_untranspose(pe, a1, 1)
            k_chunks(1)

            def project(a, s_T_, s_sb, s_p, w):
                for t in range(NT):
                    pe.wait_ge(a.s_O, t + 1)
                    last = pe.transpose(bank(0, P * t, P * t + P), a.otok[:, P * t:P * t + P], ident[:, :])
                last.then_inc(s_T_, 1)
                pe.wait_ge(s_sb, 1)
                for t in range(NT):
                    last = pe.matmul(bank(1, P * t, P * t + P), a.ott[:, P * t:P * t + P], w,
                                     start=(t == 0), stop=True, skip_group_check=True)
                last.then_inc(s_p, 1)

            project(a1, s_OtT, s_ott, s_pj, wA[:, A_WP:A_WP + P])

            pe.wait_ge(s_xn, 2 * NT)
            for t in range(NT):
                last = pe.transpose(bank(0, P * t, P * t + P), ln[:, P * t:P * t + P], ident[:, :])
            last.then_inc(s_lnT, 1)
            pe.wait_ge(s_lnTs, 2)
            pe.wait_ge(s_ldq, 16)
            pe.wait_ge(s_kdn, 16)
            for n, (kind, c) in enumerate(LCH):
                if n >= 8:
                    kinds = [k for k, _ in LCH[:n - 7]]
                    pe.wait_ge(s_llo, sum(k != "v" for k in kinds))
                    if "v" in kinds:
                        pe.wait_ge(s_lhi, n - 7)
                bk = n % 8
                if kind == "q":
                    pe.matmul(bank(bk, 0, S), xq_w[:, P * c:P * c + P], lnT[:, 0:S],
                              start=True, stop=True).then_inc(s_lch, 1)
                elif kind == "k":
                    cc = slice(P * c, P * c + P)
                    three(bank(bk), wkvh[:, cc], wkvl[:, cc], lnTh[:, :], lnTl[:, :]).then_inc(s_lch, 1)
                else:
                    t, half = c // 2, c % 2
                    w = slice(1024 + 512 * half, 1536 + 512 * half)
                    tt = slice(P * t, P * t + P)
                    three(bank(bk), lnTh[:, tt], lnTl[:, tt], wkvh[:, w], wkvl[:, w]).then_inc(s_lch, 1)

            def x_scores(s):
                b, c, i = STEPS[s]
                if s == 0:
                    pe.wait_ge(s_lhi, len(LCH))
                    pe.wait_ge(s_llo, 2 * NP)
                if s == NP * 2:
                    pe.wait_ge(s_q1l, NP)
                if s > 0:
                    pe.wait_ge(s_ex, 2 * s)
                q = slice(S * c + P * i, S * c + P * i + P)
                kc = slice((b * NP + c) * SC, (b * NP + c + 1) * SC)
                kl = slice((b * NP + c) * S, (b * NP + c + 1) * S)
                for n, (qq, kk, ll) in enumerate(((qh, kch, klh), (qh, kcl, kll), (ql, kch, klh))):
                    for hh in range(2):
                        rows = slice(64 * hh, 64 * hh + 64)
                        pe.matmul(bank(2 * hh), qq[rows, q], kk[rows, kc], start=(n == 0), stop=(n == 2))
                    for hh in range(2):
                        rows = slice(64 * hh, 64 * hh + 64)
                        last = pe.matmul(bank(2 * hh + 1, 0, S), qq[rows, q], ll[rows, kl],
                                         start=(n == 0), stop=(n == 2))
                        if n == 2:
                            last.then_inc(s_S, 1)

            def x_transposes(s):
                for u in range(2):
                    pe.wait_ge(s_ex, 2 * s + u + 1)
                    slot = (2 * s + u) % 4
                    for kt in range(KT):
                        n = KT * u + kt
                        if n % 4 == 0 and s > 0:
                            if n // 4 == 1:
                                pe.wait_ge(s_cpA, s)
                            else:
                                pe.wait_ge(s_cpD, 2 * (s - 1) + (1 if n == 0 else 2))
                        last = pe.transpose(bank(4 + n // 4, P * (n % 4), P * (n % 4) + P),
                                            pr[:, (slot * KT + kt) * P:(slot * KT + kt + 1) * P], ident[:, :])
                        if n % 4 == 3:
                            last.then_inc(s_tr, 1)

            def x_values(s):
                b, c, i = STEPS[s]
                pe.wait_ge(s_cpA, s + 1)
                pe.wait_ge(s_cpD, 2 * s + 2)
                if s > 0:
                    pe.wait_ge(s_oev, s)
                buf = (s % 2) * 12 * P
                for kt in range(KT):
                    for hh in range(2):
                        if kt < CT:
                            v0 = (b * CT + kt) * 1024 + P * c + 64 * hh
                            v = vc[:, v0:v0 + 64]
                        else:
                            v0 = (b * 2 + kt - CT) * 1024 + P * c + 64 * hh
                            v = vl[:, v0:v0 + 64]
                        p0 = buf + (KT * hh + kt) * P
                        last = pe.matmul(ps[64 * hh:64 * hh + 64, 7, 0:P], v, pT[:, p0:p0 + P],
                                         start=(kt == 0), stop=(kt == KT - 1))
                last.then_inc(s_pv, 1)

            def x_output(b):
                pe.wait_ge(s_rc, b + 1)
                for i in range(2):
                    last = pe.transpose(ps[0:16, 4, P * i:P * i + P], rc[:, 32 * b + 16 * i:32 * b + 16 * i + 16],
                                        ident[:, :])
                last.then_inc(s_rcT, 1)
                pe.wait_ge(s_rcS, b + 1)
                for c in range(NP):
                    for hh in range(2):
                        last = pe.matmul(ps[64 * hh:64 * hh + 64, c // 2, 256 * (c % 2):256 * (c % 2) + 256],
                                         ident[0:16, 2 * c + hh:2 * c + hh + 1].to_broadcast([16, 64]),
                                         recT[0:16, :], start=True, stop=True, skip_group_check=True)
                    last.then_inc(s_R, 1)
                pe.wait_ge(s_on, 4 * (b + 1))
                pe.wait_ge(s_ldo, 16)
                for i in range(2):
                    for c in range(NP):
                        last = pe.matmul(bank(5, P * i, P * i + P), ot[:, S * c + P * i:S * c + P * i + P],
                                         xout_w[:, D * c:D * c + D], start=(c == 0), stop=(c == NP - 1),
                                         skip_group_check=True)
                last.then_inc(s_xo, 1)

            for b in range(B):
                s0 = 16 * b
                for s in range(s0, s0 + 16):
                    x_scores(s)
                    if s > s0:
                        x_transposes(s - 1)
                    if s > s0 + 1:
                        x_values(s - 2)
                x_transposes(s0 + 15)
                x_values(s0 + 14)
                x_values(s0 + 15)
                x_output(b)
                if b == 0:
                    for c in range(NP):
                        if c >= 4:
                            pe.wait_ge(s_q1l, c - 3)
                        pe.matmul(bank(c % 4, 0, S), xq_w[:, P * c:P * c + P], lnT[:, S:2 * S],
                                  start=True, stop=True).then_inc(s_q1, 1)

            g = s_g
            pe.wait_ge(s_xn, 3 * NT)
            for t in range(NT):
                last = pe.transpose(bank(0, P * t, P * t + P), xs[:, P * t:P * t + P], ident[:, :])
            last.then_inc(g["x2T"], 1)
            pe.wait_ge(g["x2Tsb"], 1)
            pe.wait_ge(s_ldg, 32)
            for t in range(NT):
                pe.matmul(bank(4 + t, 0, 192), x2T[:, P * t:P * t + P], wG[:, G_QKV:G_QKV + 192],
                          start=True, stop=True).then_inc(g["qkv"], 1)
            pe.wait_ge(g["h"], 4)
            pe_stacks(pe, a2)
            for r in range(4):
                pe_scores(pe, a2, r)
            pe_maxrows(pe, a2, 0)
            pe_scores(pe, a2, 4)
            pe_scores(pe, a2, 5)
            pe_maxrows(pe, a2, 1)
            pe_scoresT(pe, a2, 0)
            pe_scoresT(pe, a2, 1)
            pe_scoresT(pe, a2, 2)
            pe_values(pe, a2, 0, 0)
            pe_scoresT(pe, a2, 3)
            pe_values(pe, a2, 0, 1)
            pe_scoresT(pe, a2, 4)
            pe_untranspose(pe, a2, 0)
            pe_scoresT(pe, a2, 5)
            pe_values(pe, a2, 1, 0)
            pe_values(pe, a2, 1, 1)
            pe_untranspose(pe, a2, 1)
            project(a2, g["OtT"], g["ott"], g["gl"], wG[:, G_WG:G_WG + P])
            pe.wait_ge(g["gated"], 1)
            for t in range(NT):
                last = pe.transpose(bank(2, P * t, P * t + P), a2.otok[:, P * t:P * t + P], ident[:, :])
            last.then_inc(g["gT"], 1)
            pe.wait_ge(g["gTs"], 1)
            for t in range(NT):
                last = pe.matmul(bank(3, P * t, P * t + P), fT[:, P * t:P * t + P], wG[:, G_WO:G_WO + P],
                                 start=(t == 0), stop=True, skip_group_check=True)
            last.then_inc(g["wo"], 1)
            pe.wait_ge(g["h2"], NT)
            for t in range(NT):
                last = pe.transpose(bank(4, P * t, P * t + P), h2[:, P * t:P * t + P], ident[:, :])
            last.then_inc(g["h2T"], 1)
            pe.wait_ge(g["h2Ts"], 1)
            for t in range(NT):
                last = pe.matmul(bank(5, NE * t, NE * t + NE), h2T[:, P * t:P * t + P], wG[:, G_WR:G_WR + NE],
                                 start=(t == 0), stop=True, skip_group_check=True)
            last.then_inc(g["lg"], 1)
            pe.wait_ge(g["mk"], 1)
            for t in range(NT):
                last = pe.transpose(ps[0:NE, 6, P * t:P * t + P], mk[:, NE * t:NE * t + NE], ident[:, :])
            last.then_inc(g["mkT"], 1)
            pe.wait_ge(g["mkTs"], 2)
            for e in range(NE):
                if e >= 4:
                    pe.wait_ge(g["xm"], 2 * (e - 3))
                pe.matmul(bank(4 + e % 4), idR[0:NE, e:e + 1].to_broadcast([NE, P]), mkR[0:NE, :],
                          start=True, stop=True).then_inc(g["bc"], 1)
            pe.wait_ge(s_w1l, NE)

            def experts_u(e, t):
                xx = slice(512 * e + P * t, 512 * e + P * t + P)
                ww = slice(512 * e, 512 * e + 512)
                pe.matmul(bank(t), xmh[:, xx], w1h[:, ww], start=(e == 0), stop=False)
                pe.matmul(bank(t), xmh[:, xx], w1l[:, ww], start=False, stop=False)
                pe.matmul(bank(t), xml[:, xx], w1h[:, ww], start=False, stop=False)

            def bias_u(t):
                tt = slice(P * t, P * t + P)
                pe.matmul(bank(t), mkR[0:NE, tt], beh[0:NE, :], start=False, stop=False)
                pe.matmul(bank(t), mkR[0:NE, tt], bel[0:NE, :], start=False, stop=True).then_inc(g["u"], 1)

            for e in range(NE):
                pe.wait_ge(g["xm"], 2 * (e + 1))
                for t in range(2):
                    experts_u(e, t)
            pe.wait_ge(g["be"], 2)
            bias_u(0)
            bias_u(1)
            for t in range(NT):
                last = pe.matmul(bank(7, P * t, P * t + P), mkT[0:NE, P * t:P * t + P], wbe[0:NE, 512:640],
                                 start=(t == 0), stop=True, skip_group_check=True)
            last.then_inc(g["b2"], 1)
            for t in range(2, NT):
                for e in range(NE):
                    experts_u(e, t)
                bias_u(t)
            pe.wait_ge(s_w2l, 4)

            def act_T(t):
                pe.wait_ge(g["act"], t + 1)
                if t == 1:
                    pe.wait_ge(g["b2r"], 1)
                if t >= 2:
                    pe.wait_ge(g["acTl"], t - 1)
                for k in range(2):
                    last = pe.transpose(bank(6 + t % 2, P * k, P * k + P),
                                        actf[:, HID * t + P * k:HID * t + P * k + P], ident[:, :])
                last.then_inc(g["actT"], 1)

            act_T(0)
            act_T(1)
            for t in range(NT):
                pe.wait_ge(g["acTl"], t + 1)
                if t >= 2:
                    pe.wait_ge(g["yr"], 2 * (t - 1))
                for half in range(2):
                    n = 0
                    for k in range(2):
                        a0 = slice(HID * t + P * k, HID * t + P * k + P)
                        w0 = slice(1024 * k + 512 * half, 1024 * k + 512 * half + 512)
                        for aa, ww in ((acTh, w2h), (acTh, w2l), (acTl, w2h)):
                            last = pe.matmul(bank(4 - 4 * (t % 2) + half), aa[:, a0], ww[:, w0],
                                             start=(n == 0), stop=(n == 5))
                            n += 1
                    last.then_inc(g["y"], 1)
                if t + 2 < NT:
                    act_T(t + 2)

        @block.scalar
        def _(act):
            A = nc.scalar
            n_ac = [0]

            def link(ins):
                n_ac[0] += 1
                ins.then_inc(s_ac, 1)
                act.wait_ge(s_ac, n_ac[0])

            act.dma_start(cols[:, :], d_cols).then_inc(s_ldc, 16)
            act.dma_start(wkv[:, 0:1024], d_wkv[:, 0:1024]).then_inc(s_ldk, 16)
            act.dma_start(xs[:, :], d_x).then_inc(s_ldx, 16)
            A.preload_act_table_set("natural_log_exp_and_others")

            def rstd(out, var, scale, eps):
                link(A.activation(out, var, ACT.Ln, bias=eps, scale=scale))
                return A.activation(out, out, ACT.Exp, scale=-0.5)

            def sigmoid(out, z):
                link(A.activation(out, z, ACT.Exp, scale=-1.0))
                link(A.activation(out, out, ACT.Ln, bias=1.0))
                return A.activation(out, out, ACT.Exp, scale=-1.0)

            mv = st[:, 0:32].rearrange("p (t c) -> p t c", c=2)
            e5 = cols[:, C_E5:C_E5 + 1]
            e6 = cols[:, C_E6:C_E6 + 1]
            act.wait_ge(s_ldc, 32)
            for b in range(B):
                act.wait_ge(s_cst, b + 1)
                rstd(st[:, 32 + 4 * b:36 + 4 * b], mv[:, 4 * b:4 * b + 4, 1], 1.0, e5).then_inc(s_crs, 1)
            act.wait_ge(s_ldv, 16)
            A.activation(wkvh[:, 1024:2048], wkv[:, 1024:2048], ACT.Copy).then_inc(s_vhi, 1)

            hv = a1.h[:, :].rearrange("p (n c d) -> p n c d", c=3, d=HD)
            qs = a1.qs[:, :].rearrange("p (n r d) -> p n r d", r=4, d=HD)
            ks = a1.ks[:, :].rearrange("p (n r d) -> p n r d", r=4, d=HD)
            for b in range(B):
                act.wait_ge(s_h, 2 * b + 2)
                m = slice(32 * b, 32 * b + 32)
                A.activation(qs[:, m, 0, :].bitcast(R), hv[:, m, 0, :], ACT.Copy,
                             scale=HD ** -0.5).then_inc(s_kev, 1)
                A.activation(ks[:, m, 0, :].bitcast(R), hv[:, m, 1, :], ACT.Copy).then_inc(s_kev, 1)
            for b in range(B):
                act.wait_ge(s_cT, b + 1)
                A.activation(cTh[:, SC * b:SC * b + SC], bank(b), ACT.Identity, bias=cols[:, C_B1:C_B1 + 1],
                             scale=cols[:, C_G1:C_G1 + 1]).then_inc(s_cTh, 1)
            act.wait_ge(s_ldk, 16)
            A.activation(wkvh[:, 0:1024], wkv[:, 0:1024], ACT.Copy).then_inc(s_khi, 1)
            for b in range(B):
                act.wait_ge(a1.s_T, 16 * b + 8)
                A.activation(a1.qst[:, :].rearrange("p (g t) -> p g t", g=4)[:, :, 256 * b:256 * b + 256],
                             ps[:, 4 * b:4 * b + 2, :].rearrange("p a (g t) -> p (a g) t", g=2),
                             ACT.Copy).then_inc(a1.s_q_ev, 1)
            act.wait_ge(s_zero, 3)
            A.activation(a1.vp[:, :].rearrange("p (n c) -> p n c", c=32)[:, :, 0:HD], hv[:, :, 2, :],
                         ACT.Copy).then_inc(a1.s_vp, 1)
            for n in range(16):
                t, half = n // 2, n % 2
                act.wait_ge(s_vch, n + 1)
                A.activation(vc[:, 1024 * t + 512 * half:1024 * t + 512 * half + 512], bank(4 + n % 4),
                             ACT.Copy).then_inc(s_vev, 1)
            act_maxrows(act, a1, 0)
            act_maxrows(act, a1, 1)

            kn = 0

            def k_hi(m):
                nonlocal kn
                for _ in range(m):
                    c, b = kn // 2, kn % 2
                    act.wait_ge(s_kch, kn + 1)
                    A.activation(kch[:, (b * NP + c) * SC:(b * NP + c + 1) * SC], bank(6 + kn % 2),
                                 ACT.Copy).then_inc(s_khi, 1)
                    kn += 1

            act.wait_ge(s_vch, 16)
            for r, m in enumerate((2, 2, 2, 2, 3, 3)):
                if r == 2:
                    act.wait_ge(a1.s_vp, 1)
                act_exp(act, a1, r)
                k_hi(m)
            k_hi(2)

            act.wait_ge(s_OtT, 1)
            A.activation(a1.ott[:, :], bank(0), ACT.Copy).then_inc(s_ott, 1)

            def ln_rstd(k):
                act.wait_ge(s_st, k + 1)
                rstd(st[:, 32:36], mv[:, 0:4, 1], 1.0, e5).then_inc(s_rs, 1)

            ln_rstd(0)
            ln_rstd(1)
            act.wait_ge(s_lnT, 1)
            link(A.activation(lnT[:, :], bank(0), ACT.Identity, bias=cols[:, C_B2:C_B2 + 1],
                              scale=cols[:, C_G2:C_G2 + 1]))
            A.activation(lnTh[:, :], lnT[:, :], ACT.Copy).then_inc(s_lnTs, 1)
            for n, (kind, c) in enumerate(LCH):
                act.wait_ge(s_lch, n + 1)
                bk = n % 8
                if kind == "q":
                    if n == 0:
                        act.wait_ge(s_pj, 1)
                    A.activation(qh[:, S * c:S * c + S], bank(bk, 0, S), ACT.Copy, scale=XD ** -0.5).then_inc(s_lhi, 1)
                elif kind == "k":
                    A.activation(klh[:, :].rearrange("p (b c t) -> p b c t", b=B, c=NP)[:, :, c, :],
                                 bank(bk).rearrange("p (b t) -> p b t", b=B), ACT.Copy).then_inc(s_lhi, 1)
                else:
                    t, half = c // 2, c % 2
                    A.activation(vl[:, 1024 * t + 512 * half:1024 * t + 512 * half + 512], bank(bk),
                                 ACT.Copy).then_inc(s_lhi, 1)

            def x_exp(s):
                for u in range(2):
                    b, c, i = STEPS[s]
                    k = 32 * b + 16 * i + 2 * c + u
                    slot = (2 * s + u) % 4
                    act.wait_ge(s_mx, 2 * s + u + 1)
                    if s == 0 and u == 0:
                        act.wait_ge(s_lch, len(LCH))
                    if s >= 2:
                        act.wait_ge(s_tr, 3 * (s - 1))
                    A.activation(pr[:, slot * 768:slot * 768 + 768],
                                 ps[:, 2 * u:2 * u + 2, :].rearrange("p a b -> p (a b)")[:, 0:768],
                                 ACT.Exp, bias=negmax[:, (2 * s + u) % 8:(2 * s + u) % 8 + 1],
                                 accum_out=psums[:, k:k + 1]).then_inc(s_ex, 1)

            def x_copy(s):
                act.wait_ge(s_tr, 3 * s + 2)
                if s >= 2:
                    act.wait_ge(s_pv, s - 1)
                p0 = (s % 2) * 1536 + 512
                A.activation(pT[:, p0:p0 + 512], bank(5), ACT.Copy).then_inc(s_cpA, 1)

            for b in range(B):
                s0 = 16 * b
                for s in range(s0, s0 + 16):
                    x_exp(s)
                    if s > s0:
                        x_copy(s - 1)
                x_copy(s0 + 15)
                act.wait_ge(s_rcT, b + 1)
                A.activation(recT[0:16, :], ps[0:16, 4, 0:256], ACT.Copy).then_inc(s_rcS, 1)
                if b == 0:
                    for c in range(NP):
                        act.wait_ge(s_q1, c + 1)
                        A.activation(qh[:, S * c:S * c + S], bank(c % 4, 0, S), ACT.Copy,
                                     scale=XD ** -0.5).then_inc(s_q1h, 1)
            ln_rstd(2)

            g = s_g
            act.wait_ge(s_xn, 3 * NT)
            for t in range(NT):
                last = A.activation(gat[:, P * t:P * t + P], xs[:, P * t:P * t + P], ACT.Square,
                                    accum_out=st[:, 36 + t:37 + t])
            link(last)
            act.wait_ge(g["x2T"], 1)
            A.activation(x2T[:, :], bank(0), ACT.Copy, scale=cols[:, C_L1:C_L1 + 1]).then_inc(g["x2Tsb"], 1)
            rstd(st[:, 40:44], st[:, 36:40], 1.0 / D, e6).then_inc(g["rstd"], 1)
            for b in range(B):
                act.wait_ge(g["sq"], b + 1)
                rstd(rq[:, 320 * b:320 * b + 40], rq[:, 320 * b + 40:320 * b + 80], 1.0 / HD,
                     e6).then_inc(g["rms"], 1)
            hq = rp[:, :].rearrange("p (t n d) -> p t n d", t=NT, n=20)
            qs2 = a2.qs[:, :].rearrange("p (t n r d) -> p t n r d", t=NT, n=16, r=4)
            ks2 = a2.ks[:, :].rearrange("p (t n r d) -> p t n r d", t=NT, n=4, r=4)
            for b in range(B):
                act.wait_ge(g["ss"], b + 1)
                m = slice(2 * b, 2 * b + 2)
                A.activation(qs2[:, m, :, 0, :].bitcast(R), hq[:, m, 0:16, :], ACT.Copy,
                             scale=HD ** -0.5).then_inc(g["e"], 1)
                A.activation(ks2[:, m, :, 0, :].bitcast(R), hq[:, m, 16:20, :], ACT.Copy).then_inc(g["e"], 1)
            act.wait_ge(s_zero, 6)
            A.activation(a2.vp[:, :].rearrange("p (t n c) -> p t n c", t=NT, c=32)[:, :, :, 0:HD],
                         a2.h[:, 0:NT * 192].rearrange("p (t n d) -> p t n d", t=NT, d=HD)[:, :, 20:24, :],
                         ACT.Copy).then_inc(a2.s_vp, 1)
            for b in range(B):
                act.wait_ge(a2.s_T, 10 * b + 8)
                A.activation(a2.qst[:, :].rearrange("p (g t) -> p g t", g=4)[:, :, 256 * b:256 * b + 256],
                             ps[:, 4 * b:4 * b + 2, :].rearrange("p a (g t) -> p (a g) t", g=2),
                             ACT.Copy).then_inc(a2.s_q_ev, 1)
            act_maxrows(act, a2, 0)
            act_maxrows(act, a2, 1)
            for r in range(6):
                if r == 2:
                    act.wait_ge(a2.s_vp, 1)
                act_exp(act, a2, r)
            act.wait_ge(g["OtT"], 1)
            A.activation(a2.ott[:, :], bank(0), ACT.Copy).then_inc(g["ott"], 1)
            act.wait_ge(g["gpre"], 1)
            sigmoid(gat[:, :], gat[:, :]).then_inc(g["e"], 1)
            act.wait_ge(g["gT"], 1)
            A.activation(fT[:, :], bank(2), ACT.Copy).then_inc(g["gTs"], 1)
            act.wait_ge(g["x3"], 1)
            for t in range(NT):
                last = A.activation(gat[:, P * t:P * t + P], x3[:, P * t:P * t + P], ACT.Square,
                                    accum_out=st[:, 36 + t:37 + t])
            link(last)
            rstd(st[:, 44:48], st[:, 36:40], 1.0 / D, e6).then_inc(g["rstd3"], 1)
            act.wait_ge(g["h2T"], 1)
            link(A.activation(h2T[:, :], bank(4), ACT.Copy, scale=cols[:, C_L2:C_L2 + 1]))
            A.activation(h2h[:, :], h2T[:, :], ACT.Copy).then_inc(g["h2Ts"], 1)
            act.wait_ge(s_ldg, 32)
            A.activation(beh[0:NE, :], wbe[0:NE, 0:512], ACT.Copy).then_inc(g["be"], 1)
            act.wait_ge(g["mkT"], 1)
            A.activation(mkT[0:NE, :], ps[0:NE, 6, :], ACT.Copy).then_inc(g["mkTs"], 1)
            A.activation(mkR[0:NE, :], ps[0:NE, 6, :], ACT.Copy).then_inc(g["mkTs"], 1)

            def gate_u(t):
                act.wait_ge(g["u"], t + 1)
                sigmoid(sg[:, HID * t:HID * t + HID], bank(t, 256, 512)).then_inc(g["eu"], 1)

            def act_hi(t):
                act.wait_ge(g["actT"], t + 1)
                A.activation(acTh[:, HID * t:HID * t + HID], bank(6 + t % 2, 0, 256), ACT.Copy).then_inc(g["acTh"], 1)

            for t in range(NT):
                gate_u(t)
            for t in range(NT):
                act_hi(t)
            ln_rstd(3)

        @block.vector
        def _(dve):
            V = nc.vector
            n_dv = [0]

            def v(ins):
                n_dv[0] += 1
                ins.then_inc(s_dv, 1)
                return n_dv[0]

            def need(n):
                dve.wait_ge(s_dv, n)

            mv = st[:, 0:32].rearrange("p (t c) -> p t c", c=2)
            bn = bnst

            def stats(src, tiles, s_done, raw):
                need(n_dv[0])
                for k, t in enumerate(tiles):
                    n = v(V.bn_stats(bn[:, 6 * k:6 * k + 6], src[:, P * t:P * t + P]))
                for k, t in enumerate(tiles):
                    need(n - len(tiles) + 1 + k)
                    last = V.bn_aggr(raw[:, t, :], bn[:, 6 * k:6 * k + 6])
                    if k < len(tiles) - 1:
                        v(last)
                last.then_inc(s_done, 1)

            def ctx_stats(b):
                if b > 0:
                    dve.wait_ge(s_cst, b)
                stats(cx, range(4 * b, 4 * b + 4), s_cst, mv)

            def ctx_apply(b):
                dve.wait_ge(s_crs, b + 1)
                for k in range(4):
                    t = 4 * b + k
                    V.tensor_scalar(cx[:, P * t:P * t + P], cx[:, P * t:P * t + P], mv[:, t, 0:1],
                                    st[:, 32 + t:33 + t], ALU.subtract, ALU.mult).then_inc(s_cln, 1)

            def ctx_low(b):
                dve.wait_ge(s_cTh, b + 1)
                if b == 1:
                    dve.wait_ge(s_cTl, 1)
                n = v(V.tensor_scalar(cX[:, :], bank(b), cols[:, C_G1:C_G1 + 1], cols[:, C_B1:C_B1 + 1],
                                      ALU.mult, ALU.add))
                need(n)
                V.tensor_tensor(cTl[:, SC * b:SC * b + SC], cX[:, :], cTh[:, SC * b:SC * b + SC].bitcast(F),
                                ALU.subtract).then_inc(s_cTl, 1)

            dve.wait_ge(s_ldc, 32)
            ctx_stats(0)
            ctx_stats(1)
            dve.wait_ge(s_const, 3)
            V.tensor_copy(cR[:, 0:P], ident[:, :]).then_inc(s_constR, 1)
            V.tensor_copy(cR[:, P:3 * P], cS[:, :]).then_inc(s_constR, 1)
            dve.wait_ge(s_ldA, 16)
            for t in range(NT):
                dve.wait_ge(s_qkv, t + 1)
                V.tensor_tensor(a1.h[:, 384 * t:384 * t + 384], bank(4 + t, 0, 384), wA[:, A_B1:A_B1 + 384],
                                ALU.add).then_inc(s_h, 1)
            ctx_apply(0)
            ctx_apply(1)
            hv = a1.h[:, :].rearrange("p (n c d) -> p n c d", c=3, d=HD)
            qs = a1.qs[:, :].rearrange("p (n r d) -> p n r d", r=4, d=HD)
            ks = a1.ks[:, :].rearrange("p (n r d) -> p n r d", r=4, d=HD)
            for b in range(B):
                m = slice(32 * b, 32 * b + 32)
                dve.wait_ge(s_kev, 2 * b + 1)
                dve.wait_ge(s_h, 2 * b + 2)
                n = v(V.scalar_tensor_tensor(out=qs[:, m, 1, :], in0=hv[:, m, 0, :], scalar=HD ** -0.5,
                                             in1=qs[:, m, 0, :], op0=ALU.mult, op1=ALU.subtract))
                dve.wait_ge(s_kev, 2 * b + 2)
                n2 = v(V.tensor_tensor(ks[:, m, 2, :], hv[:, m, 1, :], ks[:, m, 0, :], ALU.subtract))
                need(n)
                V.tensor_copy(qs[:, m, 2, :], qs[:, m, 0, :]).then_inc(a1.s_qsplit, 1)
                need(n2)
                V.tensor_copy(ks[:, m, 1, :], ks[:, m, 0, :]).then_inc(a1.s_ksplit, 1)
            ctx_low(0)
            ctx_low(1)
            dve.wait_ge(s_vhi, 1)
            V.tensor_tensor(wkvl[:, 1024:2048], wkv[:, 1024:2048], wkvh[:, 1024:2048].bitcast(F),
                            ALU.subtract).then_inc(s_vlo, 1)

            def k_stack_ev(a, b):
                kg = a.kg
                dve.wait_ge(a.s_T, (8 + 2 * kg) * (b + 1))
                out = a.kst[:, :].rearrange("p (g t) -> p g t", g=kg)[:, :, 256 * b:256 * b + 256]
                if kg > 1:
                    src = ps[:, 4 * b + 2:4 * b + 4, :].rearrange("p a (g t) -> p (a g) t", g=2)
                else:
                    src = ps[:, 4 * b + 2:4 * b + 3, 0:256]
                V.tensor_copy(out, src).then_inc(a.s_k_ev, 1)

            k_stack_ev(a1, 0)
            k_stack_ev(a1, 1)
            dve.wait_ge(s_khi, 1)
            V.tensor_tensor(wkvl[:, 0:1024], wkv[:, 0:1024], wkvh[:, 0:1024].bitcast(F),
                            ALU.subtract).then_inc(s_klo, 1)
            for r in range(6):
                dve_max(dve, a1, r, v, need)

            kn = 0

            def k_lo(m):
                nonlocal kn
                for _ in range(m):
                    c, b = kn // 2, kn % 2
                    dve.wait_ge(s_khi, kn + 2)
                    kk = slice((b * NP + c) * SC, (b * NP + c + 1) * SC)
                    V.tensor_tensor(kcl[:, kk], bank(6 + kn % 2), kch[:, kk].bitcast(F),
                                    ALU.subtract).then_inc(s_kdn, 1)
                    kn += 1

            def ots(a, b):
                dve.wait_ge(a.s_PV, 2 * b + 2)
                if b > 0:
                    dve.wait_ge(a.s_OT, 2 * b)
                V.tensor_copy(a.ots[:, :], ps[:, 4:6, :].rearrange("p a b -> p (a b)")).then_inc(a.s_ots, 1)

            k_lo(6)
            ots(a1, 0)
            k_lo(2)
            dve_norm(dve, a1, 0, v, need)
            k_lo(6)
            ots(a1, 1)
            k_lo(1)
            dve_norm(dve, a1, 1, v, need)
            k_lo(1)

            def layernorm(k, src, dst, s_done):
                dve.wait_ge(s_st, k) if k else dve.wait_ge(s_cst, 2)
                stats(src, range(NT), s_st, mv)
                dve.wait_ge(s_rs, k + 1)
                for t in range(NT):
                    V.tensor_scalar(dst[:, P * t:P * t + P], src[:, P * t:P * t + P], mv[:, t, 0:1],
                                    st[:, 32 + t:33 + t], ALU.subtract, ALU.mult).then_inc(s_done, 1)

            dve.wait_ge(s_ldx, 16)
            n = v(V.tensor_tensor(xs[:, :].rearrange("p (t d) -> p t d", t=NT),
                                  xs[:, :].rearrange("p (t d) -> p t d", t=NT),
                                  wA[:, A_BP:A_BP + P].unsqueeze(1).to_broadcast([P, NT, P]), ALU.add))
            need(n)
            dve.wait_ge(s_pj, 1)
            n = v(V.tensor_tensor(xs[:, :], bank(1), xs[:, :], ALU.add))
            need(n)
            layernorm(0, xs, xs, s_xn)
            dve.wait_ge(s_xn, NT)
            layernorm(1, xs, ln, s_xn)
            dve.wait_ge(s_lnTs, 1)
            V.tensor_tensor(lnTl[:, :], lnT[:, :], lnTh[:, :].bitcast(F), ALU.subtract).then_inc(s_lnTs, 1)
            for n, (kind, c) in enumerate(LCH):
                if kind == "v":
                    continue
                dve.wait_ge(s_lhi, n + 1)
                bk = n % 8
                if kind == "q":
                    V.scalar_tensor_tensor(out=ql[:, S * c:S * c + S], in0=bank(bk, 0, S), scalar=XD ** -0.5,
                                           in1=qh[:, S * c:S * c + S].bitcast(F), op0=ALU.mult,
                                           op1=ALU.subtract).then_inc(s_llo, 1)
                else:
                    vv = lambda z: z[:, :].rearrange("p (b c t) -> p b c t", b=B, c=NP)[:, :, c, :]
                    V.tensor_tensor(vv(kll), bank(bk).rearrange("p (b t) -> p b t", b=B), vv(klh).bitcast(F),
                                    ALU.subtract).then_inc(s_llo, 1)

            def x_max(s):
                for u in range(2):
                    dve.wait_ge(s_S, 2 * s + u + 1)
                    if s >= 4:
                        dve.wait_ge(s_ex, 2 * (s - 4) + u + 1)
                    k = (2 * s + u) % 8
                    V.tensor_reduce(negmax[:, k:k + 1],
                                    ps[:, 2 * u:2 * u + 2, :].rearrange("p a b -> p (a b)")[:, 0:768],
                                    X, ALU.max, negate=True).then_inc(s_mx, 1)

            def x_copies(s):
                if s >= 2:
                    dve.wait_ge(s_pv, s - 1)
                for m in (0, 2):
                    dve.wait_ge(s_tr, 3 * s + m + 1)
                    p0 = (s % 2) * 1536 + 512 * m
                    V.tensor_copy(pT[:, p0:p0 + 512], bank(4 + m)).then_inc(s_cpD, 1)

            def x_out(s):
                b, c, i = STEPS[s]
                dve.wait_ge(s_pv, s + 1)
                V.tensor_copy(ot[:, S * c + P * i:S * c + P * i + P], bank(7, 0, P)).then_inc(s_oev, 1)

            for b in range(B):
                s0 = 16 * b
                for s in range(s0, s0 + 16):
                    x_max(s)
                    if s > s0:
                        x_copies(s - 1)
                    if s > s0 + 1:
                        x_out(s - 2)
                x_copies(s0 + 15)
                dve.wait_ge(s_ex, 2 * s0 + 32)
                V.reciprocal(rc[:, 32 * b:32 * b + 32], psums[:, 32 * b:32 * b + 32]).then_inc(s_rc, 1)
                x_out(s0 + 14)
                x_out(s0 + 15)
                dve.wait_ge(s_oev, s0 + 16)
                for c in range(4):
                    dve.wait_ge(s_R, 8 * b + 2 * c + 2)
                    V.tensor_tensor(ot[:, 512 * c:512 * c + 512], bank(c), ot[:, 512 * c:512 * c + 512],
                                    ALU.mult).then_inc(s_on, 1)
                dve.wait_ge(s_xo, b + 1)
                n = v(V.tensor_tensor(xs[:, S * b:S * b + S], bank(5, 0, S), xs[:, S * b:S * b + S], ALU.add))
                need(n)
                if b == 0:
                    for c in range(NP):
                        dve.wait_ge(s_q1h, c + 1)
                        V.scalar_tensor_tensor(out=ql[:, S * c:S * c + S], in0=bank(c % 4, 0, S), scalar=XD ** -0.5,
                                               in1=qh[:, S * c:S * c + S].bitcast(F), op0=ALU.mult,
                                               op1=ALU.subtract).then_inc(s_q1l, 1)
            layernorm(2, xs, xs, s_xn)

            g = s_g
            dve.wait_ge(g["rstd"], 1)
            dve.wait_ge(s_ldg, 32)
            for t in range(NT):
                dve.wait_ge(g["qkv"], t + 1)
                V.scalar_tensor_tensor(out=a2.h[:, 192 * t:192 * t + 192], in0=bank(4 + t, 0, 192),
                                       scalar=st[:, 40 + t:41 + t], in1=wG[:, G_BQKV:G_BQKV + 192],
                                       op0=ALU.mult, op1=ALU.add).then_inc(g["h"], 1)
            hh = a2.h[:, 0:NT * 192].rearrange("p (t n d) -> p t n d", t=NT, d=HD)
            rope = wG[:, G_ROPE:G_ROPE + 32].rearrange("p (t k d) -> p t k d", t=2, k=2)
            rpv = rp[:, :].rearrange("p (t n d) -> p t n d", t=NT, d=HD)
            qn = wG[:, G_QN:G_QN + 160]
            dve.wait_ge(g["h"], 4)
            for b in range(B):
                n0 = []
                for i in range(2):
                    t = 2 * b + i
                    src = hh[:, t, 0:20, :]
                    tmp = rq[:, 160 * t:160 * t + 160].rearrange("p (n d) -> p n d", d=HD)
                    v(V.tensor_tensor(rpv[:, t, :, :], src, rope[:, i, 0:1, :].to_broadcast([P, 20, HD]), ALU.mult))
                    v(V.tensor_tensor(tmp[:, :, 0:4], src[:, :, 4:8], rope[:, i, 1:2, 0:4].to_broadcast([P, 20, 4]),
                                      ALU.mult))
                    n0.append(v(V.tensor_tensor(tmp[:, :, 4:8], src[:, :, 0:4],
                                                rope[:, i, 1:2, 4:8].to_broadcast([P, 20, 4]), ALU.mult)))
                need(n0[1])
                w = slice(320 * b, 320 * b + 320)
                n = v(V.tensor_tensor(rp[:, w], rp[:, w], rq[:, w], ALU.add))
                need(n)
                n = v(V.tensor_tensor(rq[:, w], rp[:, w], rp[:, w], ALU.mult))
                need(n)
                ssq = st[:, 44:84]
                n = v(V.tensor_reduce(ssq, rq[:, w].rearrange("p (n d) -> p n d", d=HD), X, ALU.add))
                need(n)
                V.tensor_copy(rq[:, 320 * b + 40:320 * b + 80], ssq).then_inc(g["sq"], 1)
                dve.wait_ge(g["rms"], b + 1)
                n = v(V.tensor_tensor(rp[:, w].rearrange("p (n d) -> p n d", d=HD),
                                      rp[:, w].rearrange("p (n d) -> p n d", d=HD),
                                      rq[:, 320 * b:320 * b + 40].unsqueeze(2).to_broadcast([P, 40, HD]), ALU.mult))
                need(n)
                V.tensor_tensor(rp[:, w].rearrange("p (t c) -> p t c", t=2),
                                rp[:, w].rearrange("p (t c) -> p t c", t=2),
                                qn.unsqueeze(1).to_broadcast([P, 2, 160]), ALU.mult).then_inc(g["ss"], 1)
            qs2 = a2.qs[:, :].rearrange("p (t n r d) -> p t n r d", t=NT, n=16, r=4)
            ks2 = a2.ks[:, :].rearrange("p (t n r d) -> p t n r d", t=NT, n=4, r=4)
            for b in range(B):
                m = slice(2 * b, 2 * b + 2)
                dve.wait_ge(g["e"], 2 * b + 1)
                n = v(V.scalar_tensor_tensor(out=qs2[:, m, :, 1, :], in0=rpv[:, m, 0:16, :], scalar=HD ** -0.5,
                                             in1=qs2[:, m, :, 0, :], op0=ALU.mult, op1=ALU.subtract))
                dve.wait_ge(g["e"], 2 * b + 2)
                n2 = v(V.tensor_tensor(ks2[:, m, :, 2, :], rpv[:, m, 16:20, :], ks2[:, m, :, 0, :], ALU.subtract))
                need(n)
                q3 = a2.qs[:, 1024 * b:1024 * b + 1024].rearrange("p (n r d) -> p n r d", r=4, d=HD)
                V.tensor_copy(q3[:, :, 2, :], q3[:, :, 0, :]).then_inc(a2.s_qsplit, 1)
                need(n2)
                k3 = a2.ks[:, 256 * b:256 * b + 256].rearrange("p (n r d) -> p n r d", r=4, d=HD)
                V.tensor_copy(k3[:, :, 1, :], k3[:, :, 0, :]).then_inc(a2.s_ksplit, 1)
            k_stack_ev(a2, 0)
            k_stack_ev(a2, 1)
            for r in range(6):
                dve_max(dve, a2, r, v, need)
            ots(a2, 0)
            dve_norm(dve, a2, 0, v, need)
            ots(a2, 1)
            dve_norm(dve, a2, 1, v, need)
            bc = lambda ap: ap.unsqueeze(1).to_broadcast([P, NT, P])
            t3 = lambda z: z.rearrange("p (t d) -> p t d", t=NT)
            dve.wait_ge(g["gl"], 1)
            V.tensor_tensor(t3(gat[:, :]), t3(bank(1)), bc(wG[:, G_BG:G_BG + P]), ALU.add).then_inc(g["gpre"], 1)
            dve.wait_ge(g["e"], 5)
            V.tensor_tensor(a2.otok[:, :], a2.otok[:, :], gat[:, :], ALU.mult).then_inc(g["gated"], 1)
            n = v(V.tensor_tensor(t3(x3[:, :]), t3(xs[:, :]), bc(wG[:, G_BO:G_BO + P]), ALU.add))
            need(n)
            dve.wait_ge(g["wo"], 1)
            V.tensor_tensor(x3[:, :], bank(3), x3[:, :], ALU.add).then_inc(g["x3"], 1)
            dve.wait_ge(g["rstd3"], 1)
            for t in range(NT):
                V.tensor_scalar(h2[:, P * t:P * t + P], x3[:, P * t:P * t + P], st[:, 44 + t:45 + t], None,
                                ALU.mult).then_inc(g["h2"], 1)
            n = v(V.tensor_tensor(xs[:, :], xs[:, :], x3[:, :], ALU.add))
            dve.wait_ge(g["h2Ts"], 1)
            l3 = lg[:, 0:32].rearrange("p (t e) -> p t e", t=NT)
            l4 = lg[:, 32:64].rearrange("p (t e) -> p t e", t=NT)
            dve.wait_ge(g["lg"], 1)
            n = v(V.tensor_tensor(l3, bank(5, 0, 32).rearrange("p (t e) -> p t e", t=NT),
                                  wG[:, G_BR:G_BR + NE].unsqueeze(1).to_broadcast([P, NT, NE]), ALU.add))
            need(n)
            n = v(V.tensor_reduce(st[:, 48:52], l3, X, ALU.max))
            need(n)
            n = v(V.tensor_tensor(l4, l3, st[:, 48:52].unsqueeze(2).to_broadcast([P, NT, NE]), ALU.is_equal))
            need(n)
            n = v(V.tensor_tensor(l3, l4, wG[:, G_RK:G_RK + NE].unsqueeze(1).to_broadcast([P, NT, NE]), ALU.mult))
            need(n)
            n = v(V.tensor_reduce(st[:, 52:56], l3, X, ALU.max))
            need(n)
            V.tensor_tensor(mk[:, :].rearrange("p (t e) -> p t e", t=NT), l3,
                            st[:, 52:56].unsqueeze(2).to_broadcast([P, NT, NE]), ALU.is_equal).then_inc(g["mk"], 1)
            n = v(V.tensor_tensor(h2[:, :], h2T[:, :], h2h[:, :].bitcast(F), ALU.subtract))
            dve.wait_ge(g["be"], 1)
            V.tensor_tensor(bel[0:NE, :], wbe[0:NE, 0:512], beh[0:NE, :].bitcast(F), ALU.subtract).then_inc(g["be"], 1)
            need(n)
            for e in range(NE):
                dve.wait_ge(g["bc"], e + 1)
                w = slice(512 * e, 512 * e + 512)
                V.tensor_tensor(xmh[:, w], bank(4 + e % 4), h2h[:, :].bitcast(F), ALU.mult).then_inc(g["xm"], 1)
                V.tensor_tensor(xml[:, w], bank(4 + e % 4), h2[:, :], ALU.mult).then_inc(g["xm"], 1)
            dve.wait_ge(g["b2"], 1)
            V.tensor_tensor(xs[:, :], bank(7), xs[:, :], ALU.add).then_inc(g["b2r"], 1)

            def gated_u(t):
                w = slice(HID * t, HID * t + HID)
                dve.wait_ge(g["eu"], t + 1)
                V.tensor_tensor(actf[:, w], bank(t, 0, 256), sg[:, w], ALU.mult).then_inc(g["act"], 1)

            def act_low(t):
                w = slice(HID * t, HID * t + HID)
                dve.wait_ge(g["acTh"], t + 1)
                V.tensor_tensor(acTl[:, w], bank(6 + t % 2, 0, 256), acTh[:, w].bitcast(F),
                                ALU.subtract).then_inc(g["acTl"], 1)

            def choose(t):
                for half in range(2):
                    dve.wait_ge(g["y"], 2 * t + half + 1)
                    V.tensor_tensor(
                        prod[:, 1024 * (t % 2) + 512 * half:1024 * (t % 2) + 512 * half + 512].rearrange(
                            "p (e d) -> p e d", e=4),
                        bank(4 - 4 * (t % 2) + half).rearrange("p (e d) -> p e d", e=4),
                        mk[:, NE * t + 4 * half:NE * t + 4 * half + 4].unsqueeze(2).to_broadcast([P, 4, P]),
                        ALU.mult).then_inc(g["yr"], 1)
                dve.wait_ge(g["yr"], 2 * t + 2)
                n = v(V.tensor_reduce(yv[:, P * t:P * t + P],
                                      prod[:, 1024 * (t % 2):1024 * (t % 2) + 1024].rearrange("p (e d) -> p d e", e=NE),
                                      X, ALU.add))
                need(n)
                return v(V.tensor_tensor(xs[:, P * t:P * t + P], xs[:, P * t:P * t + P], yv[:, P * t:P * t + P],
                                         ALU.add))

            dve.wait_ge(g["b2r"], 1)
            for t in range(NT):
                gated_u(t)
            act_low(0)
            act_low(1)
            choose(0)
            act_low(2)
            choose(1)
            act_low(3)
            choose(2)
            n = choose(3)
            need(n)
            layernorm(3, xs, xs, g["v"])


def kernel(**inputs):
    import numpy as np
    import concourse.bacc as bacc
    from concourse import mybir as mb
    from concourse.bass_utils import run_bass_kernel_spmd

    a = {k: np.asarray(v) for k, v in inputs.items()}
    f32 = np.float32

    def rows(v):
        return np.broadcast_to(v.reshape(1, -1), (P, v.size))

    def tiles(m):
        t = m.shape[0] // P
        return m.reshape(t, P, -1).transpose(1, 0, 2).reshape(P, -1)

    x = a["x"].reshape(B * S, D)
    d_a = np.concatenate([x.T, a["L0_attn_W1"], rows(a["L0_attn_b1"]), a["L0_attn_Wp"], rows(a["L0_attn_bp"])], 1)
    def gm(m):
        return m.reshape(-1, KV, H // KV, HD).transpose(0, 2, 1, 3).reshape(m.shape[0], -1)
    wq, bq = gm(a["L0_ffn_Wq"]), gm(a["L0_ffn_bq"].reshape(1, -1))
    wo = gm(a["L0_ffn_Wo"].T).T
    pos = np.arange(S, dtype=f32).reshape(2, P)
    inv = (1.0 / 10000.0 ** (np.arange(0, HD, 2, dtype=f32) / HD)).astype(f32)
    ang = (pos[:, :, None] * inv).astype(f32)
    cos, sin = np.cos(ang).astype(f32), np.sin(ang).astype(f32)
    rope = np.stack([np.concatenate([cos, cos], -1), np.concatenate([-sin, sin], -1)], 1)
    rope = rope.transpose(2, 0, 1, 3).reshape(P, -1)
    wg = np.zeros((P, P), f32)
    for h in range(H):
        wg[HD * h:HD * h + HD, HD * h:HD * h + HD] = a["L0_ffn_Wg"]
    d_g = np.concatenate([
        wq, a["L0_ffn_Wk"], a["L0_ffn_Wv"], rows(bq), rows(a["L0_ffn_bk"]), rows(a["L0_ffn_bv"]), rope,
        rows(np.concatenate([np.tile(a["L0_ffn_qn_w"], 16), np.tile(a["L0_ffn_kn_w"], 4)])),
        wg, rows(np.tile(a["L0_ffn_bg"], H)), wo, rows(a["L0_ffn_bo"]), a["L0_ffn_Wr"], rows(a["L0_ffn_br"]),
        rows(np.arange(NE, 0, -1).astype(f32))], 1)
    col = np.stack([a["L0_xattn_g1"], a["L0_xattn_b1"], a["L0_xattn_g2"], a["L0_xattn_b2"], a["L0_ffn_ln1_w"],
                    a["L0_ffn_ln2_w"], np.full(P, 1e-5, f32), np.full(P, 1e-6, f32)], 1)
    arrays = {
        "d_a": d_a, "d_x": tiles(x), "d_ctx": tiles(a["ctx_1024"].reshape(B * SC, D)), "d_cols": col,
        "d_wkv": a["L0_xattn_Wkv"], "d_wq": a["L0_xattn_Wq"], "d_wout": tiles(a["L0_xattn_Wout"]), "d_g": d_g,
        "d_we1": a["L0_ffn_W1"].transpose(1, 0, 2).reshape(D, -1),
        "d_we2": a["L0_ffn_W2"].reshape(NE, 2, P, D).transpose(2, 1, 0, 3).reshape(P, -1),
        "d_be": np.concatenate([a["L0_ffn_b1"], a["L0_ffn_b2"]], 1),
    }
    arrays = {k: np.ascontiguousarray(v) for k, v in arrays.items()}
    nc = bacc.Bacc("TRN2", target_bir_lowering=False, num_devices=1)
    args = [nc.dram_tensor(k, v.shape, mb.dt.from_np(v.dtype), kind="ExternalInput").ap() for k, v in arrays.items()]
    out = nc.dram_tensor("d_out", (P, NT * D), mb.dt.from_np(np.dtype(f32)), kind="ExternalOutput").ap()
    decoder_layer(nc, *args, out)
    r = run_bass_kernel_spmd(nc, [arrays], core_ids=[0])
    y = r.results[0]["d_out"]
    return y.reshape(P, NT, D).transpose(1, 0, 2).reshape(B, S, D)
```

```python
import concourse.bass as bass
from concourse import mybir
from contextlib import ExitStack

F = mybir.dt.float32
R = mybir.dt.float32r
ACT = mybir.ActivationFunctionType
ALU = mybir.AluOpType
X = mybir.AxisListType.X

P = 128
NEG = -2.0 ** 100
KB = 1024

B, S, D, SC = 2, 256, 128, 512
NT = B * S // P
H, HD = 16, 8
XH, XD = 16, 64
NP = XH // 2
CT = SC // P
KT = CT + S // P
NE, HID = 8, 256
KV = 4

A_XT, A_W1, A_B1, A_WP, A_BP, A_N = 0, 512, 896, 1280, 1408, 1536
G_QKV, G_BQKV, G_ROPE, G_QN, G_WG, G_BG, G_WO, G_BO, G_WR, G_BR, G_RK, G_N = (
    0, 192, 384, 416, 576, 704, 832, 960, 1088, 1096, 1104, 1112)
C_G1, C_B1, C_G2, C_B2, C_L1, C_L2, C_E5, C_E6 = range(8)


class Attn:
    pass


def decoder_layer(nc, d_a, d_x, d_ctx, d_cols, d_wkv, d_wq, d_wout, d_g, d_we1, d_we2, d_be, d_out):
    ctx = ExitStack()
    with ctx:
        def sem(name):
            return ctx.enter_context(nc.semaphore(name))

        base = 16512

        def at(name, cols, dt, off):
            return nc.alloc_sbuf_tensor_at(name, [P, cols], dt, offset=base + off)

        ident = at("ident", P, F, 0)
        cR = at("const_r", 3 * P, R, 512)
        xs = at("xs", NT * D, F, 2112)
        lnT = at("lnT", B * S, F, 4160)
        recT = at("recT", 2 * P, F, 4160)
        xq_w = at("xq_w", XH * XD, F, 6208)
        st = at("stats", 256, F, 10304)
        cols = at("cols", 8, F, 11328)
        bnst = at("bn_stats", 32, F, 11360)
        negmax = at("negmax", 8, F, 11488)
        rc = at("rc", 64, F, 11616)
        psums = st[:, 64:128]
        o_w = 11904
        o_ot = 16000
        o_q = 24192
        o_sc = 40576
        o_kch = 65152
        o_kcl = o_kch + 32 * KB
        o_vc = o_kcl + 32 * KB
        o_klh = o_vc + 32 * KB
        o_kll = o_klh + 16 * KB
        o_vl = o_kll + 16 * KB
        assert base + o_vl + 16 * KB <= 229344

        kch = at("kc_hi", B * NP * SC, R, o_kch)
        kcl = at("kc_lo", B * NP * SC, R, o_kcl)
        vc = at("vc", B * CT * XH * XD, F, o_vc)
        klh = at("kl_hi", B * NP * S, R, o_klh)
        kll = at("kl_lo", B * NP * S, R, o_kll)
        vl = at("vl", B * 2 * XH * XD, F, o_vl)
        qh = at("q_hi", NP * S, R, o_q)
        ql = at("q_lo", NP * S, R, o_q + 8 * KB)
        xout_w = at("xout_w", NP * D, F, o_w)
        ot = at("ot", NP * S, F, o_ot)
        pr = at("probs", 4 * 6 * P, F, o_sc)
        pT = at("probsT", 2 * 12 * P, F, o_sc + 12 * KB)
        wkvh = at("wkv_hi", 2048, R, o_sc)
        wkvl = at("wkv_lo", 2048, R, o_sc + 8 * KB)
        cTh = at("ctxT_hi", B * SC, R, o_sc + 16 * KB)
        cTl = at("ctxT_lo", B * SC, R, o_sc + 20 * KB)
        lnTh = at("lnT_hi", B * S, R, o_sc + 16 * KB)
        lnTl = at("lnT_lo", B * S, R, o_sc + 18 * KB)
        wkv = at("wkv_raw", 2048, F, o_q)
        wA = at("wA", A_N, F, o_q + 8 * KB)
        ln = at("ln_tok", NT * D, F, o_q + 14 * KB)
        cx = at("ctx_tok", B * SC, F, o_ot)
        cS = at("const_f", 2 * P, F, o_kcl)
        cX = at("ctxT_f", SC, F, o_kch)

        ps = ctx.enter_context(nc.psum_tensor("ps", [P, 8, 512], F))

        def bank(n, a=0, b=512):
            return ps[:, n, a:b]

        idR = cR[:, 0:P]
        up = cR[:, P:2 * P]
        low = cR[:, 2 * P:3 * P]

        def attn_buffers(tag, o_qst, o_kst, o_vp, o_pt, o_ots, o_otok, o_ott, o_qs, o_ks, o_h, kgroups):
            a = Attn()
            a.s_qsplit, a.s_ksplit = sem(tag + "q_split"), sem(tag + "k_split")
            a.s_T, a.s_q_ev, a.s_k_ev = sem(tag + "transposed"), sem(tag + "q_ready"), sem(tag + "k_ready")
            a.s_vp = sem(tag + "v_padded")
            a.s_S, a.s_max, a.s_nm = sem(tag + "scores"), sem(tag + "max_taken"), sem(tag + "negmax_split")
            a.s_q2T, a.s_q2a, a.s_q2d = (sem(tag + n) for n in (
                "q_with_max_T", "q_with_max_ready_act", "q_with_max_ready_dve"))
            a.s_ST, a.s_E, a.s_PV = sem(tag + "scores_t"), sem(tag + "exp_done"), sem(tag + "pv_done")
            a.s_ots, a.s_OT, a.s_O = sem(tag + "o_copied"), sem(tag + "o_untransposed"), sem(tag + "o_normed")
            a.kg = kgroups
            a.qst = at(tag + "qst", 4 * 512, R, o_qst)
            a.kst = at(tag + "kst", 2048, R, o_kst)
            a.vh = 4 * kgroups
            a.vp = at(tag + "vpad", NT * a.vh * 32, F, o_vp)
            a.pt = [at(f"{tag}pt{i}", 2048, F, o_pt[i]) for i in range(3)]
            a.ots = at(tag + "ots", 1024, F, o_ots)
            a.otok = at(tag + "otok", NT * P, F, o_otok)
            a.ott = at(tag + "ott", NT * P, F, o_ott)
            a.qs = at(tag + "qs", NT * 512, F, o_qs)
            a.ks = at(tag + "ks", NT * kgroups * P, F, o_ks)
            a.h = at(tag + "h", NT * (P + 64 * kgroups), F, o_h)
            return a

        LAT = o_klh
        a1 = attn_buffers("sa_", LAT + 24 * KB, LAT + 32 * KB, LAT + 40 * KB,
                          [LAT, LAT + 8 * KB, LAT + 16 * KB], o_ot + 4 * KB,
                          o_q, o_q + 2 * KB, LAT, LAT + 8 * KB, LAT + 16 * KB, 4)
        f0 = o_kch + 16 * KB
        f1 = o_kcl + 16 * KB
        f2 = o_vc + 16 * KB
        e1, e2 = o_kch, o_klh
        a2 = attn_buffers("ga_", f0, f0 + 8 * KB, e2 + 2 * KB, [f1, f1 + 8 * KB, f2],
                          f2 + 8 * KB, f2 + 12 * KB, f2 + 14 * KB, e1 + 8 * KB, e2, e1 + 5 * KB, 1)
        rp = at("rope_out", NT * 160, F, e1)
        rq = at("rope_tmp", NT * 160, F, e1 + 2560)
        x2T = at("x2T", NT * D, F, e2 + 4 * KB)
        wG = at("wG", G_N, F, 5184)
        wbe = at("wbe", 640, F, o_w)
        w1r = at("w1_raw", NE * 512, F, o_kch)
        w1h = at("w1_hi", NE * 512, R, o_kcl)
        w1l = at("w1_lo", NE * 512, R, o_vc)
        w2r = at("w2_raw", NE * 256, F, o_klh)
        w2h = at("w2_hi", NE * 256, R, o_kll)
        w2l = at("w2_lo", NE * 256, R, o_vl)
        beh = at("be_hi", 512, R, o_kll + 8 * KB)
        bel = at("be_lo", 512, R, o_kll + 10 * KB)
        x3 = at("x3", NT * D, F, o_kll + 12 * KB)
        xmh = [at("xm_hi0", NE * S, R, o_klh + 8 * KB), at("xm_hi1", NE * S, R, f1)]
        xml = [at("xm_lo0", NE * S, R, o_vl + 8 * KB), at("xm_lo1", NE * S, R, f1 + 8 * KB)]
        mkB = at("mask_rows", 1024, F, o_ot + 2 * KB)
        h2l = at("h2T_lo", NT * D, F, o_kll + 14 * KB)
        sc = o_sc
        h2 = at("h2_tok", NT * D, F, sc)
        h2T = at("h2T", NT * D, F, sc + 2 * KB)
        gat = at("gate", NT * D, F, sc + 4 * KB)
        lg = at("logits", 3 * NT * NE, F, sc + 6 * KB)
        mk = at("mask", NT * NE, F, sc + 6 * KB + 512)
        mkT = at("maskT", NT * P, F, sc + 8 * KB)
        mkR = at("maskT_r", NT * P, R, sc + 10 * KB)
        sg = at("sig", NT * HID, F, sc + 12 * KB)
        actf = at("act", NT * HID, F, sc + 16 * KB)
        acTh = at("actT_hi", NT * HID, R, sc + 20 * KB)
        acTl = at("actT_lo", NT * HID, R, o_q)
        prod = at("prod", 2 * 1024, F, o_q + 4 * KB)
        yv = at("y", NT * D, F, o_q + 12 * KB)
        h2h = at("h2T_hi", NT * D, R, o_q + 14 * KB)
        fT = at("gatedT", NT * D, F, o_ot)

        s_ldA, s_ldx, s_ldc, s_ldv, s_ldk, s_ldq, s_ldo = (sem(n) for n in (
            "ld_self_attn", "ld_x", "ld_ctx", "ld_wv", "ld_wk", "ld_wq", "ld_wout"))
        s_ldg, s_ldb, s_ld1, s_ld2, s_store = (sem(n) for n in ("ld_ffn", "ld_be", "ld_w1", "ld_w2", "store"))
        s_c0, s_const, s_zero, s_constR = (sem(n) for n in ("const0", "const", "zeroed", "const_r_ready"))
        s_dv, s_ac, s_po = sem("dve_chain"), sem("act_chain"), sem("pool_chain")
        s_vhi, s_vlo, s_khi, s_klo = (sem(n) for n in ("wv_hi", "wv_lo", "wk_hi", "wk_lo"))
        s_cst, s_crs, s_cln, s_cT, s_cTh, s_cTl = (sem(n) for n in (
            "ctx_stats", "ctx_rstd", "ctx_ln", "ctx_T", "ctxT_hi_ready", "ctxT_ready"))
        s_qkv, s_h = sem("qkv"), sem("h")
        s_vch, s_vev, s_kch, s_kev, s_kdn = (sem(n) for n in (
            "v_chunk", "v_evacuated", "k_chunk", "k_hi_done", "k_done"))
        s_OtT, s_ott, s_pj, s_x1p = (sem(n) for n in ("o_T", "o_T_sb", "proj", "x_pre"))
        s_st, s_rs, s_xn = sem("ln_stats"), sem("ln_rstd"), sem("ln_done")
        s_lnT, s_lnTf, s_lnTs = sem("lat_T"), sem("lat_T_sb"), sem("lat_T_split")
        s_lch, s_lhi, s_llo = sem("lat_chunk"), sem("lat_hi"), sem("lat_done")
        s_S, s_mx, s_ex, s_tr, s_cpA, s_cpD, s_pv, s_oev = (sem(n) for n in (
            "x_scores", "x_max", "x_exp", "x_transposed", "x_copied_act", "x_copied_dve", "x_pv", "x_o_evacuated"))
        s_rc, s_rcT, s_rcS, s_R, s_on, s_xo, s_xadd = (sem(n) for n in (
            "x_recip", "x_recip_T", "x_recip_sb", "x_recip_bcast", "x_normed", "x_out", "x_added"))
        s_q1, s_q1h, s_q1l = sem("q_chunk"), sem("q_hi_done"), sem("q_done")
        s_w1h, s_w1l, s_w2h, s_w2l = (sem(n) for n in ("w1_hi_done", "w1_lo_done", "w2_hi_done", "w2_lo_done"))
        s_g = {n: sem("g_" + n) for n in (
            "x2T", "x2Tsb", "ss", "rstd", "qkv", "h", "sq", "rms", "OtT", "ott", "gl", "gpre", "e", "gated", "gT",
            "gTs", "wo", "x3", "lgr", "hr", "rstd3", "h2", "h2T", "h2Ts", "h2h", "lg", "mk", "mkT", "mkTs", "bc", "xm",
            "hi", "mb", "sum", "low", "xml", "be", "b2r", "u", "eu", "act", "actT", "acTh", "acTl", "y", "yr", "b2", "v")}

        STEPS = [(b, c, i) for b in range(B) for c in range(NP) for i in range(2)]
        NS = len(STEPS)
        SLOT = {}
        for _c in range(NP):
            SLOT[2 * _c + 2] = ("q", _c)
        for _b in range(B):
            for _n in range(3):
                SLOT[16 * _b + 4 * _n + 5] = ("rc", _b, _n)
                SLOT[16 * _b + 4 * _n + 7] = ("R", _b, _n)
        SLOT[17] = ("rc", 0, 3)
        SLOT[18] = ("R", 0, 3)
        SLOT[26] = ("x2T", 0)
        SLOT[28] = ("qkv", 0)
        LCH = [x for c in range(NP) for x in (("q", c), ("k", c))] + [("v", n) for n in range(8)]

        block = ctx.enter_context(nc.Block())

        @block.sync
        def _(sp):
            sp.dma_start(wA[:, :], d_a).then_inc(s_ldA, 16)
            sp.dma_start(cx[:, :], d_ctx).then_inc(s_ldc, 16)
            sp.dma_start(wkv[:, 1024:2048], d_wkv[:, 1024:2048]).then_inc(s_ldv, 16)
            sp.dma_start(xq_w[:, :], d_wq).then_inc(s_ldq, 16)
            sp.dma_start(xout_w[:, :], d_wout).then_inc(s_ldo, 16)
            sp.wait_ge(s_pv, 16)
            sp.dma_start(w1r[:, :], d_we1).then_inc(s_ld1, 16)
            sp.dma_start(w2r[:, :], d_we2).then_inc(s_ld2, 16)
            sp.wait_ge(s_q1, NP)
            sp.dma_start(wG[:, :], d_g).then_inc(s_ldg, 16)
            sp.wait_ge(s_xo, B)
            sp.dma_start(wbe[0:NE, :], d_be).then_inc(s_ldb, 16)
            for b in range(B):
                sp.wait_ge(s_g["v"], 2 * b + 2)
                sp.dma_start(d_out[:, S * b:S * b + S], xs[:, S * b:S * b + S]).then_inc(s_store, 16)
            sp.wait_ge(s_store, 16 * B)

        @block.gpsimd
        def _(pool):
            def max_slots(a):
                pool.memset(a.qs[:, :].rearrange("p (n r d) -> p n r d", r=4, d=HD)[:, :, 3, :], 0.0).then_inc(s_zero, 1)
                pool.memset(a.ks[:, :].rearrange("p (n r d) -> p n r d", r=4, d=HD)[:, :, 3, :], 1.0).then_inc(s_zero, 1)

            pool.memset(ident[:, :], 0.0).then_inc(s_c0, 1)
            pool.memset(cS[:, :], 0.0).then_inc(s_c0, 1)
            pool.wait_ge(s_c0, 2)
            pool.affine_select(out=ident[:, :], in_=ident[:, :], compare_op=ALU.not_equal, fill=1.0,
                               base=0, pattern=[[-1, P]], channel_multiplier=1).then_inc(s_const, 1)
            pool.affine_select(out=cS[:, 0:P], in_=cS[:, 0:P], compare_op=ALU.is_ge, fill=NEG,
                               base=0, pattern=[[-1, P]], channel_multiplier=1).then_inc(s_const, 1)
            pool.affine_select(out=cS[:, P:2 * P], in_=cS[:, P:2 * P], compare_op=ALU.is_ge, fill=NEG,
                               base=0, pattern=[[1, P]], channel_multiplier=-1).then_inc(s_const, 1)
            max_slots(a1)
            pool.memset(a1.vp[:, :], 0.0).then_inc(s_po, 1)
            pool.wait_ge(s_po, 1)
            pool.memset(a1.vp[:, :].rearrange("p (n c) -> p n c", c=32)[:, :, HD:HD + 1], 1.0).then_inc(s_zero, 1)
            pool.wait_ge(s_ld1, 16)
            for e in range(NE):
                w = slice(512 * e, 512 * e + 512)
                pool.tensor_copy(w1h[:, w], w1r[:, w]).then_inc(s_w1h, 1)
                pool.wait_ge(s_w1h, e + 1)
                pool.tensor_tensor(w1l[:, w], w1r[:, w], w1h[:, w].bitcast(F), ALU.subtract).then_inc(s_w1l, 1)
            pool.wait_ge(s_ld2, 16)
            for e in range(4):
                w = slice(512 * e, 512 * e + 512)
                pool.tensor_copy(w2h[:, w], w2r[:, w]).then_inc(s_w2h, 1)
                pool.wait_ge(s_w2h, e + 1)
                pool.tensor_tensor(w2l[:, w], w2r[:, w], w2h[:, w].bitcast(F), ALU.subtract).then_inc(s_w2l, 1)
            pool.wait_ge(s_w1l, NE)
            pool.wait_ge(s_w2l, 4)
            max_slots(a2)
            pool.memset(a2.vp[:, :], 0.0).then_inc(s_po, 1)
            pool.wait_ge(s_po, 2)
            pool.memset(a2.vp[:, :].rearrange("p (n c) -> p n c", c=32)[:, :, HD:HD + 1], 1.0).then_inc(s_zero, 1)
            pool.wait_ge(s_pv, NS)
            pool.memset(a2.kst[:, :].bitcast(F), 0.0).then_inc(s_zero, 1)
            for b in range(B):
                pool.wait_ge(s_g["low"], b + 1)
                for j in range(4):
                    pool.wait_ge(s_g["mb"], 4 * b + j + 1)
                    pool.tensor_tensor(xml[b][:, 512 * j:512 * j + 512].rearrange("p (e t) -> p e t", e=2),
                                       mkB[:, 512 * (j % 2):512 * (j % 2) + 512].rearrange("p (e t) -> p e t", e=2),
                                       h2l[:, S * b:S * b + S].unsqueeze(1).to_broadcast([P, 2, S]),
                                       ALU.mult).then_inc(s_g["xml"], 1)

        ROUNDS = [(b, kind) for b in range(B) for kind in range(3)]

        def q_transposes(pe, a, b, bk, s_done):
            for g in range(4):
                for i in range(2):
                    pe.transpose(ps[:, bk + g // 2, 256 * (g % 2) + P * i:256 * (g % 2) + P * i + P],
                                 a.qs[:, (2 * b + i) * 512 + P * g:(2 * b + i) * 512 + P * g + P],
                                 ident[:, :]).then_inc(s_done, 1)

        def pe_stacks(pe, a, b, bq, bk):
            kg = a.kg
            if b == 0:
                pe.wait_ge(s_zero, 2 if a is a1 else 5)
            pe.wait_ge(a.s_qsplit, b + 1)
            q_transposes(pe, a, b, bq, a.s_T)
            pe.wait_ge(a.s_ksplit, b + 1)
            for g in range(kg):
                for i in range(2):
                    pe.transpose(ps[:, bk + g // 2, 256 * (g % 2) + P * i:256 * (g % 2) + P * i + P],
                                 a.ks[:, ((2 * b + i) * kg + g) * P:((2 * b + i) * kg + g + 1) * P],
                                 ident[:, :]).then_inc(a.s_T, 1)

        def free_scoresT(a, r, hf):
            if r % 3 == 0 and (r == 0 or a is a2):
                return a.s_max, (11 if a is a1 else 5 + 2 * r) + hf
            return a.s_E, 2 * (r - 1) + hf + 1

        def pe_scores(pe, a, r):
            b, kind = ROUNDS[r]
            if r % 3 == 0:
                pe.wait_ge(a.s_q_ev, b + 1)
                pe.wait_ge(a.s_k_ev, b + 1)
            tok = 256 * b
            n = 4 if kind == 0 else 2
            w = 512 // n
            for hf in range(2):
                if r > 0:
                    pe.wait_ge(a.s_max, 2 * (r - 1) + hf + 1)
                quads = (2 * hf, 2 * hf + 1)
                for j in quads:
                    pe.matmul(ps[:, j, :].rearrange("p (n w) -> p n w", n=n)[:, :, w - P:w], idR,
                              up.unsqueeze(1).to_broadcast([P, n, P]), start=True, stop=False,
                              skip_group_check=True)
                for m in range(n):
                    g = m if kind == 0 else 2 * (kind - 1) + m
                    q0 = 512 * g + tok + (0 if kind == 0 else P)
                    k0 = 512 * g + tok
                    for j in quads:
                        s = slice(32 * j, 32 * j + 32)
                        last = pe.matmul(ps[:, j, w * m:w * m + w], a.qst[s, q0:q0 + P], a.kst[s, k0:k0 + w],
                                         start=False, stop=True, skip_group_check=True)
                last.then_inc(a.s_S, 1)

        def pe_maxrows(pe, a, b, bk):
            pe.wait_ge(a.s_nm, b + 1)
            q_transposes(pe, a, b, bk, a.s_q2T)

        def pe_scoresT(pe, a, r):
            b, kind = ROUNDS[r]
            if kind == 0:
                pe.wait_ge(a.s_q2a, b + 1)
                pe.wait_ge(a.s_q2d, b + 1)
            tok = 256 * b
            n = 4 if kind == 0 else 2
            w = 512 // n
            q1 = tok + (P if kind == 0 else 0)
            for hf in range(2):
                pe.wait_ge(*free_scoresT(a, r, hf))
                quads = (2 * hf, 2 * hf + 1)
                for j in quads:
                    pe.matmul(ps[:, j, :].rearrange("p (n w) -> p n w", n=n)[:, :, 0:P], idR,
                              low.unsqueeze(1).to_broadcast([P, n, P]), start=True, stop=False,
                              skip_group_check=True)
                for m in range(n):
                    g = m if kind == 0 else 2 * (kind - 1) + m
                    k0 = 512 * g + tok + (P if kind == 0 else 0)
                    q0 = 512 * g + q1
                    for j in quads:
                        s = slice(32 * j, 32 * j + 32)
                        last = pe.matmul(ps[:, j, w * m:w * m + w], a.kst[s, k0:k0 + P], a.qst[s, q0:q0 + w],
                                         start=False, stop=True, skip_group_check=True)
                last.then_inc(a.s_ST, 1)

        def pe_scores_shared(pe, a, r):
            b, kind = ROUNDS[r]
            if kind == 0:
                pe.wait_ge(a.s_q_ev, b + 1)
                pe.wait_ge(a.s_k_ev, 4 * b + 4)
            n = 4 if kind == 0 else 2
            w = 512 // n
            kk = a.kst[:, 1024 * b:1024 * b + 1024].rearrange("p (j t) -> p j t", j=4)
            for hf in range(2):
                if r == 3:
                    pe.wait_ge(a.s_E, 5 + hf)
                elif r > 0:
                    pe.wait_ge(a.s_max, 2 * (r - 1) + hf + 1)
                for m in range(2):
                    bk = 2 * hf + m
                    g = bk if kind == 0 else 2 * (kind - 1) + hf
                    q0 = 512 * g + 256 * b + (0 if kind == 0 else P)
                    j0 = 0 if kind == 0 else 2 * m
                    pe.matmul(ps[:, bk, :].rearrange("p (n w) -> p n w", n=n)[:, :, w - P:w], idR,
                              up.unsqueeze(1).to_broadcast([P, n, P]), start=True, stop=False,
                              skip_group_check=True)
                    last = pe.matmul(ps[:, bk, :].rearrange("p (n w) -> p n w", n=n), a.qst[:, q0:q0 + P],
                                     kk[:, j0:j0 + n, 0:w], start=False, stop=True, skip_group_check=True)
                last.then_inc(a.s_S, 1)

        def pe_scoresT_shared(pe, a, r):
            b, kind = ROUNDS[r]
            if kind == 0:
                pe.wait_ge(a.s_q2a, b + 1)
                pe.wait_ge(a.s_q2d, b + 1)
            n = 4 if kind == 0 else 2
            w = 512 // n
            g0 = 0 if kind == 0 else 2 * (kind - 1)
            t0 = P if kind == 0 else 0
            qq = a.qst[:, :].rearrange("p (g t) -> p g t", g=4)
            for hf in range(2):
                pe.wait_ge(*free_scoresT(a, r, hf))
                for j in (2 * hf, 2 * hf + 1):
                    k0 = 1024 * b + 256 * j + t0
                    out = ps[:, j, :].rearrange("p (n w) -> p n w", n=n)
                    pe.matmul(out[:, :, 0:P], idR, low.unsqueeze(1).to_broadcast([P, n, P]),
                              start=True, stop=False, skip_group_check=True)
                    last = pe.matmul(out, a.kst[:, k0:k0 + P],
                                     qq[:, g0:g0 + n, 256 * b + t0:256 * b + t0 + w],
                                     start=False, stop=True, skip_group_check=True)
                last.then_inc(a.s_ST, 1)

        def pe_values(pe, a, b, half):
            pe.wait_ge(a.s_E, 2 * (3 * b + 2 + half))
            if half == 0:
                pe.wait_ge(a.s_vp, b + 1 if a is a2 else 1)
                if b > 0:
                    pe.wait_ge(a.s_O, 2 * b)
            short = a.pt[(3 * b) % 3]
            long = a.pt[(3 * b + 1 + half) % 3]
            for m in range(2):
                g = 2 * half + m
                for t, (buf, c0, w) in enumerate(((long, 256 * m, 256), (short, P * g, P))):
                    for j in range(4):
                        head = (4 * g + j) if a.kg > 1 else j
                        v0 = ((2 * b + t) * a.vh + head) * 32
                        last = pe.matmul(ps[32 * j:32 * j + 32, 4 + half, 256 * m + 256 - w:256 * m + 256],
                                         a.vp[:, v0:v0 + 32], buf[:, 512 * j + c0:512 * j + c0 + w],
                                         start=(t == 0), stop=(t == 1), skip_group_check=True)
            last.then_inc(a.s_PV, 1)

        def pe_untranspose(pe, a, b):
            pe.wait_ge(a.s_ots, 2 * b + 2)
            for i in range(2):
                for g in range(4):
                    c = 512 * (g // 2) + 256 * (g % 2) + P * i
                    last = pe.transpose(ps[:, 4 + i, P * g:P * g + P], a.ots[:, c:c + P], ident[:, :])
                last.then_inc(a.s_OT, 1)

        def act_maxrows(act, a, b, bk):
            act.wait_ge(a.s_q2T, 8 * (b + 1))
            act.wait_ge(a.s_S, 6 * (b + 1))
            nc.scalar.activation(a.qst[:, :].rearrange("p (g t) -> p g t", g=4)[:, 0:2, 256 * b:256 * b + 256],
                                 ps[:, bk, :].rearrange("p (g t) -> p g t", g=2), ACT.Copy).then_inc(a.s_q2a, 1)

        def dve_maxrows(dve, a, b, bk):
            dve.wait_ge(a.s_q2T, 8 * (b + 1))
            dve.tensor_copy(a.qst[:, :].rearrange("p (g t) -> p g t", g=4)[:, 2:4, 256 * b:256 * b + 256],
                            ps[:, bk + 1, :].rearrange("p (g t) -> p g t", g=2)).then_inc(a.s_q2d, 1)

        def act_exp(act, a, r):
            if r == 0 and a is a1:
                act.wait_ge(a.s_q2T, 16)
                act.wait_ge(a.s_T, 16 + 4 * a.kg)
            if r == 3:
                act.wait_ge(a.s_PV, 2)
            for hf in range(2):
                act.wait_ge(a.s_ST, 2 * r + hf + 1)
                nc.scalar.activation(a.pt[r % 3][:, 1024 * hf:1024 * hf + 1024],
                                     ps[:, 2 * hf:2 * hf + 2, :].rearrange("p a b -> p (a b)"),
                                     ACT.Exp).then_inc(a.s_E, 1)

        def dve_max(dve, a, r, v, need):
            b, kind = ROUNDS[r]
            t = 2 * b + (0 if kind == 0 else 1)
            nmf = st[:, 128:192].rearrange("p (t g j) -> p t g j", t=NT, g=4)
            for hf in range(2):
                dve.wait_ge(a.s_S, 2 * r + hf + 1)
                jj = slice(2 * hf, 2 * hf + 2)
                if a is a2:
                    src = ps[:, jj, :].rearrange("p j (g w) -> p (j g) w", g=4 if kind == 0 else 2)
                    g0 = 2 * hf if kind == 0 else 2 * (kind - 1) + hf
                    dst = st[:, 128 + 16 * t + 4 * g0:128 + 16 * t + 4 * g0 + (8 if kind == 0 else 4)]
                elif kind == 0:
                    src = ps[:, jj, :].rearrange("p j (g w) -> p j g w", g=4)
                    dst = nmf[:, t, :, jj].rearrange("p g j -> p j g")
                else:
                    src = ps[:, jj, :].rearrange("p j (g w) -> p j g w", g=2)
                    dst = nmf[:, t, 2 * (kind - 1):2 * kind, jj].rearrange("p g j -> p j g")
                dve.tensor_reduce(dst, src, X, ALU.max, negate=True).then_inc(a.s_max, 1)
            if kind == 2:
                dve.wait_ge(a.s_max, 2 * r + 2)
                dve.wait_ge(a.s_T, (8 + 2 * a.kg) * (b + 1))
                src = st[:, 128:192].rearrange("p (t c) -> p t c", t=NT)[:, 2 * b:2 * b + 2, :]
                dst = a.qs[:, :].rearrange("p (t n r d) -> p t n r d", t=NT, n=16, r=4)[:, 2 * b:2 * b + 2, :, 3, :]
                n = v(dve.tensor_copy(dst[:, :, :, 0].bitcast(R), src))
                need(n)
                dve.tensor_tensor(dst[:, :, :, 1], src, dst[:, :, :, 0], ALU.subtract).then_inc(a.s_nm, 1)

        def dve_norm(dve, a, b, v, need):
            for i in range(2):
                t = 2 * b + i
                dve.wait_ge(a.s_OT, t + 1)
                src = ps[:, 4 + i, :].rearrange("p (h c) -> p h c", c=32)
                n = v(dve.reciprocal(st[:, 192 + 16 * t:208 + 16 * t], src[:, :, HD]))
                need(n)
                dve.tensor_tensor(a.otok[:, P * t:P * t + P].rearrange("p (h c) -> p h c", c=HD),
                                  src[:, :, 0:HD],
                                  st[:, 192 + 16 * t:208 + 16 * t].unsqueeze(2).to_broadcast([P, 16, HD]),
                                  ALU.mult).then_inc(a.s_O, 1)

        @block.tensor
        def _(pe):
            def three(out, xh, xl, wh, wl, start=True):
                pe.matmul(out, xh, wh, start=start, stop=False)
                pe.matmul(out, xh, wl, start=False, stop=False)
                return pe.matmul(out, xl, wh, start=False, stop=True)

            pe.wait_ge(s_ldA, 16)
            for t in range(NT):
                pe.matmul(bank(4 + t, 0, 384), wA[:, A_XT + P * t:A_XT + P * t + P], wA[:, A_W1:A_W1 + 384],
                          start=True, stop=True).then_inc(s_qkv, 1)

            def ctx_transposes(b):
                pe.wait_ge(s_cln, 4 * (b + 1))
                for i in range(4):
                    t = 4 * b + i
                    last = pe.transpose(bank(b, P * i, P * i + P), cx[:, P * t:P * t + P], ident[:, :])
                last.then_inc(s_cT, 1)

            pe.wait_ge(s_const, 1)
            ctx_transposes(0)
            ctx_transposes(1)
            pe.wait_ge(s_cTl, 2)
            pe.wait_ge(s_h, 4)
            pe_stacks(pe, a1, 0, 0, 2)
            pe_stacks(pe, a1, 1, 4, 6)
            pe.wait_ge(s_constR, 2)

            def v_chunk(n):
                t, half = n // 2, n % 2
                if n == 0:
                    pe.wait_ge(s_vlo, 1)
                    pe.wait_ge(a1.s_q_ev, 2)
                    pe.wait_ge(a1.s_k_ev, 2)
                if n >= 4:
                    pe.wait_ge(s_vev, n - 3)
                c = slice(1024 + 512 * half, 1536 + 512 * half)
                tt = slice(P * t, P * t + P)
                three(bank(4 + n % 4), cTh[:, tt], cTl[:, tt], wkvh[:, c], wkvl[:, c]).then_inc(s_vch, 1)

            vn = 0
            for r in range(6):
                pe_scores(pe, a1, r)
                for _ in range(3 if r < 4 else 2):
                    v_chunk(vn)
                    vn += 1
            pe.wait_ge(s_vev, 16)
            pe_maxrows(pe, a1, 0, 4)
            pe_maxrows(pe, a1, 1, 6)

            def k_chunk(n):
                c, b = n // 2, n % 2
                if n == 0:
                    pe.wait_ge(s_klo, 1)
                    pe.wait_ge(a1.s_q2a, 2)
                    pe.wait_ge(a1.s_q2d, 2)
                if n >= 2:
                    pe.wait_ge(s_kdn, n - 1)
                cc = slice(P * c, P * c + P)
                tt = slice(SC * b, SC * b + SC)
                three(bank(6 + n % 2), wkvh[:, cc], wkvl[:, cc], cTh[:, tt], cTl[:, tt]).then_inc(s_kch, 1)

            kn = 0

            def k_chunks(m):
                nonlocal kn
                for _ in range(m):
                    k_chunk(kn)
                    kn += 1

            pe_scoresT(pe, a1, 0)
            k_chunks(2)
            pe_scoresT(pe, a1, 1)
            k_chunks(2)
            pe_scoresT(pe, a1, 2)
            pe_values(pe, a1, 0, 0)
            k_chunks(2)
            pe_scoresT(pe, a1, 3)
            pe_values(pe, a1, 0, 1)
            k_chunks(2)
            pe_scoresT(pe, a1, 4)
            pe_untranspose(pe, a1, 0)
            k_chunks(3)
            pe_scoresT(pe, a1, 5)
            pe_values(pe, a1, 1, 0)
            k_chunks(3)
            pe_values(pe, a1, 1, 1)
            k_chunks(1)
            pe_untranspose(pe, a1, 1)
            k_chunks(1)

            for t in range(NT):
                pe.wait_ge(a1.s_O, t + 1)
                last = pe.transpose(bank(0, P * t, P * t + P), a1.otok[:, P * t:P * t + P], ident[:, :])
            last.then_inc(s_OtT, 1)
            pe.wait_ge(s_ott, 1)
            for t in range(NT):
                last = pe.matmul(bank(1, P * t, P * t + P), a1.ott[:, P * t:P * t + P], wA[:, A_WP:A_WP + P],
                                 start=(t == 0), stop=True, skip_group_check=True)
            last.then_inc(s_pj, 1)

            pe.wait_ge(s_xn, 2 * NT)
            for t in range(NT):
                last = pe.transpose(bank(0, P * t, P * t + P), ln[:, P * t:P * t + P], ident[:, :])
            last.then_inc(s_lnT, 1)
            pe.wait_ge(s_lnTs, 2)
            pe.wait_ge(s_ldq, 16)
            pe.wait_ge(s_kdn, 16)
            for n, (kind, c) in enumerate(LCH):
                if n >= 8:
                    kinds = [k for k, _ in LCH[:n - 7]]
                    pe.wait_ge(s_llo, sum(k != "v" for k in kinds))
                    if "v" in kinds:
                        pe.wait_ge(s_lhi, n - 7)
                bk = n % 8
                if kind == "q":
                    pe.matmul(bank(bk, 0, S), xq_w[:, P * c:P * c + P], lnT[:, 0:S],
                              start=True, stop=True).then_inc(s_lch, 1)
                elif kind == "k":
                    cc = slice(P * c, P * c + P)
                    three(bank(bk), wkvh[:, cc], wkvl[:, cc], lnTh[:, :], lnTl[:, :]).then_inc(s_lch, 1)
                else:
                    t, half = c // 2, c % 2
                    w = slice(1024 + 512 * half, 1536 + 512 * half)
                    tt = slice(P * t, P * t + P)
                    three(bank(bk), lnTh[:, tt], lnTl[:, tt], wkvh[:, w], wkvl[:, w]).then_inc(s_lch, 1)

            g = s_g

            def f_x2T(b, bk):
                pe.wait_ge(s_xn, 2 * NT + 2 * (b + 1))
                for i in range(2):
                    t = 2 * b + i
                    last = pe.transpose(bank(bk, P * i, P * i + P), xs[:, P * t:P * t + P], ident[:, :])
                last.then_inc(g["x2T"], 1)

            def f_qkv(b, bk):
                pe.wait_ge(g["x2Tsb"], b + 1)
                pe.wait_ge(s_ldg, 16)
                for i in range(2):
                    t = 2 * b + i
                    last = pe.matmul(bank(bk, 192 * i, 192 * i + 192), x2T[:, P * t:P * t + P],
                                     wG[:, G_QKV:G_QKV + 192], start=(i == 0), stop=True, skip_group_check=True)
                last.then_inc(g["qkv"], 1)

            bank7_read = ()

            def x_scores(s):
                b, c, i = STEPS[s]
                if s == 0:
                    pe.wait_ge(s_lhi, len(LCH))
                    pe.wait_ge(s_llo, 2 * NP)
                if b == 1 and i == 0:
                    pe.wait_ge(s_q1l, c + 1)
                if s > 0:
                    pe.wait_ge(s_ex, 2 * s)
                q = slice(S * c + P * i, S * c + P * i + P)
                kc = slice((b * NP + c) * SC, (b * NP + c + 1) * SC)
                kl = slice((b * NP + c) * S, (b * NP + c + 1) * S)
                for n, (qq, kk, ll) in enumerate(((qh, kch, klh), (qh, kcl, kll), (ql, kch, klh))):
                    for hh in range(2):
                        rows = slice(64 * hh, 64 * hh + 64)
                        pe.matmul(bank(2 * hh), qq[rows, q], kk[rows, kc], start=(n == 0), stop=(n == 2))
                    for hh in range(2):
                        rows = slice(64 * hh, 64 * hh + 64)
                        last = pe.matmul(bank(2 * hh + 1, 0, S), qq[rows, q], ll[rows, kl],
                                         start=(n == 0), stop=(n == 2))
                        if n == 2:
                            last.then_inc(s_S, 1)
                    if n == 0:
                        x_slot(s)

            def x_transposes(s):
                for u in range(2):
                    pe.wait_ge(s_ex, 2 * s + u + 1)
                    slot = (2 * s + u) % 4
                    for kt in range(KT):
                        n = KT * u + kt
                        if n % 4 == 0 and s > 0:
                            if n // 4 == 1:
                                pe.wait_ge(s_cpA, s)
                            else:
                                pe.wait_ge(s_cpD, 2 * (s - 1) + (1 if n == 0 else 2))
                        last = pe.transpose(bank(4 + n // 4, P * (n % 4), P * (n % 4) + P),
                                            pr[:, (slot * KT + kt) * P:(slot * KT + kt + 1) * P], ident[:, :])
                        if n % 4 == 3:
                            last.then_inc(s_tr, 1)

            def x_values(s):
                b, c, i = STEPS[s]
                pe.wait_ge(s_cpA, s + 1)
                pe.wait_ge(s_cpD, 2 * s + 2)
                if s > 0:
                    pe.wait_ge(s_oev, s)
                if bank7_read:
                    pe.wait_ge(*bank7_read)
                buf = (s % 2) * 12 * P
                for kt in range(KT):
                    for hh in range(2):
                        if kt < CT:
                            v0 = (b * CT + kt) * 1024 + P * c + 64 * hh
                            v = vc[:, v0:v0 + 64]
                        else:
                            v0 = (b * 2 + kt - CT) * 1024 + P * c + 64 * hh
                            v = vl[:, v0:v0 + 64]
                        p0 = buf + (KT * hh + kt) * P
                        last = pe.matmul(ps[64 * hh:64 * hh + 64, 7, 0:P], v, pT[:, p0:p0 + P],
                                         start=(kt == 0), stop=(kt == KT - 1))
                last.then_inc(s_pv, 1)

            def x_recip_rows(b, n, bk):
                pe.wait_ge(s_rc, 4 * b + n + 1)
                for i in range(2):
                    k = 32 * b + 16 * i + 4 * n
                    last = pe.transpose(ps[0:4, bk, P * i:P * i + P], rc[:, k:k + 4], ident[:, :])
                last.then_inc(s_rcT, 1)

            def x_recip_spread(b, n, bk):
                pe.wait_ge(s_rcS, 4 * b + n + 1)
                for m in range(2):
                    for hh in range(2):
                        last = pe.matmul(ps[64 * hh:64 * hh + 64, bk, 256 * m:256 * m + 256],
                                         ident[0:4, 2 * m + hh:2 * m + hh + 1].to_broadcast([4, 64]),
                                         recT[0:4, :], start=(m == 0), stop=True, skip_group_check=True)
                last.then_inc(s_R, 1)

            def x_slot(s):
                nonlocal bank7_read
                if s not in SLOT:
                    return
                if s > 2:
                    pe.wait_ge(s_oev, s - 2)
                if bank7_read:
                    pe.wait_ge(*bank7_read)
                what = SLOT[s]
                if what[0] == "q":
                    c = what[1]
                    pe.matmul(bank(7, 0, S), xq_w[:, P * c:P * c + P], lnT[:, S:2 * S],
                              start=True, stop=True).then_inc(s_q1, 1)
                    bank7_read = (s_q1l, c + 1)
                elif what[0] == "rc":
                    x_recip_rows(what[1], what[2], 7)
                    bank7_read = (s_rcS, 4 * what[1] + what[2] + 1)
                elif what[0] == "R":
                    x_recip_spread(what[1], what[2], 7)
                    bank7_read = (s_on, 4 * what[1] + what[2] + 1)
                elif what[0] == "x2T":
                    f_x2T(0, 7)
                    bank7_read = (g["x2Tsb"], 1)
                else:
                    f_qkv(0, 7)
                    bank7_read = (g["h"], 2)

            def x_output(b, bk):
                pe.wait_ge(s_on, 4 * (b + 1))
                pe.wait_ge(s_ldo, 16)
                for i in range(2):
                    for c in range(NP):
                        last = pe.matmul(bank(bk, P * i, P * i + P), ot[:, S * c + P * i:S * c + P * i + P],
                                         xout_w[:, D * c:D * c + D], start=(c == 0 and i == 0),
                                         stop=(c == NP - 1), skip_group_check=True)
                last.then_inc(s_xo, 1)

            for s in range(NS):
                x_scores(s)
                if s > 0:
                    x_transposes(s - 1)
                if s == 18:
                    x_output(0, 7)
                    bank7_read = (s_xadd, 1)
                if s > 1:
                    x_values(s - 2)
            x_transposes(NS - 1)
            x_recip_rows(1, 3, 0)
            x_values(NS - 2)
            x_recip_spread(1, 3, 1)
            x_values(NS - 1)

            def f_T(b, src, bk, s_done):
                for i in range(2):
                    t = 2 * b + i
                    last = pe.transpose(bank(bk, P * i, P * i + P), src[:, P * t:P * t + P], ident[:, :])
                last.then_inc(s_done, 1)

            def f_mm(b, lhs, w, n, bk, s_done):
                for i in range(2):
                    t = 2 * b + i
                    last = pe.matmul(bank(bk, n * i, n * i + n), lhs[:, P * t:P * t + P], w,
                                     start=(i == 0), stop=True, skip_group_check=True)
                last.then_inc(s_done, 1)

            def f_OtT(b):
                pe.wait_ge(a2.s_O, 2 * b + 2)
                if b == 0:
                    pe.wait_ge(g["x2Tsb"], 2)
                else:
                    pe.wait_ge(g["mkTs"], 2)
                f_T(b, a2.otok, 6, g["OtT"])

            def f_gate(b):
                pe.wait_ge(g["ott"], b + 1)
                if b == 0:
                    pe.wait_ge(g["h"], 4)
                else:
                    pe.wait_ge(g["lgr"], 1)
                f_mm(b, a2.ott, wG[:, G_WG:G_WG + P], P, 7, g["gl"])

            def f_gT(b):
                pe.wait_ge(g["gated"], b + 1)
                f_T(b, a2.otok, 6, g["gT"])

            def f_wo(b):
                pe.wait_ge(g["gTs"], b + 1)
                f_mm(b, fT, wG[:, G_WO:G_WO + P], P, 7, g["wo"])

            def f_h2T(b):
                pe.wait_ge(g["h2"], 2 * b + 2)
                f_T(b, h2, 6, g["h2T"])

            def f_logits(b):
                pe.wait_ge(g["h2Ts"], b + 1)
                f_mm(b, h2T, wG[:, G_WR:G_WR + NE], NE, 7, g["lg"])

            def f_mkT(b):
                pe.wait_ge(g["mk"], b + 1)
                for i in range(2):
                    t = 2 * b + i
                    last = pe.transpose(ps[0:NE, 6, P * i:P * i + P], mk[:, NE * t:NE * t + NE], ident[:, :])
                last.then_inc(g["mkT"], 1)

            def f_spread(b, j):
                bk = (2 if b == 0 else 6) + j % 2
                if j == 0:
                    pe.wait_ge(g["mkTs"], 2 * b + 2)
                    if b == 0:
                        pe.wait_ge(a2.s_E, 12)
                    else:
                        pe.wait_ge(g["lgr"], 2)
                if j >= 2:
                    pe.wait_ge(g["mb"], 4 * b + j - 1)
                for ee in range(2):
                    e = 2 * j + ee
                    last = pe.matmul(bank(bk, S * ee, S * ee + S), idR[0:NE, e:e + 1].to_broadcast([NE, P]),
                                     mkR[0:NE, S * b:S * b + S], start=(ee == 0), stop=True,
                                     skip_group_check=True)
                last.then_inc(g["bc"], 1)

            def experts_u(e, t):
                b, i = t // 2, t % 2
                pe.wait_ge(g["xm"], 4 * b + e // 2 + 1)
                pe.wait_ge(g["xml"], 4 * b + e // 2 + 1)
                if e == 0 and b == 1:
                    pe.wait_ge(g["acTl"], 2)
                xx = slice(S * e + P * i, S * e + P * i + P)
                ww = slice(512 * e, 512 * e + 512)
                pe.matmul(bank(t), xmh[b][:, xx], w1h[:, ww], start=(e == 0), stop=False)
                pe.matmul(bank(t), xmh[b][:, xx], w1l[:, ww], start=False, stop=False)
                pe.matmul(bank(t), xml[b][:, xx], w1h[:, ww], start=False, stop=False)

            def bias_u(t):
                pe.wait_ge(g["be"], 2)
                tt = slice(P * t, P * t + P)
                pe.matmul(bank(t), mkR[0:NE, tt], beh[0:NE, :], start=False, stop=False)
                pe.matmul(bank(t), mkR[0:NE, tt], bel[0:NE, :], start=False, stop=True).then_inc(g["u"], 1)

            def f_b2(b):
                if b == 0:
                    pe.wait_ge(a2.s_O, 4)
                else:
                    pe.wait_ge(g["yr"], 2)
                f_mm(b, mkT[0:NE, :], wbe[0:NE, 512:640], P, 5, g["b2"])

            def act_T(t):
                pe.wait_ge(g["act"], t + 1)
                bk = (2 if t < 2 else 6) + t % 2
                if t >= 2:
                    pe.wait_ge(g["mb"], 8)
                for k in range(2):
                    last = pe.transpose(bank(bk, P * k, P * k + P),
                                        actf[:, HID * t + P * k:HID * t + P * k + P], ident[:, :])
                last.then_inc(g["actT"], 1)

            def experts_y(t, halves=(0, 1)):
                pe.wait_ge(g["acTl"], t + 1)
                if t % 2 == 0:
                    pe.wait_ge(g["b2r"], t // 2 + 1)
                if t == 1:
                    pe.wait_ge(g["act"], 2)
                if t >= 2:
                    pe.wait_ge(g["yr"], 2 * (t - 1))
                for half in halves:
                    n = 0
                    for k in range(2):
                        a0 = slice(HID * t + P * k, HID * t + P * k + P)
                        w0 = slice(1024 * k + 512 * half, 1024 * k + 512 * half + 512)
                        for aa, ww in ((acTh, w2h), (acTh, w2l), (acTl, w2h)):
                            last = pe.matmul(bank(4 - 4 * (t % 2) + half), aa[:, a0], ww[:, w0],
                                             start=(n == 0), stop=(n == 5))
                            n += 1
                    last.then_inc(g["y"], 1)

            pe_stacks(pe, a2, 0, 4, 6)
            x_output(1, 7)
            pe_scores_shared(pe, a2, 0)
            pe_scores_shared(pe, a2, 1)
            pe.wait_ge(a2.s_k_ev, 4)
            f_x2T(1, 6)
            pe_scores_shared(pe, a2, 2)
            pe.wait_ge(s_xadd, 2)
            f_qkv(1, 7)
            pe_maxrows(pe, a2, 0, 4)
            pe_scoresT_shared(pe, a2, 0)
            pe_scoresT_shared(pe, a2, 1)
            pe_scoresT_shared(pe, a2, 2)
            pe_values(pe, a2, 0, 0)
            pe_values(pe, a2, 0, 1)
            pe.wait_ge(a2.s_E, 6)
            pe_stacks(pe, a2, 1, 0, 2)
            pe_untranspose(pe, a2, 0)
            pe_scores_shared(pe, a2, 3)
            f_OtT(0)
            pe_scores_shared(pe, a2, 4)
            f_gate(0)
            pe_scores_shared(pe, a2, 5)
            pe.wait_ge(a2.s_O, 2)
            pe_maxrows(pe, a2, 1, 4)
            pe_scoresT_shared(pe, a2, 3)
            f_gT(0)
            pe_scoresT_shared(pe, a2, 4)
            f_wo(0)
            pe_scoresT_shared(pe, a2, 5)
            f_h2T(0)
            pe_values(pe, a2, 1, 0)
            f_logits(0)
            pe_values(pe, a2, 1, 1)
            f_mkT(0)
            pe_untranspose(pe, a2, 1)
            f_spread(0, 0)
            f_spread(0, 1)
            for e in range(2):
                experts_u(e, 0)
                experts_u(e, 1)
            f_spread(0, 2)
            f_OtT(1)
            for e in range(2, 4):
                experts_u(e, 0)
                experts_u(e, 1)
            f_spread(0, 3)
            f_gate(1)
            for t in range(2):
                for e in range(4, NE):
                    experts_u(e, t)
                bias_u(t)
            f_gT(1)
            f_b2(0)
            f_wo(1)
            act_T(0)
            experts_y(0, (0,))
            f_h2T(1)
            experts_y(0, (1,))
            f_logits(1)
            act_T(1)
            f_mkT(1)
            experts_y(1, (0,))
            for j in range(2):
                f_spread(1, j)
            experts_y(1, (1,))
            for j in range(4):
                for e in range(2 * j, 2 * j + 2):
                    experts_u(e, 2)
                if j < 2:
                    f_spread(1, j + 2)
            bias_u(2)
            f_b2(1)
            for e in range(NE):
                experts_u(e, 3)
                if e == 5:
                    act_T(2)
            bias_u(3)
            experts_y(2)
            act_T(3)
            experts_y(3)

        @block.scalar
        def _(act):
            A = nc.scalar
            n_ac = [0]

            def link(ins):
                n_ac[0] += 1
                ins.then_inc(s_ac, 1)
                act.wait_ge(s_ac, n_ac[0])

            act.dma_start(cols[:, :], d_cols).then_inc(s_ldc, 16)
            act.dma_start(wkv[:, 0:1024], d_wkv[:, 0:1024]).then_inc(s_ldk, 16)
            act.dma_start(xs[:, :], d_x).then_inc(s_ldx, 16)
            A.preload_act_table_set("natural_log_exp_and_others")

            def rstd(out, var, scale, eps):
                link(A.activation(out, var, ACT.Ln, bias=eps, scale=scale))
                return A.activation(out, out, ACT.Exp, scale=-0.5)

            mv = st[:, 0:32].rearrange("p (t c) -> p t c", c=2)
            e5 = cols[:, C_E5:C_E5 + 1]
            e6 = cols[:, C_E6:C_E6 + 1]
            act.wait_ge(s_ldc, 32)
            for b in range(B):
                act.wait_ge(s_cst, b + 1)
                rstd(st[:, 32 + 4 * b:36 + 4 * b], mv[:, 4 * b:4 * b + 4, 1], 1.0, e5).then_inc(s_crs, 1)
            act.wait_ge(s_ldv, 16)
            A.activation(wkvh[:, 1024:2048], wkv[:, 1024:2048], ACT.Copy).then_inc(s_vhi, 1)

            hv = a1.h[:, :].rearrange("p (n c d) -> p n c d", c=3, d=HD)
            qs = a1.qs[:, :].rearrange("p (n r d) -> p n r d", r=4, d=HD)
            ks = a1.ks[:, :].rearrange("p (n r d) -> p n r d", r=4, d=HD)
            for b in range(B):
                act.wait_ge(s_h, 2 * b + 2)
                m = slice(32 * b, 32 * b + 32)
                A.activation(qs[:, m, 0, :].bitcast(R), hv[:, m, 0, :], ACT.Copy,
                             scale=HD ** -0.5).then_inc(s_kev, 1)
                A.activation(ks[:, m, 0, :].bitcast(R), hv[:, m, 1, :], ACT.Copy).then_inc(s_kev, 1)
            for b in range(B):
                act.wait_ge(s_cT, b + 1)
                A.activation(cTh[:, SC * b:SC * b + SC], bank(b), ACT.Identity, bias=cols[:, C_B1:C_B1 + 1],
                             scale=cols[:, C_G1:C_G1 + 1]).then_inc(s_cTh, 1)
            act.wait_ge(s_ldk, 16)
            A.activation(wkvh[:, 0:1024], wkv[:, 0:1024], ACT.Copy).then_inc(s_khi, 1)
            for b in range(B):
                act.wait_ge(a1.s_T, 16 * b + 8)
                A.activation(a1.qst[:, :].rearrange("p (g t) -> p g t", g=4)[:, :, 256 * b:256 * b + 256],
                             ps[:, 4 * b:4 * b + 2, :].rearrange("p a (g t) -> p (a g) t", g=2),
                             ACT.Copy).then_inc(a1.s_q_ev, 1)
            act.wait_ge(s_zero, 3)
            A.activation(a1.vp[:, :].rearrange("p (n c) -> p n c", c=32)[:, :, 0:HD], hv[:, :, 2, :],
                         ACT.Copy).then_inc(a1.s_vp, 1)
            for n in range(16):
                t, half = n // 2, n % 2
                act.wait_ge(s_vch, n + 1)
                A.activation(vc[:, 1024 * t + 512 * half:1024 * t + 512 * half + 512], bank(4 + n % 4),
                             ACT.Copy).then_inc(s_vev, 1)
            act_maxrows(act, a1, 0, 4)
            act_maxrows(act, a1, 1, 6)

            kn = 0

            def k_hi(m):
                nonlocal kn
                for _ in range(m):
                    c, b = kn // 2, kn % 2
                    act.wait_ge(s_kch, kn + 1)
                    A.activation(kch[:, (b * NP + c) * SC:(b * NP + c + 1) * SC], bank(6 + kn % 2),
                                 ACT.Copy).then_inc(s_khi, 1)
                    kn += 1

            act.wait_ge(s_vch, 16)
            for r, m in enumerate((2, 2, 2, 2, 3, 3)):
                if r == 2:
                    act.wait_ge(a1.s_vp, 1)
                act_exp(act, a1, r)
                k_hi(m)
            k_hi(2)

            act.wait_ge(s_OtT, 1)
            A.activation(a1.ott[:, :], bank(0), ACT.Copy).then_inc(s_ott, 1)

            def ln_rstd(k, t0=0, t1=NT):
                act.wait_ge(s_st, k + 1)
                rstd(st[:, 32 + t0:32 + t1], mv[:, t0:t1, 1], 1.0, e5).then_inc(s_rs, 1)

            ln_rstd(0)
            ln_rstd(1)
            act.wait_ge(s_lnT, 1)
            link(A.activation(lnT[:, :], bank(0), ACT.Identity, bias=cols[:, C_B2:C_B2 + 1],
                              scale=cols[:, C_G2:C_G2 + 1]))
            A.activation(lnTh[:, :], lnT[:, :], ACT.Copy).then_inc(s_lnTs, 1)
            for n, (kind, c) in enumerate(LCH):
                act.wait_ge(s_lch, n + 1)
                bk = n % 8
                if kind == "q":
                    if n == 0:
                        act.wait_ge(s_pj, 1)
                    A.activation(qh[:, S * c:S * c + S], bank(bk, 0, S), ACT.Copy, scale=XD ** -0.5).then_inc(s_lhi, 1)
                elif kind == "k":
                    A.activation(klh[:, :].rearrange("p (b c t) -> p b c t", b=B, c=NP)[:, :, c, :],
                                 bank(bk).rearrange("p (b t) -> p b t", b=B), ACT.Copy).then_inc(s_lhi, 1)
                else:
                    t, half = c // 2, c % 2
                    A.activation(vl[:, 1024 * t + 512 * half:1024 * t + 512 * half + 512], bank(bk),
                                 ACT.Copy).then_inc(s_lhi, 1)

            def x_exp(s):
                for u in range(2):
                    b, c, i = STEPS[s]
                    k = 32 * b + 16 * i + 2 * c + u
                    slot = (2 * s + u) % 4
                    act.wait_ge(s_mx, 2 * s + u + 1)
                    if s == 0 and u == 0:
                        act.wait_ge(s_lch, len(LCH))
                    if s >= 2:
                        act.wait_ge(s_tr, 3 * (s - 1))
                    A.activation(pr[:, slot * 768:slot * 768 + 768],
                                 ps[:, 2 * u:2 * u + 2, :].rearrange("p a b -> p (a b)")[:, 0:768],
                                 ACT.Exp, bias=negmax[:, (2 * s + u) % 8:(2 * s + u) % 8 + 1],
                                 accum_out=psums[:, k:k + 1]).then_inc(s_ex, 1)

            def x_copy(s):
                act.wait_ge(s_tr, 3 * s + 2)
                if s >= 2:
                    act.wait_ge(s_pv, s - 1)
                p0 = (s % 2) * 1536 + 512
                A.activation(pT[:, p0:p0 + 512], bank(5), ACT.Copy).then_inc(s_cpA, 1)

            def act_recip_rows(b, n, bk):
                act.wait_ge(s_rcT, 4 * b + n + 1)
                A.activation(recT[0:4, :], ps[0:4, bk, 0:256], ACT.Copy).then_inc(s_rcS, 1)

            def x_slot(s):
                what = SLOT.get(s, ("",))
                if what[0] == "q":
                    c = what[1]
                    act.wait_ge(s_S, 4 * c + 4)
                    act.wait_ge(s_q1, c + 1)
                    A.activation(qh[:, S * c:S * c + S], bank(7, 0, S), ACT.Copy,
                                 scale=XD ** -0.5).then_inc(s_q1h, 1)
                elif what[0] == "x2T":
                    f_x2T(0, 7)
                elif what[0] == "rc":
                    if 4 * what[1] + what[2] > 0:
                        act.wait_ge(s_R, 4 * what[1] + what[2])
                    act_recip_rows(what[1], what[2], 7)

            g = s_g

            def squares(b, x, scratch):
                for i in range(2):
                    t = 2 * b + i
                    last = A.activation(scratch[:, P * i:P * i + P], x[:, P * t:P * t + P], ACT.Square,
                                        accum_out=st[:, 36 + t:37 + t])
                link(last)

            def f_rms(b):
                act.wait_ge(s_xn, 2 * NT + 2 * b + 2)
                squares(b, xs, rq[:, 320 * b:320 * b + 256])
                rstd(st[:, 40 + 2 * b:42 + 2 * b], st[:, 36 + 2 * b:38 + 2 * b], 1.0 / D, e6).then_inc(g["rstd"], 1)

            def f_x2T(b, bk):
                act.wait_ge(g["x2T"], b + 1)
                act.wait_ge(s_w2l, 4)
                A.activation(x2T[:, S * b:S * b + S], bank(bk, 0, S), ACT.Copy,
                             scale=cols[:, C_L1:C_L1 + 1]).then_inc(g["x2Tsb"], 1)

            def f_head_rms(b):
                act.wait_ge(g["sq"], b + 1)
                rstd(rq[:, 320 * b:320 * b + 40], rq[:, 320 * b + 40:320 * b + 80], 1.0 / HD,
                     e6).then_inc(g["rms"], 1)

            hq = rp[:, :].rearrange("p (t n d) -> p t n d", t=NT, n=20)
            qs2 = a2.qs[:, :].rearrange("p (t n r d) -> p t n r d", t=NT, n=16, r=4)
            ks2 = a2.ks[:, :].rearrange("p (t n r d) -> p t n r d", t=NT, n=4, r=4)

            def f_hi(b):
                act.wait_ge(g["ss"], b + 1)
                m = slice(2 * b, 2 * b + 2)
                A.activation(qs2[:, m, :, 0, :].bitcast(R), hq[:, m, 0:16, :], ACT.Copy,
                             scale=HD ** -0.5).then_inc(g["hi"], 1)
                A.activation(ks2[:, m, :, 0, :].bitcast(R), hq[:, m, 16:20, :], ACT.Copy).then_inc(g["hi"], 1)
                act.wait_ge(s_zero, 6)
                A.activation(a2.vp[:, :].rearrange("p (t n c) -> p t n c", t=NT, c=32)[:, m, :, 0:HD],
                             a2.h[:, :].rearrange("p (t n d) -> p t n d", t=NT, d=HD)[:, m, 20:24, :],
                             ACT.Copy).then_inc(a2.s_vp, 1)

            def f_qst(b, bk):
                act.wait_ge(a2.s_T, 10 * b + 8)
                A.activation(a2.qst[:, :].rearrange("p (g t) -> p g t", g=4)[:, :, 256 * b:256 * b + 256],
                             ps[:, bk:bk + 2, :].rearrange("p a (g t) -> p (a g) t", g=2),
                             ACT.Copy).then_inc(a2.s_q_ev, 1)

            def f_copy(b, s_in, dst, bk, s_out, **kw):
                act.wait_ge(s_in, b + 1)
                return A.activation(dst[:, S * b:S * b + S], bank(bk, 0, S), ACT.Copy, **kw).then_inc(s_out, 1)

            def f_gate(b):
                act.wait_ge(g["gpre"], b + 1)
                A.activation(gat[:, S * b:S * b + S], gat[:, S * b:S * b + S], ACT.Exp,
                             scale=-1.0).then_inc(g["e"], 1)

            def f_rms3(b):
                act.wait_ge(g["x3"], b + 1)
                squares(b, x3, gat[:, S * b:S * b + S])
                rstd(st[:, 84 + 2 * b:86 + 2 * b], st[:, 36 + 2 * b:38 + 2 * b], 1.0 / D,
                     e6).then_inc(g["rstd3"], 1)

            def f_h2T(b):
                act.wait_ge(g["h2T"], b + 1)
                link(A.activation(h2T[:, S * b:S * b + S], bank(6, 0, S), ACT.Copy, scale=cols[:, C_L2:C_L2 + 1]))
                A.activation(h2h[:, S * b:S * b + S], h2T[:, S * b:S * b + S], ACT.Copy).then_inc(g["h2Ts"], 1)

            def f_mkT(b):
                act.wait_ge(g["mkT"], b + 1)
                A.activation(mkR[0:NE, S * b:S * b + S], ps[0:NE, 6, 0:S], ACT.Copy).then_inc(g["mkTs"], 1)
                A.activation(mkT[0:NE, S * b:S * b + S], ps[0:NE, 6, 0:S], ACT.Copy).then_inc(g["mkTs"], 1)

            def gate_u(t):
                act.wait_ge(g["u"], t + 1)
                A.activation(sg[:, HID * t:HID * t + HID], bank(t, 256, 512), ACT.Exp, scale=-1.0).then_inc(g["eu"], 1)

            def act_hi(t):
                act.wait_ge(g["actT"], t + 1)
                A.activation(acTh[:, HID * t:HID * t + HID], bank((2 if t < 2 else 6) + t % 2, 0, 256),
                             ACT.Copy).then_inc(g["acTh"], 1)

            def mask_rows(b, j):
                act.wait_ge(g["bc"], 4 * b + j + 1)
                if 4 * b + j >= 2:
                    act.wait_ge(g["xm"], 4 * b + j - 1)
                    act.wait_ge(g["xml"], 4 * b + j - 1)
                A.activation(mkB[:, 512 * (j % 2):512 * (j % 2) + 512], bank((2 if b == 0 else 6) + j % 2),
                             ACT.Copy).then_inc(g["mb"], 1)

            def mask_y(t, halves):
                if t >= 2:
                    act.wait_ge(g["sum"], t - 1)
                for e in (e for e in range(NE) if e // 4 in halves):
                    if e % 4 == 0:
                        act.wait_ge(g["y"], 2 * t + e // 4 + 1)
                    k = 1024 * (t % 2) + P * e
                    last = A.activation(prod[:, k:k + P], bank(4 - 4 * (t % 2) + e // 4, P * (e % 4), P * (e % 4) + P),
                                        ACT.Copy, scale=mk[:, NE * t + e:NE * t + e + 1])
                    if e % 4 == 3:
                        last.then_inc(g["yr"], 1)

            for s in range(NS):
                x_slot(s)
                x_exp(s)
                if s > 0:
                    x_copy(s - 1)
                if s == 19:
                    ln_rstd(2, 0, 2)
                if s == 27:
                    act.wait_ge(s_w1l, NE)
                    f_rms(0)
                if s == 29:
                    f_head_rms(0)
                if s == 30:
                    f_hi(0)
            x_copy(NS - 1)
            act_recip_rows(1, 3, 0)
            f_qst(0, 4)
            ln_rstd(3, 2, 4)
            f_rms(1)
            f_x2T(1, 6)
            act_maxrows(act, a2, 0, 4)
            act_exp(act, a2, 0)
            f_head_rms(1)
            act_exp(act, a2, 1)
            f_hi(1)
            act_exp(act, a2, 2)
            f_qst(1, 0)
            f_copy(0, g["OtT"], a2.ott, 6, g["ott"])
            f_gate(0)
            act_maxrows(act, a2, 1, 4)
            act_exp(act, a2, 3)
            f_copy(0, g["gT"], fT, 6, g["gTs"])
            act_exp(act, a2, 4)
            f_rms3(0)
            act_exp(act, a2, 5)
            f_h2T(0)
            act.wait_ge(s_ldb, 16)
            A.activation(beh[0:NE, :], wbe[0:NE, 0:512], ACT.Copy).then_inc(g["be"], 1)
            f_mkT(0)
            for j in range(3):
                mask_rows(0, j)
            f_copy(1, g["OtT"], a2.ott, 6, g["ott"])
            mask_rows(0, 3)
            f_gate(1)
            gate_u(0)
            gate_u(1)
            f_copy(1, g["gT"], fT, 6, g["gTs"])
            act_hi(0)
            f_rms3(1)
            f_h2T(1)
            mask_y(0, (0, 1))
            act_hi(1)
            f_mkT(1)
            mask_rows(1, 0)
            mask_rows(1, 1)
            mask_y(1, (0,))
            mask_rows(1, 2)
            mask_y(1, (1,))
            mask_rows(1, 3)
            ln_rstd(4, 0, 2)
            gate_u(2)
            act_hi(2)
            gate_u(3)
            mask_y(2, (0,))
            act_hi(3)
            mask_y(2, (1,))
            mask_y(3, (0, 1))
            ln_rstd(5, 2, 4)

        @block.vector
        def _(dve):
            V = nc.vector
            n_dv = [0]

            def v(ins):
                n_dv[0] += 1
                ins.then_inc(s_dv, 1)
                return n_dv[0]

            def need(n):
                dve.wait_ge(s_dv, n)

            mv = st[:, 0:32].rearrange("p (t c) -> p t c", c=2)
            bn = bnst

            def stats(src, tiles, s_done, raw):
                need(n_dv[0])
                for k, t in enumerate(tiles):
                    n = v(V.bn_stats(bn[:, 6 * k:6 * k + 6], src[:, P * t:P * t + P]))
                for k, t in enumerate(tiles):
                    need(n - len(tiles) + 1 + k)
                    last = V.bn_aggr(raw[:, t, :], bn[:, 6 * k:6 * k + 6])
                    if k < len(tiles) - 1:
                        v(last)
                last.then_inc(s_done, 1)

            def ctx_stats(b):
                if b > 0:
                    dve.wait_ge(s_cst, b)
                stats(cx, range(4 * b, 4 * b + 4), s_cst, mv)

            def ctx_apply(b):
                dve.wait_ge(s_crs, b + 1)
                for k in range(4):
                    t = 4 * b + k
                    V.tensor_scalar(cx[:, P * t:P * t + P], cx[:, P * t:P * t + P], mv[:, t, 0:1],
                                    st[:, 32 + t:33 + t], ALU.subtract, ALU.mult).then_inc(s_cln, 1)

            def ctx_low(b):
                dve.wait_ge(s_cTh, b + 1)
                if b == 1:
                    dve.wait_ge(s_cTl, 1)
                n = v(V.tensor_scalar(cX[:, :], bank(b), cols[:, C_G1:C_G1 + 1], cols[:, C_B1:C_B1 + 1],
                                      ALU.mult, ALU.add))
                need(n)
                V.tensor_tensor(cTl[:, SC * b:SC * b + SC], cX[:, :], cTh[:, SC * b:SC * b + SC].bitcast(F),
                                ALU.subtract).then_inc(s_cTl, 1)

            dve.wait_ge(s_ldc, 32)
            ctx_stats(0)
            ctx_stats(1)
            dve.wait_ge(s_const, 3)
            V.tensor_copy(cR[:, 0:P], ident[:, :]).then_inc(s_constR, 1)
            V.tensor_copy(cR[:, P:3 * P], cS[:, :]).then_inc(s_constR, 1)
            dve.wait_ge(s_ldA, 16)
            for t in range(NT):
                dve.wait_ge(s_qkv, t + 1)
                V.tensor_tensor(a1.h[:, 384 * t:384 * t + 384], bank(4 + t, 0, 384), wA[:, A_B1:A_B1 + 384],
                                ALU.add).then_inc(s_h, 1)
            ctx_apply(0)
            ctx_apply(1)
            hv = a1.h[:, :].rearrange("p (n c d) -> p n c d", c=3, d=HD)
            qs = a1.qs[:, :].rearrange("p (n r d) -> p n r d", r=4, d=HD)
            ks = a1.ks[:, :].rearrange("p (n r d) -> p n r d", r=4, d=HD)
            for b in range(B):
                m = slice(32 * b, 32 * b + 32)
                dve.wait_ge(s_kev, 2 * b + 1)
                dve.wait_ge(s_h, 2 * b + 2)
                n = v(V.scalar_tensor_tensor(out=qs[:, m, 1, :], in0=hv[:, m, 0, :], scalar=HD ** -0.5,
                                             in1=qs[:, m, 0, :], op0=ALU.mult, op1=ALU.subtract))
                dve.wait_ge(s_kev, 2 * b + 2)
                n2 = v(V.tensor_tensor(ks[:, m, 2, :], hv[:, m, 1, :], ks[:, m, 0, :], ALU.subtract))
                need(n)
                V.tensor_copy(qs[:, m, 2, :], qs[:, m, 0, :]).then_inc(a1.s_qsplit, 1)
                need(n2)
                V.tensor_copy(ks[:, m, 1, :], ks[:, m, 0, :]).then_inc(a1.s_ksplit, 1)
            ctx_low(0)
            ctx_low(1)
            dve.wait_ge(s_vhi, 1)
            V.tensor_tensor(wkvl[:, 1024:2048], wkv[:, 1024:2048], wkvh[:, 1024:2048].bitcast(F),
                            ALU.subtract).then_inc(s_vlo, 1)

            def k_stack_ev(a, b, bk):
                kg = a.kg
                dve.wait_ge(a.s_T, (8 + 2 * kg) * (b + 1))
                if a is a2:
                    dve.wait_ge(s_zero, 7)
                    for j in range(4):
                        s = slice(32 * j, 32 * j + 32)
                        k0 = 1024 * b + 256 * j
                        V.tensor_copy(a.kst[s, k0:k0 + 256], ps[s, bk, 0:256]).then_inc(a.s_k_ev, 1)
                    return
                V.tensor_copy(a.kst[:, :].rearrange("p (g t) -> p g t", g=kg)[:, :, 256 * b:256 * b + 256],
                              ps[:, bk:bk + 2, :].rearrange("p a (g t) -> p (a g) t", g=2)).then_inc(a.s_k_ev, 1)

            k_stack_ev(a1, 0, 2)
            k_stack_ev(a1, 1, 6)
            dve.wait_ge(s_khi, 1)
            V.tensor_tensor(wkvl[:, 0:1024], wkv[:, 0:1024], wkvh[:, 0:1024].bitcast(F),
                            ALU.subtract).then_inc(s_klo, 1)
            for r in range(6):
                dve_max(dve, a1, r, v, need)
            dve_maxrows(dve, a1, 0, 4)
            dve_maxrows(dve, a1, 1, 6)

            kn = 0

            def k_lo(m):
                nonlocal kn
                for _ in range(m):
                    c, b = kn // 2, kn % 2
                    dve.wait_ge(s_khi, kn + 2)
                    kk = slice((b * NP + c) * SC, (b * NP + c + 1) * SC)
                    V.tensor_tensor(kcl[:, kk], bank(6 + kn % 2), kch[:, kk].bitcast(F),
                                    ALU.subtract).then_inc(s_kdn, 1)
                    kn += 1

            def ots(a, b, half):
                dve.wait_ge(a.s_PV, 2 * b + half + 1)
                if b > 0:
                    dve.wait_ge(a.s_OT, 2 * b)
                V.tensor_copy(a.ots[:, 512 * half:512 * half + 512], bank(4 + half)).then_inc(a.s_ots, 1)

            k_lo(6)
            ots(a1, 0, 0)
            ots(a1, 0, 1)
            k_lo(2)
            dve_norm(dve, a1, 0, v, need)
            k_lo(6)
            ots(a1, 1, 0)
            ots(a1, 1, 1)
            k_lo(1)
            dve_norm(dve, a1, 1, v, need)
            k_lo(1)

            def ln_stats(k, src, t0=0, t1=NT):
                dve.wait_ge(s_st, k) if k else dve.wait_ge(s_cst, 2)
                stats(src, range(t0, t1), s_st, mv)

            def ln_apply(k, src, dst, s_done, t0=0, t1=NT):
                dve.wait_ge(s_rs, k + 1)
                for t in range(t0, t1):
                    V.tensor_scalar(dst[:, P * t:P * t + P], src[:, P * t:P * t + P], mv[:, t, 0:1],
                                    st[:, 32 + t:33 + t], ALU.subtract, ALU.mult).then_inc(s_done, 1)

            def layernorm(k, src, dst, s_done):
                ln_stats(k, src)
                ln_apply(k, src, dst, s_done)

            dve.wait_ge(s_ldx, 16)
            n = v(V.tensor_tensor(xs[:, :].rearrange("p (t d) -> p t d", t=NT),
                                  xs[:, :].rearrange("p (t d) -> p t d", t=NT),
                                  wA[:, A_BP:A_BP + P].unsqueeze(1).to_broadcast([P, NT, P]), ALU.add))
            need(n)
            dve.wait_ge(s_pj, 1)
            n = v(V.tensor_tensor(xs[:, :], bank(1), xs[:, :], ALU.add))
            need(n)
            layernorm(0, xs, xs, s_xn)
            dve.wait_ge(s_xn, NT)
            layernorm(1, xs, ln, s_xn)
            dve.wait_ge(s_lnTs, 1)
            V.tensor_tensor(lnTl[:, :], lnT[:, :], lnTh[:, :].bitcast(F), ALU.subtract).then_inc(s_lnTs, 1)
            for n, (kind, c) in enumerate(LCH):
                if kind == "v":
                    continue
                dve.wait_ge(s_lhi, n + 1)
                bk = n % 8
                if kind == "q":
                    V.scalar_tensor_tensor(out=ql[:, S * c:S * c + S], in0=bank(bk, 0, S), scalar=XD ** -0.5,
                                           in1=qh[:, S * c:S * c + S].bitcast(F), op0=ALU.mult,
                                           op1=ALU.subtract).then_inc(s_llo, 1)
                else:
                    vv = lambda z: z[:, :].rearrange("p (b c t) -> p b c t", b=B, c=NP)[:, :, c, :]
                    V.tensor_tensor(vv(kll), bank(bk).rearrange("p (b t) -> p b t", b=B), vv(klh).bitcast(F),
                                    ALU.subtract).then_inc(s_llo, 1)

            def x_max(s):
                for u in range(2):
                    dve.wait_ge(s_S, 2 * s + u + 1)
                    if s >= 4:
                        dve.wait_ge(s_ex, 2 * (s - 4) + u + 1)
                    k = (2 * s + u) % 8
                    V.tensor_reduce(negmax[:, k:k + 1],
                                    ps[:, 2 * u:2 * u + 2, :].rearrange("p a b -> p (a b)")[:, 0:768],
                                    X, ALU.max, negate=True).then_inc(s_mx, 1)

            def x_copies(s):
                if s >= 2:
                    dve.wait_ge(s_pv, s - 1)
                for m in (0, 2):
                    dve.wait_ge(s_tr, 3 * s + m + 1)
                    p0 = (s % 2) * 1536 + 512 * m
                    V.tensor_copy(pT[:, p0:p0 + 512], bank(4 + m)).then_inc(s_cpD, 1)

            def x_out(s):
                b, c, i = STEPS[s]
                dve.wait_ge(s_pv, s + 1)
                V.tensor_copy(ot[:, S * c + P * i:S * c + P * i + P], bank(7, 0, P)).then_inc(s_oev, 1)

            def x_recip(b, n):
                dve.wait_ge(s_ex, 2 * (16 * b + 4 * n + 4))
                w = slice(32 * b, 32 * b + 32)
                pick = lambda z: z.rearrange("p (i h) -> p i h", i=2)[:, :, 4 * n:4 * n + 4]
                V.reciprocal(pick(rc[:, w]), pick(psums[:, w])).then_inc(s_rc, 1)

            def x_norm(b, n, bk):
                dve.wait_ge(s_R, 4 * b + n + 1)
                dve.wait_ge(s_oev, 16 * b + 4 * n + 4)
                V.tensor_tensor(ot[:, 512 * n:512 * n + 512], bank(bk), ot[:, 512 * n:512 * n + 512],
                                       ALU.mult).then_inc(s_on, 1)

            def x_add(b, bk):
                dve.wait_ge(s_xo, b + 1)
                V.tensor_tensor(xs[:, S * b:S * b + S], bank(bk, 0, S), xs[:, S * b:S * b + S],
                                ALU.add).then_inc(s_xadd, 1)

            def x_slot(s):
                what = SLOT.get(s, ("",))
                if what[0] == "q":
                    c = what[1]
                    dve.wait_ge(s_q1h, c + 1)
                    V.scalar_tensor_tensor(out=ql[:, S * c:S * c + S], in0=bank(7, 0, S), scalar=XD ** -0.5,
                                           in1=qh[:, S * c:S * c + S].bitcast(F), op0=ALU.mult,
                                           op1=ALU.subtract).then_inc(s_q1l, 1)
                elif what[0] == "R":
                    x_norm(what[1], what[2], 7)
                elif what[0] == "qkv":
                    f_h(0, 7)

            g = s_g

            def f_h(b, bk):
                dve.wait_ge(g["rstd"], b + 1)
                dve.wait_ge(s_ldg, 16)
                dve.wait_ge(g["qkv"], b + 1)
                for i in range(2):
                    t = 2 * b + i
                    V.scalar_tensor_tensor(out=a2.h[:, 192 * t:192 * t + 192], in0=bank(bk, 192 * i, 192 * i + 192),
                                           scalar=st[:, 40 + t:41 + t], in1=wG[:, G_BQKV:G_BQKV + 192],
                                           op0=ALU.mult, op1=ALU.add).then_inc(g["h"], 1)

            hh = a2.h[:, :].rearrange("p (t n d) -> p t n d", t=NT, d=HD)
            rope = wG[:, G_ROPE:G_ROPE + 32].rearrange("p (t k d) -> p t k d", t=2, k=2)
            rpv = rp[:, :].rearrange("p (t n d) -> p t n d", t=NT, d=HD)
            qn = wG[:, G_QN:G_QN + 160]

            def f_rope(b):
                dve.wait_ge(g["h"], 2 * b + 2)
                for i in range(2):
                    t = 2 * b + i
                    src = hh[:, t, 0:20, :]
                    tmp = rq[:, 160 * t:160 * t + 160].rearrange("p (n d) -> p n d", d=HD)
                    v(V.tensor_tensor(rpv[:, t, :, :], src, rope[:, i, 0:1, :].to_broadcast([P, 20, HD]), ALU.mult))
                    v(V.tensor_tensor(tmp[:, :, 0:4], src[:, :, 4:8], rope[:, i, 1:2, 0:4].to_broadcast([P, 20, 4]),
                                      ALU.mult))
                    n = v(V.tensor_tensor(tmp[:, :, 4:8], src[:, :, 0:4],
                                          rope[:, i, 1:2, 4:8].to_broadcast([P, 20, 4]), ALU.mult))
                need(n)
                w = slice(320 * b, 320 * b + 320)
                return v(V.tensor_tensor(rp[:, w], rp[:, w], rq[:, w], ALU.add))

            def f_squares(b, n):
                w = slice(320 * b, 320 * b + 320)
                need(n)
                n = v(V.tensor_tensor(rq[:, w], rp[:, w], rp[:, w], ALU.mult))
                need(n)
                ssq = st[:, 44:84]
                n = v(V.tensor_reduce(ssq, rq[:, w].rearrange("p (n d) -> p n d", d=HD), X, ALU.add))
                need(n)
                V.tensor_copy(rq[:, 320 * b + 40:320 * b + 80], ssq).then_inc(g["sq"], 1)

            def f_scale(b):
                w = slice(320 * b, 320 * b + 320)
                dve.wait_ge(g["rms"], b + 1)
                n = v(V.tensor_tensor(rp[:, w].rearrange("p (n d) -> p n d", d=HD),
                                      rp[:, w].rearrange("p (n d) -> p n d", d=HD),
                                      rq[:, 320 * b:320 * b + 40].unsqueeze(2).to_broadcast([P, 40, HD]), ALU.mult))
                need(n)
                V.tensor_tensor(rp[:, w].rearrange("p (t c) -> p t c", t=2),
                                rp[:, w].rearrange("p (t c) -> p t c", t=2),
                                qn.unsqueeze(1).to_broadcast([P, 2, 160]), ALU.mult).then_inc(g["ss"], 1)

            qs2 = a2.qs[:, :].rearrange("p (t n r d) -> p t n r d", t=NT, n=16, r=4)
            ks2 = a2.ks[:, :].rearrange("p (t n r d) -> p t n r d", t=NT, n=4, r=4)

            def f_low(b):
                m = slice(2 * b, 2 * b + 2)
                dve.wait_ge(g["ss"], b + 1)
                dve.wait_ge(g["hi"], 2 * b + 1)
                n = v(V.scalar_tensor_tensor(out=qs2[:, m, :, 1, :], in0=rpv[:, m, 0:16, :], scalar=HD ** -0.5,
                                             in1=qs2[:, m, :, 0, :], op0=ALU.mult, op1=ALU.subtract))
                dve.wait_ge(g["hi"], 2 * b + 2)
                n2 = v(V.tensor_tensor(ks2[:, m, :, 2, :], rpv[:, m, 16:20, :], ks2[:, m, :, 0, :], ALU.subtract))
                need(n)
                q3 = a2.qs[:, 1024 * b:1024 * b + 1024].rearrange("p (n r d) -> p n r d", r=4, d=HD)
                V.tensor_copy(q3[:, :, 2, :], q3[:, :, 0, :]).then_inc(a2.s_qsplit, 1)
                need(n2)
                k3 = a2.ks[:, 256 * b:256 * b + 256].rearrange("p (n r d) -> p n r d", r=4, d=HD)
                V.tensor_copy(k3[:, :, 1, :], k3[:, :, 0, :]).then_inc(a2.s_ksplit, 1)

            pair = lambda z, b: z[:, S * b:S * b + S].rearrange("p (t d) -> p t d", t=2)
            both = lambda ap: ap.unsqueeze(1).to_broadcast([P, 2, P])

            def f_gate_in(b):
                dve.wait_ge(g["gl"], b + 1)
                V.tensor_tensor(pair(gat, b), bank(7, 0, S).rearrange("p (t d) -> p t d", t=2),
                                both(wG[:, G_BG:G_BG + P]), ALU.add).then_inc(g["gpre"], 1)

            def f_gated(b):
                w = slice(S * b, S * b + S)
                dve.wait_ge(g["e"], b + 1)
                n = v(V.tensor_scalar(gat[:, w], gat[:, w], 1.0, None, ALU.add))
                need(n)
                n = v(V.reciprocal(gat[:, w], gat[:, w]))
                need(n)
                V.tensor_tensor(a2.otok[:, w], a2.otok[:, w], gat[:, w], ALU.mult).then_inc(g["gated"], 1)
                return v(V.tensor_tensor(pair(x3, b), pair(xs, b), both(wG[:, G_BO:G_BO + P]), ALU.add))

            def f_x3(b, n):
                w = slice(S * b, S * b + S)
                need(n)
                dve.wait_ge(g["wo"], b + 1)
                V.tensor_tensor(x3[:, w], bank(7, 0, S), x3[:, w], ALU.add).then_inc(g["x3"], 1)

            def f_h2(b):
                w = slice(S * b, S * b + S)
                dve.wait_ge(g["rstd3"], b + 1)
                for t in (2 * b, 2 * b + 1):
                    V.tensor_scalar(h2[:, P * t:P * t + P], x3[:, P * t:P * t + P], st[:, 84 + t:85 + t], None,
                                    ALU.mult).then_inc(g["h2"], 1)
                v(V.tensor_tensor(xs[:, w], xs[:, w], x3[:, w], ALU.add))

            def f_router(b):
                l3 = lg[:, 16 * b:16 * b + 16].rearrange("p (t e) -> p t e", t=2)
                l4 = lg[:, 32 + 16 * b:48 + 16 * b].rearrange("p (t e) -> p t e", t=2)
                top, pick = st[:, 88 + 2 * b:90 + 2 * b], st[:, 92 + 2 * b:94 + 2 * b]
                dve.wait_ge(g["lg"], b + 1)
                V.tensor_tensor(l3, bank(7, 0, 16).rearrange("p (t e) -> p t e", t=2),
                                wG[:, G_BR:G_BR + NE].unsqueeze(1).to_broadcast([P, 2, NE]), ALU.add
                                ).then_inc(g["lgr"], 1)
                dve.wait_ge(g["lgr"], b + 1)
                n = v(V.tensor_reduce(top, l3, X, ALU.max))
                need(n)
                n = v(V.tensor_tensor(l4, l3, top.unsqueeze(2).to_broadcast([P, 2, NE]), ALU.is_equal))
                need(n)
                n = v(V.tensor_tensor(l3, l4, wG[:, G_RK:G_RK + NE].unsqueeze(1).to_broadcast([P, 2, NE]), ALU.mult))
                need(n)
                n = v(V.tensor_reduce(pick, l3, X, ALU.max))
                need(n)
                V.tensor_tensor(mk[:, 16 * b:16 * b + 16].rearrange("p (t e) -> p t e", t=2), l3,
                                pick.unsqueeze(2).to_broadcast([P, 2, NE]), ALU.is_equal).then_inc(g["mk"], 1)
                w = slice(S * b, S * b + S)
                dve.wait_ge(g["h2Ts"], b + 1)
                V.tensor_tensor(h2l[:, w], h2T[:, w], h2h[:, w].bitcast(F), ALU.subtract).then_inc(g["low"], 1)

            def f_masked(b, j):
                dve.wait_ge(g["mb"], 4 * b + j + 1)
                src = mkB[:, 512 * (j % 2):512 * (j % 2) + 512].rearrange("p (e t) -> p e t", e=2)
                V.tensor_tensor(xmh[b][:, 512 * j:512 * j + 512].rearrange("p (e t) -> p e t", e=2), src,
                                h2h[:, S * b:S * b + S].bitcast(F).unsqueeze(1).to_broadcast([P, 2, S]),
                                ALU.mult).then_inc(g["xm"], 1)

            def gated_u(t):
                w = slice(HID * t, HID * t + HID)
                dve.wait_ge(g["eu"], t + 1)
                n = v(V.tensor_scalar(sg[:, w], sg[:, w], 1.0, None, ALU.add))
                need(n)
                n = v(V.reciprocal(sg[:, w], sg[:, w]))
                need(n)
                V.tensor_tensor(actf[:, w], bank(t, 0, 256), sg[:, w], ALU.mult).then_inc(g["act"], 1)

            def act_low(t):
                w = slice(HID * t, HID * t + HID)
                dve.wait_ge(g["acTh"], t + 1)
                V.tensor_tensor(acTl[:, w], bank((2 if t < 2 else 6) + t % 2, 0, 256), acTh[:, w].bitcast(F),
                                ALU.subtract).then_inc(g["acTl"], 1)

            def f_b2(b):
                w = slice(S * b, S * b + S)
                dve.wait_ge(g["b2"], b + 1)
                V.tensor_tensor(xs[:, w], bank(5, 0, S), xs[:, w], ALU.add).then_inc(g["b2r"], 1)

            def choose(t):
                dve.wait_ge(g["yr"], 2 * t + 2)
                V.tensor_reduce(yv[:, P * t:P * t + P],
                                prod[:, 1024 * (t % 2):1024 * (t % 2) + 1024].rearrange("p (e d) -> p d e", e=NE),
                                X, ALU.add).then_inc(g["sum"], 1)
                dve.wait_ge(g["sum"], t + 1)
                dve.wait_ge(g["b2r"], t // 2 + 1)
                return v(V.tensor_tensor(xs[:, P * t:P * t + P], xs[:, P * t:P * t + P], yv[:, P * t:P * t + P],
                                         ALU.add))

            n_rope = 0
            for s in range(NS):
                if SLOT.get(s, ("",))[0] == "rc":
                    x_recip(*SLOT[s][1:])
                x_slot(s)
                x_max(s)
                if s > 0:
                    x_copies(s - 1)
                if s == 18:
                    x_add(0, 7)
                if s > 1:
                    x_out(s - 2)
                if s == 19:
                    dve.wait_ge(s_xadd, 1)
                    ln_stats(2, xs, 0, 2)
                if s == 20:
                    ln_apply(2, xs, xs, s_xn, 0, 2)
                if s == 28:
                    n_rope = f_rope(0)
                if s == 29:
                    f_squares(0, n_rope)
                if s == 30:
                    f_scale(0)
                if s == 31:
                    f_low(0)
            x_copies(NS - 1)
            x_recip(1, 3)
            x_out(NS - 2)
            x_out(NS - 1)
            x_norm(1, 3, 1)
            k_stack_ev(a2, 0, 6)
            x_add(1, 7)
            dve.wait_ge(s_xadd, 2)
            ln_stats(3, xs, 2, 4)
            dve_max(dve, a2, 0, v, need)
            ln_apply(3, xs, xs, s_xn, 2, 4)
            dve_max(dve, a2, 1, v, need)
            dve_max(dve, a2, 2, v, need)
            dve_maxrows(dve, a2, 0, 4)
            f_h(1, 7)
            n_rope = f_rope(1)
            f_squares(1, n_rope)
            f_scale(1)
            f_low(1)
            ots(a2, 0, 0)
            ots(a2, 0, 1)
            k_stack_ev(a2, 1, 2)
            dve_norm(dve, a2, 0, v, need)
            dve_max(dve, a2, 3, v, need)
            dve_max(dve, a2, 4, v, need)
            f_gate_in(0)
            dve_max(dve, a2, 5, v, need)
            dve_maxrows(dve, a2, 1, 4)
            n = f_gated(0)
            f_x3(0, n)
            f_h2(0)
            f_router(0)
            ots(a2, 1, 0)
            ots(a2, 1, 1)
            dve_norm(dve, a2, 1, v, need)
            dve.wait_ge(g["be"], 1)
            V.tensor_tensor(bel[0:NE, :], wbe[0:NE, 0:512], beh[0:NE, :].bitcast(F), ALU.subtract).then_inc(g["be"], 1)
            for j in range(4):
                f_masked(0, j)
            f_gate_in(1)
            n = f_gated(1)
            gated_u(0)
            f_b2(0)
            f_x3(1, n)
            act_low(0)
            f_h2(1)
            gated_u(1)
            f_router(1)
            act_low(1)
            choose(0)
            f_masked(1, 0)
            f_masked(1, 1)
            f_masked(1, 2)
            f_masked(1, 3)
            n = choose(1)
            need(n)
            ln_stats(4, xs, 0, 2)
            gated_u(2)
            f_b2(1)
            ln_apply(4, xs, xs, g["v"], 0, 2)
            act_low(2)
            gated_u(3)
            act_low(3)
            choose(2)
            n = choose(3)
            need(n)
            ln_stats(5, xs, 2, 4)
            ln_apply(5, xs, xs, g["v"], 2, 4)


def kernel(**inputs):
    import numpy as np
    import concourse.bacc as bacc
    from concourse import mybir as mb
    from concourse.bass_utils import run_bass_kernel_spmd

    a = {k: np.asarray(v) for k, v in inputs.items()}
    f32 = np.float32

    def rows(v):
        return np.broadcast_to(v.reshape(1, -1), (P, v.size))

    def tiles(m):
        t = m.shape[0] // P
        return m.reshape(t, P, -1).transpose(1, 0, 2).reshape(P, -1)

    x = a["x"].reshape(B * S, D)
    d_a = np.concatenate([x.T, a["L0_attn_W1"], rows(a["L0_attn_b1"]), a["L0_attn_Wp"], rows(a["L0_attn_bp"])], 1)
    def gm(m):
        return m.reshape(-1, KV, H // KV, HD).transpose(0, 2, 1, 3).reshape(m.shape[0], -1)
    wq, bq = gm(a["L0_ffn_Wq"]), gm(a["L0_ffn_bq"].reshape(1, -1))
    wo = gm(a["L0_ffn_Wo"].T).T
    pos = np.arange(S, dtype=f32).reshape(2, P)
    inv = (1.0 / 10000.0 ** (np.arange(0, HD, 2, dtype=f32) / HD)).astype(f32)
    ang = (pos[:, :, None] * inv).astype(f32)
    cos, sin = np.cos(ang).astype(f32), np.sin(ang).astype(f32)
    rope = np.stack([np.concatenate([cos, cos], -1), np.concatenate([-sin, sin], -1)], 1)
    rope = rope.transpose(2, 0, 1, 3).reshape(P, -1)
    wg = np.zeros((P, P), f32)
    for h in range(H):
        wg[HD * h:HD * h + HD, HD * h:HD * h + HD] = a["L0_ffn_Wg"]
    d_g = np.concatenate([
        wq, a["L0_ffn_Wk"], a["L0_ffn_Wv"], rows(bq), rows(a["L0_ffn_bk"]), rows(a["L0_ffn_bv"]), rope,
        rows(np.concatenate([np.tile(a["L0_ffn_qn_w"], 16), np.tile(a["L0_ffn_kn_w"], 4)])),
        wg, rows(np.tile(a["L0_ffn_bg"], H)), wo, rows(a["L0_ffn_bo"]), a["L0_ffn_Wr"], rows(a["L0_ffn_br"]),
        rows(np.arange(NE, 0, -1).astype(f32))], 1)
    col = np.stack([a["L0_xattn_g1"], a["L0_xattn_b1"], a["L0_xattn_g2"], a["L0_xattn_b2"], a["L0_ffn_ln1_w"],
                    a["L0_ffn_ln2_w"], np.full(P, 1e-5, f32), np.full(P, 1e-6, f32)], 1)
    arrays = {
        "d_a": d_a, "d_x": tiles(x), "d_ctx": tiles(a["ctx_1024"].reshape(B * SC, D)), "d_cols": col,
        "d_wkv": a["L0_xattn_Wkv"], "d_wq": a["L0_xattn_Wq"], "d_wout": tiles(a["L0_xattn_Wout"]), "d_g": d_g,
        "d_we1": a["L0_ffn_W1"].transpose(1, 0, 2).reshape(D, -1),
        "d_we2": a["L0_ffn_W2"].reshape(NE, 2, P, D).transpose(2, 1, 0, 3).reshape(P, -1),
        "d_be": np.concatenate([a["L0_ffn_b1"], a["L0_ffn_b2"]], 1),
    }
    arrays = {k: np.ascontiguousarray(v) for k, v in arrays.items()}
    nc = bacc.Bacc("TRN2", target_bir_lowering=False, num_devices=1)
    args = [nc.dram_tensor(k, v.shape, mb.dt.from_np(v.dtype), kind="ExternalInput").ap() for k, v in arrays.items()]
    out = nc.dram_tensor("d_out", (P, NT * D), mb.dt.from_np(np.dtype(f32)), kind="ExternalOutput").ap()
    decoder_layer(nc, *args, out)
    r = run_bass_kernel_spmd(nc, [arrays], core_ids=[0])
    y = r.results[0]["d_out"]
    return y.reshape(P, NT, D).transpose(1, 0, 2).reshape(B, S, D)
```

```python
import concourse.bass as bass
from concourse import mybir
from contextlib import ExitStack

F = mybir.dt.float32
R = mybir.dt.float32r
ACT = mybir.ActivationFunctionType
ALU = mybir.AluOpType
X = mybir.AxisListType.X

P = 128
NEG = -2.0 ** 100
KB = 1024

B, S, D, SC = 2, 256, 128, 512
NT = B * S // P
H, HD = 16, 8
XH, XD = 16, 64
NP = XH // 2
CT = SC // P
KT = CT + S // P
NE, HID = 8, 256
KV = 4

A_XT, A_W1, A_B1, A_WP, A_BP, A_N = 0, 512, 896, 1280, 1408, 1536
G_QKV, G_BQKV, G_ROPE, G_QN, G_WG, G_BG, G_WO, G_BO, G_WR, G_BR, G_RK, G_N = (
    0, 192, 384, 416, 576, 704, 832, 960, 1088, 1096, 1104, 1112)
C_G1, C_B1, C_G2, C_B2, C_L1, C_L2, C_E5, C_E6 = range(8)


class Attn:
    pass


def decoder_layer(nc, d_a, d_x, d_ctx, d_cols, d_wkv, d_wq, d_wout, d_g, d_we1, d_we2, d_be, d_out):
    ctx = ExitStack()
    with ctx:
        def sem(name):
            return ctx.enter_context(nc.semaphore(name))

        base = 16512

        def at(name, cols, dt, off):
            return nc.alloc_sbuf_tensor_at(name, [P, cols], dt, offset=base + off)

        ident = at("ident", P, F, 0)
        cR = at("const_r", 3 * P, R, 512)
        xs = at("xs", NT * D, F, 2112)
        lnT = at("lnT", B * S, F, 4160)
        recT = at("recT", 2 * P, F, 4160)
        xq_w = at("xq_w", XH * XD, F, 6208)
        st = at("stats", 256, F, 10304)
        cols = at("cols", 8, F, 11328)
        bnst = at("bn_stats", 32, F, 11360)
        negmax = at("negmax", 8, F, 11488)
        rc = at("rc", 64, F, 11616)
        psums = st[:, 64:128]
        o_w = 11904
        o_ot = 16000
        o_q = 24192
        o_sc = 40576
        o_kch = 65152
        o_kcl = o_kch + 32 * KB
        o_vc = o_kcl + 32 * KB
        o_klh = o_vc + 32 * KB
        o_kll = o_klh + 16 * KB
        o_vl = o_kll + 16 * KB
        assert base + o_vl + 16 * KB <= 229344

        kch = at("kc_hi", B * NP * SC, R, o_kch)
        kcl = at("kc_lo", B * NP * SC, R, o_kcl)
        vc = at("vc", B * CT * XH * XD, F, o_vc)
        klh = at("kl_hi", B * NP * S, R, o_klh)
        kll = at("kl_lo", B * NP * S, R, o_kll)
        vl = at("vl", B * 2 * XH * XD, F, o_vl)
        qh = at("q_hi", NP * S, R, o_q)
        ql = at("q_lo", NP * S, R, o_q + 8 * KB)
        xout_w = at("xout_w", NP * D, F, o_w)
        ot = at("ot", NP * S, F, o_ot)
        pr = at("probs", 4 * 6 * P, F, o_sc)
        pT = at("probsT", 2 * 12 * P, F, o_sc + 12 * KB)
        wkvh = at("wkv_hi", 2048, R, o_sc)
        wkvl = at("wkv_lo", 2048, R, o_sc + 8 * KB)
        cTh = at("ctxT_hi", B * SC, R, o_sc + 16 * KB)
        cTl = at("ctxT_lo", B * SC, R, o_sc + 20 * KB)
        lnTh = at("lnT_hi", B * S, R, o_sc + 16 * KB)
        lnTl = at("lnT_lo", B * S, R, o_sc + 18 * KB)
        wkv = at("wkv_raw", 2048, F, o_q)
        wA = at("wA", A_N, F, o_q + 8 * KB)
        ln = at("ln_tok", NT * D, F, o_q + 14 * KB)
        cx = at("ctx_tok", B * SC, F, o_ot)
        cS = at("const_f", 2 * P, F, o_kcl)
        cX = at("ctxT_f", SC, F, o_kch)

        ps = ctx.enter_context(nc.psum_tensor("ps", [P, 8, 512], F))

        def bank(n, a=0, b=512):
            return ps[:, n, a:b]

        idR = cR[:, 0:P]
        up = cR[:, P:2 * P]
        low = cR[:, 2 * P:3 * P]

        def attn_buffers(tag, o_qst, o_kst, o_vp, o_pt, o_ots, o_otok, o_ott, o_qs, o_ks, o_h, kgroups):
            a = Attn()
            a.s_qsplit, a.s_ksplit = sem(tag + "q_split"), sem(tag + "k_split")
            a.s_T, a.s_q_ev, a.s_k_ev = sem(tag + "transposed"), sem(tag + "q_ready"), sem(tag + "k_ready")
            a.s_vp = sem(tag + "v_padded")
            a.s_S, a.s_max, a.s_nm = sem(tag + "scores"), sem(tag + "max_taken"), sem(tag + "negmax_split")
            a.s_q2T, a.s_q2a, a.s_q2d = (sem(tag + n) for n in (
                "q_with_max_T", "q_with_max_ready_act", "q_with_max_ready_dve"))
            a.s_ST, a.s_E, a.s_PV = sem(tag + "scores_t"), sem(tag + "exp_done"), sem(tag + "pv_done")
            a.s_ots, a.s_OT, a.s_O = sem(tag + "o_copied"), sem(tag + "o_untransposed"), sem(tag + "o_normed")
            a.kg = kgroups
            a.qst = at(tag + "qst", 4 * 512, R, o_qst)
            a.kst = at(tag + "kst", 2048, R, o_kst)
            a.vh = 4 * kgroups
            a.vp = at(tag + "vpad", NT * a.vh * 32, F, o_vp)
            a.pt = [at(f"{tag}pt{i}", 2048, F, o_pt[i]) for i in range(3)]
            a.ots = at(tag + "ots", 1024, F, o_ots)
            a.otok = at(tag + "otok", NT * P, F, o_otok)
            a.ott = at(tag + "ott", NT * P, F, o_ott)
            a.qs = at(tag + "qs", NT * 512, F, o_qs)
            a.ks = at(tag + "ks", NT * kgroups * P, F, o_ks)
            a.h = at(tag + "h", NT * (P + 64 * kgroups), F, o_h)
            return a

        LAT = o_klh
        a1 = attn_buffers("sa_", LAT + 24 * KB, LAT + 32 * KB, LAT + 40 * KB,
                          [LAT, LAT + 8 * KB, LAT + 16 * KB], o_ot + 4 * KB,
                          o_q, o_q + 2 * KB, LAT, LAT + 8 * KB, LAT + 16 * KB, 4)
        f0 = o_kch + 16 * KB
        f1 = o_kcl + 16 * KB
        f2 = o_vc + 16 * KB
        e1, e2 = o_kch, o_klh
        a2 = attn_buffers("ga_", f0, f0 + 8 * KB, e2 + 2 * KB, [f1, f1 + 8 * KB, f2],
                          f2 + 8 * KB, f2 + 12 * KB, f2 + 14 * KB, e1 + 8 * KB, e2, e1 + 5 * KB, 1)
        rp = at("rope_out", NT * 160, F, e1)
        rq = at("rope_tmp", NT * 160, F, e1 + 2560)
        x2T = at("x2T", NT * D, F, e2 + 4 * KB)
        wG = at("wG", G_N, F, 5184)
        wbe = at("wbe", 640, F, o_w)
        w1r = at("w1_raw", NE * 512, F, o_kch)
        w1h = at("w1_hi", NE * 512, R, o_kcl)
        w1l = at("w1_lo", NE * 512, R, o_vc)
        w2r = at("w2_raw", NE * 256, F, o_klh)
        w2h = at("w2_hi", NE * 256, R, o_kll)
        w2l = at("w2_lo", NE * 256, R, o_vl)
        beh = at("be_hi", 512, R, o_kll + 8 * KB)
        bel = at("be_lo", 512, R, o_kll + 10 * KB)
        x3 = at("x3", NT * D, F, o_kll + 12 * KB)
        xmh = [at("xm_hi0", NE * S, R, o_klh + 8 * KB), at("xm_hi1", NE * S, R, f1)]
        xml = [at("xm_lo0", NE * S, R, o_vl + 8 * KB), at("xm_lo1", NE * S, R, f1 + 8 * KB)]
        mkB = at("mask_rows", 1024, F, o_ot + 2 * KB)
        h2l = at("h2T_lo", NT * D, F, o_kll + 14 * KB)
        sc = o_sc
        h2 = at("h2_tok", NT * D, F, sc)
        h2T = at("h2T", NT * D, F, sc + 2 * KB)
        gat = at("gate", NT * D, F, sc + 4 * KB)
        lg = at("logits", 3 * NT * NE, F, sc + 6 * KB)
        mk = at("mask", NT * NE, F, sc + 6 * KB + 512)
        mkT = at("maskT", NT * P, F, sc + 8 * KB)
        mkR = at("maskT_r", NT * P, R, sc + 10 * KB)
        sg = at("sig", NT * HID, F, sc + 12 * KB)
        actf = at("act", NT * HID, F, sc + 16 * KB)
        acTh = at("actT_hi", NT * HID, R, sc + 20 * KB)
        acTl = at("actT_lo", NT * HID, R, o_q)
        prod = at("prod", 2 * 1024, F, o_q + 4 * KB)
        yv = at("y", NT * D, F, o_q + 12 * KB)
        h2h = at("h2T_hi", NT * D, R, o_q + 14 * KB)
        fT = at("gatedT", NT * D, F, o_ot)

        s_ldA, s_ldx, s_ldc, s_ldv, s_ldk, s_ldq, s_ldo = (sem(n) for n in (
            "ld_self_attn", "ld_x", "ld_ctx", "ld_wv", "ld_wk", "ld_wq", "ld_wout"))
        s_ldg, s_ldb, s_ld1, s_ld2, s_store = (sem(n) for n in ("ld_ffn", "ld_be", "ld_w1", "ld_w2", "store"))
        s_c0, s_const, s_zero, s_constR = (sem(n) for n in ("const0", "const", "zeroed", "const_r_ready"))
        s_dv, s_ac, s_po = sem("dve_chain"), sem("act_chain"), sem("pool_chain")
        s_vhi, s_vlo, s_khi, s_klo = (sem(n) for n in ("wv_hi", "wv_lo", "wk_hi", "wk_lo"))
        s_cst, s_crs, s_cln, s_cT, s_cTh, s_cTl = (sem(n) for n in (
            "ctx_stats", "ctx_rstd", "ctx_ln", "ctx_T", "ctxT_hi_ready", "ctxT_ready"))
        s_qkv, s_h = sem("qkv"), sem("h")
        s_vch, s_vev, s_kch, s_kev, s_kdn = (sem(n) for n in (
            "v_chunk", "v_evacuated", "k_chunk", "k_hi_done", "k_done"))
        s_OtT, s_ott, s_pj = (sem(n) for n in ("o_T", "o_T_sb", "proj"))
        s_st, s_rs, s_xn = sem("ln_stats"), sem("ln_rstd"), sem("ln_done")
        s_lnT, s_lnTs = sem("lat_T"), sem("lat_T_split")
        s_lch, s_lhi, s_llo = sem("lat_chunk"), sem("lat_hi"), sem("lat_done")
        s_S, s_mx, s_ex, s_tr, s_cpA, s_cpD, s_pv, s_oev = (sem(n) for n in (
            "x_scores", "x_max", "x_exp", "x_transposed", "x_copied_act", "x_copied_dve", "x_pv", "x_o_evacuated"))
        s_rc, s_rcT, s_rcS, s_R, s_on, s_xo, s_xadd = (sem(n) for n in (
            "x_recip", "x_recip_T", "x_recip_sb", "x_recip_bcast", "x_normed", "x_out", "x_added"))
        s_q1, s_q1h, s_q1l = sem("q_chunk"), sem("q_hi_done"), sem("q_done")
        s_w1h, s_w1l, s_w2h, s_w2l = (sem(n) for n in ("w1_hi_done", "w1_lo_done", "w2_hi_done", "w2_lo_done"))
        s_g = {n: sem("g_" + n) for n in (
            "x2T", "x2Tsb", "ss", "rstd", "qkv", "h", "sq", "rms", "OtT", "ott", "gl", "gpre", "e", "gated", "gT",
            "gTs", "wo", "x3", "lgr", "rstd3", "h2", "h2T", "h2Ts", "lg", "mk", "mkT", "mkTs", "bc", "xm",
            "hi", "rot", "swap", "hsq", "mb", "sum", "low", "xml", "be", "b2r", "u", "eu", "act", "actT", "acTh", "acTl", "y", "yr", "b2", "v")}

        STEPS = [(b, c, i) for b in range(B) for c in range(NP) for i in range(2)]
        NS = len(STEPS)
        SLOT = {}
        for _c in range(NP):
            SLOT[2 * _c + 2] = ("q", _c)
        for _b in range(B):
            for _n in range(3):
                SLOT[16 * _b + 4 * _n + 5] = ("rc", _b, _n)
                SLOT[16 * _b + 4 * _n + 7] = ("R", _b, _n)
        SLOT[17] = ("rc", 0, 3)
        SLOT[18] = ("R", 0, 3)
        SLOT[26] = ("x2T", 0)
        SLOT[28] = ("qkv", 0)
        LCH = [("q", c) for c in (0, 2, 4, 6, 1, 3, 5, 7)] + [("v", 0), ("v", 2)] + [("k", c) for c in range(NP)] + [
            ("v", 4), ("v", 6)] + [("v", 2 * n + 1) for n in range(4)]

        block = ctx.enter_context(nc.Block())

        @block.sync
        def _(sp):
            sp.dma_start(wA[:, :], d_a).then_inc(s_ldA, 16)
            sp.dma_start(cx[:, :], d_ctx).then_inc(s_ldc, 16)
            sp.dma_start(wkv[:, 1024:2048], d_wkv[:, 1024:2048]).then_inc(s_ldv, 16)
            sp.dma_start(xq_w[:, :], d_wq).then_inc(s_ldq, 16)
            sp.dma_start(xout_w[:, :], d_wout).then_inc(s_ldo, 16)
            sp.wait_ge(s_pv, 16)
            sp.dma_start(w1r[:, :], d_we1).then_inc(s_ld1, 16)
            sp.dma_start(w2r[:, :], d_we2).then_inc(s_ld2, 16)
            sp.wait_ge(s_q1, NP)
            sp.dma_start(wG[:, :], d_g).then_inc(s_ldg, 16)
            sp.wait_ge(s_xo, B)
            sp.dma_start(wbe[0:NE, :], d_be).then_inc(s_ldb, 16)
            for b in range(B):
                sp.wait_ge(s_g["v"], 2 * b + 2)
                sp.dma_start(d_out[:, S * b:S * b + S], xs[:, S * b:S * b + S]).then_inc(s_store, 16)
            sp.wait_ge(s_store, 16 * B)

        @block.gpsimd
        def _(pool):
            def max_slots(a):
                pool.memset(a.qs[:, :].rearrange("p (n r d) -> p n r d", r=4, d=HD)[:, :, 3, :], 0.0).then_inc(s_zero, 1)
                pool.memset(a.ks[:, :].rearrange("p (n r d) -> p n r d", r=4, d=HD)[:, :, 3, :], 1.0).then_inc(s_zero, 1)

            pool.memset(ident[:, :], 0.0).then_inc(s_c0, 1)
            pool.memset(cS[:, :], 0.0).then_inc(s_c0, 1)
            pool.wait_ge(s_c0, 2)
            pool.affine_select(out=ident[:, :], in_=ident[:, :], compare_op=ALU.not_equal, fill=1.0,
                               base=0, pattern=[[-1, P]], channel_multiplier=1).then_inc(s_const, 1)
            pool.affine_select(out=cS[:, 0:P], in_=cS[:, 0:P], compare_op=ALU.is_ge, fill=NEG,
                               base=0, pattern=[[-1, P]], channel_multiplier=1).then_inc(s_const, 1)
            pool.affine_select(out=cS[:, P:2 * P], in_=cS[:, P:2 * P], compare_op=ALU.is_ge, fill=NEG,
                               base=0, pattern=[[1, P]], channel_multiplier=-1).then_inc(s_const, 1)
            max_slots(a1)
            pool.memset(a1.vp[:, :], 0.0).then_inc(s_po, 1)
            pool.wait_ge(s_po, 1)
            pool.memset(a1.vp[:, :].rearrange("p (n c) -> p n c", c=32)[:, :, HD:HD + 1], 1.0).then_inc(s_zero, 1)
            def kv_low(s_hi, c0, s_lo):
                w = slice(c0, c0 + 1024)
                pool.wait_ge(s_hi, 1)
                pool.tensor_tensor(wkvl[:, w], wkv[:, w], wkvh[:, w].bitcast(F), ALU.subtract).then_inc(s_lo, 1)

            kv_low(s_vhi, 1024, s_vlo)
            mv = st[:, 0:32].rearrange("p (t c) -> p t c", c=2)
            for b in range(B):
                pool.wait_ge(s_crs, b + 1)
                for t in range(4 * b, 4 * b + 4):
                    pool.tensor_scalar(cx[:, P * t:P * t + P], cx[:, P * t:P * t + P], mv[:, t, 0:1],
                                       st[:, 32 + t:33 + t], ALU.subtract, ALU.mult).then_inc(s_cln, 1)
            kv_low(s_khi, 0, s_klo)
            pool.wait_ge(s_ld1, 16)
            for e in range(NE):
                w = slice(512 * e, 512 * e + 512)
                pool.tensor_copy(w1h[:, w], w1r[:, w]).then_inc(s_w1h, 1)
                pool.wait_ge(s_w1h, e + 1)
                pool.tensor_tensor(w1l[:, w], w1r[:, w], w1h[:, w].bitcast(F), ALU.subtract).then_inc(s_w1l, 1)
            pool.wait_ge(s_ld2, 16)
            for e in range(4):
                w = slice(512 * e, 512 * e + 512)
                pool.tensor_copy(w2h[:, w], w2r[:, w]).then_inc(s_w2h, 1)
                pool.wait_ge(s_w2h, e + 1)
                pool.tensor_tensor(w2l[:, w], w2r[:, w], w2h[:, w].bitcast(F), ALU.subtract).then_inc(s_w2l, 1)
            pool.wait_ge(s_w1l, NE)
            pool.wait_ge(s_w2l, 4)
            max_slots(a2)
            pool.memset(a2.vp[:, :], 0.0).then_inc(s_po, 1)
            pool.wait_ge(s_po, 2)
            pool.memset(a2.vp[:, :].rearrange("p (n c) -> p n c", c=32)[:, :, HD:HD + 1], 1.0).then_inc(s_zero, 1)
            rope = wG[:, G_ROPE:G_ROPE + 32].rearrange("p (t k d) -> p t k d", t=2, k=2)
            ks2 = a2.ks[:, :].rearrange("p (t n r d) -> p t n r d", t=NT, n=4, r=4)

            def f_swapped(b):
                pool.wait_ge(s_ldg, 16)
                pool.wait_ge(s_g["h"], 2 * b + 2)
                for i in range(2):
                    t = 2 * b + i
                    src = a2.h[:, 192 * t:192 * t + 160].rearrange("p (n d) -> p n d", d=HD)
                    tmp = rq[:, 160 * t:160 * t + 160].rearrange("p (n d) -> p n d", d=HD)
                    pool.tensor_tensor(tmp[:, :, 0:4], src[:, :, 4:8], rope[:, i, 1:2, 0:4].to_broadcast([P, 20, 4]),
                                       ALU.mult).then_inc(s_g["swap"], 1)
                    pool.tensor_tensor(tmp[:, :, 4:8], src[:, :, 0:4], rope[:, i, 1:2, 4:8].to_broadcast([P, 20, 4]),
                                       ALU.mult).then_inc(s_g["swap"], 1)

            def f_k_low(b):
                m = slice(2 * b, 2 * b + 2)
                pool.wait_ge(s_g["hi"], 2 * b + 2)
                kv = rp[:, 320 * b:320 * b + 320].rearrange("p (t n d) -> p t n d", t=2, n=20)[:, :, 16:20, :]
                k3 = a2.ks[:, 256 * b:256 * b + 256].rearrange("p (n r d) -> p n r d", r=4, d=HD)
                pool.tensor_tensor(ks2[:, m, :, 2, :], kv, ks2[:, m, :, 0, :], ALU.subtract).then_inc(a2.s_ksplit, 1)
                pool.tensor_copy(k3[:, :, 1, :], k3[:, :, 0, :]).then_inc(a2.s_ksplit, 1)

            f_swapped(0)
            f_k_low(0)
            pool.wait_ge(s_pv, NS)
            pool.memset(a2.kst[:, :].bitcast(F), 0.0).then_inc(s_zero, 1)
            f_swapped(1)
            f_k_low(1)
            for b in range(B):
                pool.wait_ge(s_g["low"], b + 1)
                for j in range(4):
                    pool.wait_ge(s_g["mb"], 4 * b + j + 1)
                    pool.tensor_tensor(xml[b][:, 512 * j:512 * j + 512].rearrange("p (e t) -> p e t", e=2),
                                       mkB[:, 512 * (j % 2):512 * (j % 2) + 512].rearrange("p (e t) -> p e t", e=2),
                                       h2l[:, S * b:S * b + S].unsqueeze(1).to_broadcast([P, 2, S]),
                                       ALU.mult).then_inc(s_g["xml"], 1)

        ROUNDS = [(b, kind) for b in range(B) for kind in range(3)]

        def q_transposes(pe, a, b, bk, s_done):
            for g in range(4):
                for i in range(2):
                    pe.transpose(ps[:, bk + g // 2, 256 * (g % 2) + P * i:256 * (g % 2) + P * i + P],
                                 a.qs[:, (2 * b + i) * 512 + P * g:(2 * b + i) * 512 + P * g + P],
                                 ident[:, :]).then_inc(s_done, 1)

        def pe_stacks(pe, a, b, bq, bk):
            kg = a.kg
            if b == 0:
                pe.wait_ge(s_zero, 2 if a is a1 else 5)
            pe.wait_ge(a.s_qsplit, b + 1)
            q_transposes(pe, a, b, bq, a.s_T)
            pe.wait_ge(a.s_ksplit, b + 1 if a is a1 else 2 * b + 2)
            for g in range(kg):
                for i in range(2):
                    pe.transpose(ps[:, bk + g // 2, 256 * (g % 2) + P * i:256 * (g % 2) + P * i + P],
                                 a.ks[:, ((2 * b + i) * kg + g) * P:((2 * b + i) * kg + g + 1) * P],
                                 ident[:, :]).then_inc(a.s_T, 1)

        def free_scoresT(a, r, hf):
            if r % 3 == 0 and (r == 0 or a is a2):
                return a.s_max, (11 if a is a1 else 5 + 2 * r) + hf
            return a.s_E, 2 * (r - 1) + hf + 1

        def pe_scores(pe, a, r):
            b, kind = ROUNDS[r]
            if r % 3 == 0:
                pe.wait_ge(a.s_q_ev, b + 1)
                pe.wait_ge(a.s_k_ev, b + 1)
            tok = 256 * b
            n = 4 if kind == 0 else 2
            w = 512 // n
            for hf in range(2):
                if r > 0:
                    pe.wait_ge(a.s_max, 2 * (r - 1) + hf + 1)
                quads = (2 * hf, 2 * hf + 1)
                for j in quads:
                    pe.matmul(ps[:, j, :].rearrange("p (n w) -> p n w", n=n)[:, :, w - P:w], idR,
                              up.unsqueeze(1).to_broadcast([P, n, P]), start=True, stop=False,
                              skip_group_check=True)
                for m in range(n):
                    g = m if kind == 0 else 2 * (kind - 1) + m
                    q0 = 512 * g + tok + (0 if kind == 0 else P)
                    k0 = 512 * g + tok
                    for j in quads:
                        s = slice(32 * j, 32 * j + 32)
                        last = pe.matmul(ps[:, j, w * m:w * m + w], a.qst[s, q0:q0 + P], a.kst[s, k0:k0 + w],
                                         start=False, stop=True, skip_group_check=True)
                last.then_inc(a.s_S, 1)

        def pe_maxrows(pe, a, b, bk):
            pe.wait_ge(a.s_nm, b + 1)
            q_transposes(pe, a, b, bk, a.s_q2T)

        def pe_scoresT(pe, a, r):
            b, kind = ROUNDS[r]
            if kind == 0:
                pe.wait_ge(a.s_q2a, b + 1)
                pe.wait_ge(a.s_q2d, b + 1)
            tok = 256 * b
            n = 4 if kind == 0 else 2
            w = 512 // n
            q1 = tok + (P if kind == 0 else 0)
            for hf in range(2):
                pe.wait_ge(*free_scoresT(a, r, hf))
                quads = (2 * hf, 2 * hf + 1)
                for j in quads:
                    pe.matmul(ps[:, j, :].rearrange("p (n w) -> p n w", n=n)[:, :, 0:P], idR,
                              low.unsqueeze(1).to_broadcast([P, n, P]), start=True, stop=False,
                              skip_group_check=True)
                for m in range(n):
                    g = m if kind == 0 else 2 * (kind - 1) + m
                    k0 = 512 * g + tok + (P if kind == 0 else 0)
                    q0 = 512 * g + q1
                    for j in quads:
                        s = slice(32 * j, 32 * j + 32)
                        last = pe.matmul(ps[:, j, w * m:w * m + w], a.kst[s, k0:k0 + P], a.qst[s, q0:q0 + w],
                                         start=False, stop=True, skip_group_check=True)
                last.then_inc(a.s_ST, 1)

        def pe_scores_shared(pe, a, r):
            b, kind = ROUNDS[r]
            if kind == 0:
                pe.wait_ge(a.s_q_ev, b + 1)
                pe.wait_ge(a.s_k_ev, 4 * b + 4)
            n = 4 if kind == 0 else 2
            w = 512 // n
            kk = a.kst[:, 1024 * b:1024 * b + 1024].rearrange("p (j t) -> p j t", j=4)
            for hf in range(2):
                if r == 3:
                    pe.wait_ge(a.s_E, 5 + hf)
                elif r > 0:
                    pe.wait_ge(a.s_max, 2 * (r - 1) + hf + 1)
                for m in range(2):
                    bk = 2 * hf + m
                    g = bk if kind == 0 else 2 * (kind - 1) + hf
                    q0 = 512 * g + 256 * b + (0 if kind == 0 else P)
                    j0 = 0 if kind == 0 else 2 * m
                    pe.matmul(ps[:, bk, :].rearrange("p (n w) -> p n w", n=n)[:, :, w - P:w], idR,
                              up.unsqueeze(1).to_broadcast([P, n, P]), start=True, stop=False,
                              skip_group_check=True)
                    last = pe.matmul(ps[:, bk, :].rearrange("p (n w) -> p n w", n=n), a.qst[:, q0:q0 + P],
                                     kk[:, j0:j0 + n, 0:w], start=False, stop=True, skip_group_check=True)
                last.then_inc(a.s_S, 1)

        def pe_scoresT_shared(pe, a, r):
            b, kind = ROUNDS[r]
            if kind == 0:
                pe.wait_ge(a.s_q2a, b + 1)
                pe.wait_ge(a.s_q2d, b + 1)
            n = 4 if kind == 0 else 2
            w = 512 // n
            g0 = 0 if kind == 0 else 2 * (kind - 1)
            t0 = P if kind == 0 else 0
            qq = a.qst[:, :].rearrange("p (g t) -> p g t", g=4)
            for hf in range(2):
                pe.wait_ge(*free_scoresT(a, r, hf))
                for j in (2 * hf, 2 * hf + 1):
                    k0 = 1024 * b + 256 * j + t0
                    out = ps[:, j, :].rearrange("p (n w) -> p n w", n=n)
                    pe.matmul(out[:, :, 0:P], idR, low.unsqueeze(1).to_broadcast([P, n, P]),
                              start=True, stop=False, skip_group_check=True)
                    last = pe.matmul(out, a.kst[:, k0:k0 + P],
                                     qq[:, g0:g0 + n, 256 * b + t0:256 * b + t0 + w],
                                     start=False, stop=True, skip_group_check=True)
                last.then_inc(a.s_ST, 1)

        def pe_values(pe, a, b, half):
            pe.wait_ge(a.s_E, 2 * (3 * b + 2 + half))
            if half == 0:
                pe.wait_ge(a.s_vp, b + 1 if a is a2 else 1)
                if b > 0:
                    pe.wait_ge(a.s_O, 2 * b)
            short = a.pt[(3 * b) % 3]
            long = a.pt[(3 * b + 1 + half) % 3]
            for m in range(2):
                g = 2 * half + m
                for t, (buf, c0, w) in enumerate(((long, 256 * m, 256), (short, P * g, P))):
                    for j in range(4):
                        head = (4 * g + j) if a.kg > 1 else j
                        v0 = ((2 * b + t) * a.vh + head) * 32
                        last = pe.matmul(ps[32 * j:32 * j + 32, 4 + half, 256 * m + 256 - w:256 * m + 256],
                                         a.vp[:, v0:v0 + 32], buf[:, 512 * j + c0:512 * j + c0 + w],
                                         start=(t == 0), stop=(t == 1), skip_group_check=True)
            last.then_inc(a.s_PV, 1)

        def pe_untranspose(pe, a, b):
            pe.wait_ge(a.s_ots, 2 * b + 2)
            for i in range(2):
                for g in range(4):
                    c = 512 * (g // 2) + 256 * (g % 2) + P * i
                    last = pe.transpose(ps[:, 4 + i, P * g:P * g + P], a.ots[:, c:c + P], ident[:, :])
                last.then_inc(a.s_OT, 1)

        def act_maxrows(act, a, b, bk):
            act.wait_ge(a.s_q2T, 8 * (b + 1))
            act.wait_ge(a.s_S, 6 * (b + 1))
            nc.scalar.activation(a.qst[:, :].rearrange("p (g t) -> p g t", g=4)[:, 0:2, 256 * b:256 * b + 256],
                                 ps[:, bk, :].rearrange("p (g t) -> p g t", g=2), ACT.Copy).then_inc(a.s_q2a, 1)

        def dve_maxrows(dve, a, b, bk):
            dve.wait_ge(a.s_q2T, 8 * (b + 1))
            dve.tensor_copy(a.qst[:, :].rearrange("p (g t) -> p g t", g=4)[:, 2:4, 256 * b:256 * b + 256],
                            ps[:, bk + 1, :].rearrange("p (g t) -> p g t", g=2)).then_inc(a.s_q2d, 1)

        def act_exp(act, a, r):
            if r == 0 and a is a1:
                act.wait_ge(a.s_q2T, 16)
                act.wait_ge(a.s_T, 16 + 4 * a.kg)
            if r == 3:
                act.wait_ge(a.s_PV, 2)
            for hf in range(2):
                act.wait_ge(a.s_ST, 2 * r + hf + 1)
                nc.scalar.activation(a.pt[r % 3][:, 1024 * hf:1024 * hf + 1024],
                                     ps[:, 2 * hf:2 * hf + 2, :].rearrange("p a b -> p (a b)"),
                                     ACT.Exp).then_inc(a.s_E, 1)

        def dve_max(dve, a, r, v, need):
            b, kind = ROUNDS[r]
            t = 2 * b + (0 if kind == 0 else 1)
            nmf = st[:, 128:192].rearrange("p (t g j) -> p t g j", t=NT, g=4)
            for hf in range(2):
                dve.wait_ge(a.s_S, 2 * r + hf + 1)
                jj = slice(2 * hf, 2 * hf + 2)
                if a is a2:
                    src = ps[:, jj, :].rearrange("p j (g w) -> p (j g) w", g=4 if kind == 0 else 2)
                    g0 = 2 * hf if kind == 0 else 2 * (kind - 1) + hf
                    dst = st[:, 128 + 16 * t + 4 * g0:128 + 16 * t + 4 * g0 + (8 if kind == 0 else 4)]
                elif kind == 0:
                    src = ps[:, jj, :].rearrange("p j (g w) -> p j g w", g=4)
                    dst = nmf[:, t, :, jj].rearrange("p g j -> p j g")
                else:
                    src = ps[:, jj, :].rearrange("p j (g w) -> p j g w", g=2)
                    dst = nmf[:, t, 2 * (kind - 1):2 * kind, jj].rearrange("p g j -> p j g")
                dve.tensor_reduce(dst, src, X, ALU.max, negate=True).then_inc(a.s_max, 1)
            if kind == 2:
                dve.wait_ge(a.s_max, 2 * r + 2)
                dve.wait_ge(a.s_T, (8 + 2 * a.kg) * (b + 1))
                src = st[:, 128:192].rearrange("p (t c) -> p t c", t=NT)[:, 2 * b:2 * b + 2, :]
                dst = a.qs[:, :].rearrange("p (t n r d) -> p t n r d", t=NT, n=16, r=4)[:, 2 * b:2 * b + 2, :, 3, :]
                n = v(dve.tensor_copy(dst[:, :, :, 0].bitcast(R), src))
                need(n)
                dve.tensor_tensor(dst[:, :, :, 1], src, dst[:, :, :, 0], ALU.subtract).then_inc(a.s_nm, 1)

        def dve_norm(dve, a, b, v, need):
            for i in range(2):
                t = 2 * b + i
                dve.wait_ge(a.s_OT, t + 1)
                src = ps[:, 4 + i, :].rearrange("p (h c) -> p h c", c=32)
                n = v(dve.reciprocal(st[:, 192 + 16 * t:208 + 16 * t], src[:, :, HD]))
                need(n)
                dve.tensor_tensor(a.otok[:, P * t:P * t + P].rearrange("p (h c) -> p h c", c=HD),
                                  src[:, :, 0:HD],
                                  st[:, 192 + 16 * t:208 + 16 * t].unsqueeze(2).to_broadcast([P, 16, HD]),
                                  ALU.mult).then_inc(a.s_O, 1)

        def lat_hi(n):
            return sum(kind != "v" or c // 2 % 2 == 0 for kind, c in LCH[:n])

        def lat_lo(n):
            return sum(kind != "v" or c // 2 % 2 == 1 for kind, c in LCH[:n])

        def lat_bank(n):
            return 2 + n % 4 if n < 8 else n % 8 if n < 16 else 4 + n % 4

        @block.tensor
        def _(pe):
            def three(out, xh, xl, wh, wl, start=True):
                pe.matmul(out, xh, wh, start=start, stop=False)
                pe.matmul(out, xh, wl, start=False, stop=False)
                return pe.matmul(out, xl, wh, start=False, stop=True)

            pe.wait_ge(s_ldA, 16)
            for t in range(NT):
                pe.matmul(bank(4 + t, 0, 384), wA[:, A_XT + P * t:A_XT + P * t + P], wA[:, A_W1:A_W1 + 384],
                          start=True, stop=True).then_inc(s_qkv, 1)

            def ctx_transposes(b):
                pe.wait_ge(s_cln, 4 * (b + 1))
                pe.wait_ge(a1.s_q_ev, 2)
                for i in range(4):
                    t = 4 * b + i
                    last = pe.transpose(bank(4 + b, P * i, P * i + P), cx[:, P * t:P * t + P], ident[:, :])
                last.then_inc(s_cT, 1)

            pe.wait_ge(s_const, 1)
            pe_stacks(pe, a1, 0, 0, 2)
            pe.wait_ge(s_h, 4)
            pe_stacks(pe, a1, 1, 4, 6)
            pe.wait_ge(s_constR, 2)

            def v_chunk(n):
                t, half = n // 2, n % 2
                if n == 0:
                    pe.wait_ge(s_vlo, 1)
                    pe.wait_ge(s_cTl, 2)
                    pe.wait_ge(a1.s_k_ev, 2)
                if n >= 4:
                    pe.wait_ge(s_vev, n - 3)
                c = slice(1024 + 512 * half, 1536 + 512 * half)
                tt = slice(P * t, P * t + P)
                three(bank(4 + n % 4), cTh[:, tt], cTl[:, tt], wkvh[:, c], wkvl[:, c]).then_inc(s_vch, 1)

            vn = 0
            for r, m in enumerate((0, 0, 3, 4, 4, 5)):
                pe_scores(pe, a1, r)
                if r == 1:
                    ctx_transposes(0)
                    ctx_transposes(1)
                for _ in range(m):
                    v_chunk(vn)
                    vn += 1
            pe.wait_ge(s_vev, 16)
            pe_maxrows(pe, a1, 0, 4)
            pe_maxrows(pe, a1, 1, 6)

            def k_chunk(n):
                c, b = n // 2, n % 2
                if n == 0:
                    pe.wait_ge(s_klo, 1)
                    pe.wait_ge(a1.s_q2a, 2)
                    pe.wait_ge(a1.s_q2d, 2)
                if n >= 2:
                    pe.wait_ge(s_kdn, n - 1)
                cc = slice(P * c, P * c + P)
                tt = slice(SC * b, SC * b + SC)
                three(bank(6 + n % 2), wkvh[:, cc], wkvl[:, cc], cTh[:, tt], cTl[:, tt]).then_inc(s_kch, 1)

            kn = 0

            def k_chunks(m):
                nonlocal kn
                for _ in range(m):
                    k_chunk(kn)
                    kn += 1

            pe_scoresT(pe, a1, 0)
            k_chunks(2)
            pe_scoresT(pe, a1, 1)
            k_chunks(2)
            pe_scoresT(pe, a1, 2)
            pe_values(pe, a1, 0, 0)
            k_chunks(2)
            pe_scoresT(pe, a1, 3)
            pe_values(pe, a1, 0, 1)
            k_chunks(2)
            pe_scoresT(pe, a1, 4)
            pe_untranspose(pe, a1, 0)
            k_chunks(2)

            def o_transposes(b, bk):
                for t in (2 * b, 2 * b + 1):
                    pe.wait_ge(a1.s_O, t + 1)
                    last = pe.transpose(bank(bk, P * (t % 2), P * (t % 2) + P), a1.otok[:, P * t:P * t + P],
                                        ident[:, :])
                last.then_inc(s_OtT, 1)

            def o_project(b, bk):
                pe.wait_ge(s_ott, b + 1)
                for t in (2 * b, 2 * b + 1):
                    last = pe.matmul(bank(bk, P * (t % 2), P * (t % 2) + P), a1.ott[:, P * t:P * t + P],
                                     wA[:, A_WP:A_WP + P], start=(t % 2 == 0), stop=True, skip_group_check=True)
                last.then_inc(s_pj, 1)

            def ln_transposes(b, bk):
                pe.wait_ge(s_xn, 4 * b + 4)
                for t in (2 * b, 2 * b + 1):
                    last = pe.transpose(bank(bk, P * (t % 2), P * (t % 2) + P), ln[:, P * t:P * t + P], ident[:, :])
                last.then_inc(s_lnT, 1)

            def lat_chunk(n):
                kind, c = LCH[n]
                m = n - (6 if 8 <= n < 16 else 4)
                if m >= 0 and n not in (8, 9, 14, 15):
                    pe.wait_ge(s_lhi, lat_hi(m + 1))
                    pe.wait_ge(s_llo, lat_lo(m + 1))
                bk = lat_bank(n)
                if kind == "q":
                    pe.matmul(bank(bk, 0, S), xq_w[:, P * c:P * c + P], lnT[:, 0:S],
                              start=True, stop=True).then_inc(s_lch, 1)
                elif kind == "k":
                    cc = slice(P * c, P * c + P)
                    three(bank(bk), wkvh[:, cc], wkvl[:, cc], lnTh[:, :], lnTl[:, :]).then_inc(s_lch, 1)
                else:
                    t, half = c // 2, c % 2
                    w = slice(1024 + 512 * half, 1536 + 512 * half)
                    tt = slice(P * t, P * t + P)
                    three(bank(bk), lnTh[:, tt], lnTl[:, tt], wkvh[:, w], wkvl[:, w]).then_inc(s_lch, 1)

            g = s_g

            def f_x2T(b, bk):
                pe.wait_ge(s_xn, 2 * NT + 2 * (b + 1))
                for i in range(2):
                    t = 2 * b + i
                    last = pe.transpose(bank(bk, P * i, P * i + P), xs[:, P * t:P * t + P], ident[:, :])
                last.then_inc(g["x2T"], 1)

            def f_qkv(b, bk):
                pe.wait_ge(g["x2Tsb"], b + 1)
                pe.wait_ge(s_ldg, 16)
                for i in range(2):
                    t = 2 * b + i
                    last = pe.matmul(bank(bk, 192 * i, 192 * i + 192), x2T[:, P * t:P * t + P],
                                     wG[:, G_QKV:G_QKV + 192], start=(i == 0), stop=True, skip_group_check=True)
                last.then_inc(g["qkv"], 1)

            o_transposes(0, 4)
            o_project(0, 5)
            k_chunks(1)
            pe_scoresT(pe, a1, 5)
            pe_values(pe, a1, 1, 0)
            k_chunks(1)
            pe.wait_ge(s_st, 1)
            pe_values(pe, a1, 1, 1)
            ln_transposes(0, 3)
            k_chunks(1)
            pe_untranspose(pe, a1, 1)
            pe.wait_ge(s_lnTs, 1)
            pe.wait_ge(s_ldq, 16)
            lat_chunk(0)
            lat_chunk(1)
            o_transposes(1, 0)
            lat_chunk(2)
            o_project(1, 1)
            lat_chunk(3)
            k_chunks(1)
            lat_chunk(4)
            lat_chunk(5)
            k_chunks(1)
            lat_chunk(6)
            k_chunks(1)
            pe.wait_ge(s_lhi, lat_hi(5))
            pe.wait_ge(s_llo, lat_lo(5))
            ln_transposes(1, 2)
            lat_chunk(7)
            pe.wait_ge(s_lnTs, 3)
            lat_chunk(8)
            lat_chunk(9)
            pe.wait_ge(s_lnTs, 5)
            pe.wait_ge(s_kdn, 16)
            for n in range(10, len(LCH) - 4):
                lat_chunk(n)
            bank7_read = ()

            def x_scores(s):
                b, c, i = STEPS[s]
                if s == 0:
                    pe.wait_ge(s_lhi, lat_hi(12))
                    pe.wait_ge(s_llo, lat_lo(12))
                if b == 1 and i == 0:
                    pe.wait_ge(s_q1l, c + 1)
                if s > 0:
                    pe.wait_ge(s_ex, 2 * s)
                q = slice(S * c + P * i, S * c + P * i + P)
                kc = slice((b * NP + c) * SC, (b * NP + c + 1) * SC)
                kl = slice((b * NP + c) * S, (b * NP + c + 1) * S)
                for n, (qq, kk, ll) in enumerate(((qh, kch, klh), (qh, kcl, kll), (ql, kch, klh))):
                    for hh in range(2):
                        rows = slice(64 * hh, 64 * hh + 64)
                        pe.matmul(bank(2 * hh), qq[rows, q], kk[rows, kc], start=(n == 0), stop=(n == 2))
                    for hh in range(2):
                        rows = slice(64 * hh, 64 * hh + 64)
                        last = pe.matmul(bank(2 * hh + 1, 0, S), qq[rows, q], ll[rows, kl],
                                         start=(n == 0), stop=(n == 2))
                        if n == 2:
                            last.then_inc(s_S, 1)
                    if n == 0:
                        x_slot(s)

            def x_transposes(s):
                if s == 0:
                    pe.wait_ge(s_lhi, lat_hi(len(LCH)))
                    pe.wait_ge(s_llo, lat_lo(len(LCH)))
                for u in range(2):
                    pe.wait_ge(s_ex, 2 * s + u + 1)
                    slot = (2 * s + u) % 4
                    for kt in range(KT):
                        n = KT * u + kt
                        if n % 4 == 0 and s > 0:
                            if n // 4 == 1:
                                pe.wait_ge(s_cpA, s)
                            else:
                                pe.wait_ge(s_cpD, 2 * (s - 1) + (1 if n == 0 else 2))
                        last = pe.transpose(bank(4 + n // 4, P * (n % 4), P * (n % 4) + P),
                                            pr[:, (slot * KT + kt) * P:(slot * KT + kt + 1) * P], ident[:, :])
                        if n % 4 == 3:
                            last.then_inc(s_tr, 1)

            def x_values(s):
                b, c, i = STEPS[s]
                pe.wait_ge(s_cpA, s + 1)
                pe.wait_ge(s_cpD, 2 * s + 2)
                if s > 0:
                    pe.wait_ge(s_oev, s)
                if bank7_read:
                    pe.wait_ge(*bank7_read)
                buf = (s % 2) * 12 * P
                for kt in range(KT):
                    for hh in range(2):
                        if kt < CT:
                            v0 = (b * CT + kt) * 1024 + P * c + 64 * hh
                            v = vc[:, v0:v0 + 64]
                        else:
                            v0 = (b * 2 + kt - CT) * 1024 + P * c + 64 * hh
                            v = vl[:, v0:v0 + 64]
                        p0 = buf + (KT * hh + kt) * P
                        last = pe.matmul(ps[64 * hh:64 * hh + 64, 7, 0:P], v, pT[:, p0:p0 + P],
                                         start=(kt == 0), stop=(kt == KT - 1))
                last.then_inc(s_pv, 1)

            def x_recip_rows(b, n, bk):
                pe.wait_ge(s_rc, 4 * b + n + 1)
                for i in range(2):
                    k = 32 * b + 16 * i + 4 * n
                    last = pe.transpose(ps[0:4, bk, P * i:P * i + P], rc[:, k:k + 4], ident[:, :])
                last.then_inc(s_rcT, 1)

            def x_recip_spread(b, n, bk):
                pe.wait_ge(s_rcS, 4 * b + n + 1)
                for m in range(2):
                    for hh in range(2):
                        last = pe.matmul(ps[64 * hh:64 * hh + 64, bk, 256 * m:256 * m + 256],
                                         ident[0:4, 2 * m + hh:2 * m + hh + 1].to_broadcast([4, 64]),
                                         recT[0:4, :], start=(m == 0), stop=True, skip_group_check=True)
                last.then_inc(s_R, 1)

            def x_slot(s):
                nonlocal bank7_read
                if s not in SLOT:
                    return
                if s > 2:
                    pe.wait_ge(s_oev, s - 2)
                if bank7_read:
                    pe.wait_ge(*bank7_read)
                what = SLOT[s]
                if what[0] == "q":
                    c = what[1]
                    pe.matmul(bank(7, 0, S), xq_w[:, P * c:P * c + P], lnT[:, S:2 * S],
                              start=True, stop=True).then_inc(s_q1, 1)
                    bank7_read = (s_q1l, c + 1)
                elif what[0] == "rc":
                    x_recip_rows(what[1], what[2], 7)
                    bank7_read = (s_rcS, 4 * what[1] + what[2] + 1)
                elif what[0] == "R":
                    x_recip_spread(what[1], what[2], 7)
                    bank7_read = (s_on, 4 * what[1] + what[2] + 1)
                elif what[0] == "x2T":
                    f_x2T(0, 7)
                    bank7_read = (g["x2Tsb"], 1)
                else:
                    f_qkv(0, 7)
                    bank7_read = (g["h"], 2)

            def x_output(b, bk):
                pe.wait_ge(s_on, 4 * (b + 1))
                pe.wait_ge(s_ldo, 16)
                for i in range(2):
                    for c in range(NP):
                        last = pe.matmul(bank(bk, P * i, P * i + P), ot[:, S * c + P * i:S * c + P * i + P],
                                         xout_w[:, D * c:D * c + D], start=(c == 0 and i == 0),
                                         stop=(c == NP - 1), skip_group_check=True)
                last.then_inc(s_xo, 1)

            for s in range(NS):
                x_scores(s)
                if s == 0:
                    for n in range(len(LCH) - 4, len(LCH)):
                        lat_chunk(n)
                if s > 0:
                    x_transposes(s - 1)
                if s == 18:
                    x_output(0, 7)
                    bank7_read = (s_xadd, 1)
                if s > 1:
                    x_values(s - 2)
            x_transposes(NS - 1)
            x_recip_rows(1, 3, 0)
            x_values(NS - 2)
            x_recip_spread(1, 3, 1)
            x_values(NS - 1)

            def f_T(b, src, bk, s_done):
                for i in range(2):
                    t = 2 * b + i
                    last = pe.transpose(bank(bk, P * i, P * i + P), src[:, P * t:P * t + P], ident[:, :])
                last.then_inc(s_done, 1)

            def f_mm(b, lhs, w, n, bk, s_done):
                for i in range(2):
                    t = 2 * b + i
                    last = pe.matmul(bank(bk, n * i, n * i + n), lhs[:, P * t:P * t + P], w,
                                     start=(i == 0), stop=True, skip_group_check=True)
                last.then_inc(s_done, 1)

            def f_OtT(b):
                pe.wait_ge(a2.s_O, 2 * b + 2)
                if b == 0:
                    pe.wait_ge(g["x2Tsb"], 2)
                else:
                    pe.wait_ge(g["mkTs"], 2)
                f_T(b, a2.otok, 6, g["OtT"])

            def f_gate(b):
                pe.wait_ge(g["ott"], b + 1)
                if b == 0:
                    pe.wait_ge(g["h"], 4)
                else:
                    pe.wait_ge(g["lgr"], 1)
                f_mm(b, a2.ott, wG[:, G_WG:G_WG + P], P, 7, g["gl"])

            def f_gT(b):
                pe.wait_ge(g["gated"], b + 1)
                f_T(b, a2.otok, 6, g["gT"])

            def f_wo(b):
                pe.wait_ge(g["gTs"], b + 1)
                f_mm(b, fT, wG[:, G_WO:G_WO + P], P, 7, g["wo"])

            def f_h2T(b):
                pe.wait_ge(g["h2"], 2 * b + 2)
                f_T(b, h2, 6, g["h2T"])

            def f_logits(b):
                pe.wait_ge(g["h2Ts"], b + 1)
                f_mm(b, h2T, wG[:, G_WR:G_WR + NE], NE, 7, g["lg"])

            def f_mkT(b):
                pe.wait_ge(g["mk"], b + 1)
                for i in range(2):
                    t = 2 * b + i
                    last = pe.transpose(ps[0:NE, 6, P * i:P * i + P], mk[:, NE * t:NE * t + NE], ident[:, :])
                last.then_inc(g["mkT"], 1)

            def f_spread(b, j):
                bk = (2 if b == 0 else 6) + j % 2
                if j == 0:
                    pe.wait_ge(g["mkTs"], 2 * b + 2)
                    if b == 0:
                        pe.wait_ge(a2.s_E, 12)
                    else:
                        pe.wait_ge(g["lgr"], 2)
                if j >= 2:
                    pe.wait_ge(g["mb"], 4 * b + j - 1)
                for ee in range(2):
                    e = 2 * j + ee
                    last = pe.matmul(bank(bk, S * ee, S * ee + S), idR[0:NE, e:e + 1].to_broadcast([NE, P]),
                                     mkR[0:NE, S * b:S * b + S], start=(ee == 0), stop=True,
                                     skip_group_check=True)
                last.then_inc(g["bc"], 1)

            def experts_u(e, t):
                b, i = t // 2, t % 2
                pe.wait_ge(g["xm"], 4 * b + e // 2 + 1)
                pe.wait_ge(g["xml"], 4 * b + e // 2 + 1)
                if e == 0 and b == 1:
                    pe.wait_ge(g["acTl"], 2)
                xx = slice(S * e + P * i, S * e + P * i + P)
                ww = slice(512 * e, 512 * e + 512)
                pe.matmul(bank(t), xmh[b][:, xx], w1h[:, ww], start=(e == 0), stop=False)
                pe.matmul(bank(t), xmh[b][:, xx], w1l[:, ww], start=False, stop=False)
                pe.matmul(bank(t), xml[b][:, xx], w1h[:, ww], start=False, stop=False)

            def bias_u(t):
                pe.wait_ge(g["be"], 2)
                tt = slice(P * t, P * t + P)
                pe.matmul(bank(t), mkR[0:NE, tt], beh[0:NE, :], start=False, stop=False)
                pe.matmul(bank(t), mkR[0:NE, tt], bel[0:NE, :], start=False, stop=True).then_inc(g["u"], 1)

            def f_b2(b):
                if b == 0:
                    pe.wait_ge(a2.s_O, 4)
                else:
                    pe.wait_ge(g["yr"], 2)
                f_mm(b, mkT[0:NE, :], wbe[0:NE, 512:640], P, 5, g["b2"])

            def act_T(t):
                pe.wait_ge(g["act"], t + 1)
                bk = (2 if t < 2 else 6) + t % 2
                if t >= 2:
                    pe.wait_ge(g["mb"], 8)
                for k in range(2):
                    last = pe.transpose(bank(bk, P * k, P * k + P),
                                        actf[:, HID * t + P * k:HID * t + P * k + P], ident[:, :])
                last.then_inc(g["actT"], 1)

            def experts_y(t, halves=(0, 1)):
                pe.wait_ge(g["acTl"], t + 1)
                if t % 2 == 0:
                    pe.wait_ge(g["b2r"], t // 2 + 1)
                if t == 1:
                    pe.wait_ge(g["act"], 2)
                if t >= 2:
                    pe.wait_ge(g["yr"], 2 * (t - 1))
                for half in halves:
                    n = 0
                    for k in range(2):
                        a0 = slice(HID * t + P * k, HID * t + P * k + P)
                        w0 = slice(1024 * k + 512 * half, 1024 * k + 512 * half + 512)
                        for aa, ww in ((acTh, w2h), (acTh, w2l), (acTl, w2h)):
                            last = pe.matmul(bank(4 - 4 * (t % 2) + half), aa[:, a0], ww[:, w0],
                                             start=(n == 0), stop=(n == 5))
                            n += 1
                    last.then_inc(g["y"], 1)

            pe_stacks(pe, a2, 0, 4, 6)
            x_output(1, 7)
            pe_scores_shared(pe, a2, 0)
            pe_scores_shared(pe, a2, 1)
            pe.wait_ge(a2.s_k_ev, 4)
            f_x2T(1, 6)
            pe_scores_shared(pe, a2, 2)
            pe.wait_ge(s_xadd, 2)
            f_qkv(1, 7)
            pe_maxrows(pe, a2, 0, 4)
            pe_scoresT_shared(pe, a2, 0)
            pe_scoresT_shared(pe, a2, 1)
            pe_scoresT_shared(pe, a2, 2)
            pe.wait_ge(a2.s_E, 6)
            pe_stacks(pe, a2, 1, 0, 2)
            pe_values(pe, a2, 0, 0)
            pe_scores_shared(pe, a2, 3)
            pe_values(pe, a2, 0, 1)
            pe_scores_shared(pe, a2, 4)
            pe_untranspose(pe, a2, 0)
            pe_scores_shared(pe, a2, 5)
            f_OtT(0)
            f_gate(0)
            pe_maxrows(pe, a2, 1, 4)
            pe_scoresT_shared(pe, a2, 3)
            f_gT(0)
            pe_scoresT_shared(pe, a2, 4)
            f_wo(0)
            pe_scoresT_shared(pe, a2, 5)
            f_h2T(0)
            pe_values(pe, a2, 1, 0)
            f_logits(0)
            pe_values(pe, a2, 1, 1)
            f_mkT(0)
            f_spread(0, 0)
            f_spread(0, 1)
            pe_untranspose(pe, a2, 1)
            for e in range(2):
                experts_u(e, 0)
                experts_u(e, 1)
            f_spread(0, 2)
            f_OtT(1)
            for e in range(2, 4):
                experts_u(e, 0)
                experts_u(e, 1)
            f_spread(0, 3)
            f_gate(1)
            for t in range(2):
                for e in range(4, NE):
                    experts_u(e, t)
                bias_u(t)
            f_gT(1)
            f_b2(0)
            f_wo(1)
            act_T(0)
            experts_y(0, (0,))
            f_h2T(1)
            experts_y(0, (1,))
            f_logits(1)
            act_T(1)
            f_mkT(1)
            experts_y(1, (0,))
            for j in range(2):
                f_spread(1, j)
            experts_y(1, (1,))
            for j in range(4):
                for e in range(2 * j, 2 * j + 2):
                    experts_u(e, 2)
                if j < 2:
                    f_spread(1, j + 2)
            bias_u(2)
            f_b2(1)
            for e in range(NE):
                experts_u(e, 3)
                if e == 5:
                    act_T(2)
            bias_u(3)
            experts_y(2)
            act_T(3)
            experts_y(3)

        @block.scalar
        def _(act):
            A = nc.scalar
            n_ac = [0]

            def link(ins):
                n_ac[0] += 1
                ins.then_inc(s_ac, 1)
                act.wait_ge(s_ac, n_ac[0])

            act.dma_start(cols[:, :], d_cols).then_inc(s_ldc, 16)
            act.dma_start(wkv[:, 0:1024], d_wkv[:, 0:1024]).then_inc(s_ldk, 16)
            act.dma_start(xs[:, :], d_x).then_inc(s_ldx, 16)
            A.preload_act_table_set("natural_log_exp_and_others")

            def rstd(out, var, scale, eps):
                link(A.activation(out, var, ACT.Ln, bias=eps, scale=scale))
                return A.activation(out, out, ACT.Exp, scale=-0.5)

            mv = st[:, 0:32].rearrange("p (t c) -> p t c", c=2)
            e5 = cols[:, C_E5:C_E5 + 1]
            e6 = cols[:, C_E6:C_E6 + 1]
            act.wait_ge(s_ldc, 32)
            hv = a1.h[:, :].rearrange("p (n c d) -> p n c d", c=3, d=HD)
            qs = a1.qs[:, :].rearrange("p (n r d) -> p n r d", r=4, d=HD)
            ks = a1.ks[:, :].rearrange("p (n r d) -> p n r d", r=4, d=HD)

            def sa_hi(b):
                act.wait_ge(s_h, 2 * b + 2)
                m = slice(32 * b, 32 * b + 32)
                A.activation(qs[:, m, 0, :].bitcast(R), hv[:, m, 0, :], ACT.Copy,
                             scale=HD ** -0.5).then_inc(s_kev, 1)
                A.activation(ks[:, m, 0, :].bitcast(R), hv[:, m, 1, :], ACT.Copy).then_inc(s_kev, 1)

            def ctx_rstd(b):
                act.wait_ge(s_cst, b + 1)
                rstd(st[:, 32 + 4 * b:36 + 4 * b], mv[:, 4 * b:4 * b + 4, 1], 1.0, e5).then_inc(s_crs, 1)

            def sa_qst(b):
                act.wait_ge(a1.s_T, 16 * b + 8)
                A.activation(a1.qst[:, :].rearrange("p (g t) -> p g t", g=4)[:, :, 256 * b:256 * b + 256],
                             ps[:, 4 * b:4 * b + 2, :].rearrange("p a (g t) -> p (a g) t", g=2),
                             ACT.Copy).then_inc(a1.s_q_ev, 1)

            sa_hi(0)
            act.wait_ge(s_ldv, 16)
            A.activation(wkvh[:, 1024:2048], wkv[:, 1024:2048], ACT.Copy).then_inc(s_vhi, 1)
            sa_hi(1)
            sa_qst(0)
            ctx_rstd(0)
            ctx_rstd(1)
            sa_qst(1)
            for b in range(B):
                act.wait_ge(s_cT, b + 1)
                A.activation(cTh[:, SC * b:SC * b + SC], bank(4 + b), ACT.Identity, bias=cols[:, C_B1:C_B1 + 1],
                             scale=cols[:, C_G1:C_G1 + 1]).then_inc(s_cTh, 1)
            act.wait_ge(s_ldk, 16)
            A.activation(wkvh[:, 0:1024], wkv[:, 0:1024], ACT.Copy).then_inc(s_khi, 1)
            act.wait_ge(s_zero, 3)
            A.activation(a1.vp[:, :].rearrange("p (n c) -> p n c", c=32)[:, :, 0:HD], hv[:, :, 2, :],
                         ACT.Copy).then_inc(a1.s_vp, 1)
            for n in range(16):
                t, half = n // 2, n % 2
                act.wait_ge(s_vch, n + 1)
                A.activation(vc[:, 1024 * t + 512 * half:1024 * t + 512 * half + 512], bank(4 + n % 4),
                             ACT.Copy).then_inc(s_vev, 1)
            act_maxrows(act, a1, 0, 4)
            act_maxrows(act, a1, 1, 6)

            kn = 0

            def k_hi(m):
                nonlocal kn
                for _ in range(m):
                    c, b = kn // 2, kn % 2
                    act.wait_ge(s_kch, kn + 1)
                    A.activation(kch[:, (b * NP + c) * SC:(b * NP + c + 1) * SC], bank(6 + kn % 2),
                                 ACT.Copy).then_inc(s_khi, 1)
                    kn += 1

            act.wait_ge(s_vch, 16)
            for r in range(5):
                if r == 2:
                    act.wait_ge(a1.s_vp, 1)
                act_exp(act, a1, r)
                k_hi(2 if r < 4 else 1)

            def o_copy(b, bk):
                act.wait_ge(s_OtT, b + 1)
                A.activation(a1.ott[:, S * b:S * b + S], bank(bk, 0, S), ACT.Copy).then_inc(s_ott, 1)

            def ln_rstd(k, t0=0, t1=NT):
                act.wait_ge(s_st, k + 1)
                rstd(st[:, 32 + t0:32 + t1], mv[:, t0:t1, 1], 1.0, e5).then_inc(s_rs, 1)

            def ln_gain(b, bk):
                act.wait_ge(s_lnT, b + 1)
                return A.activation(lnT[:, S * b:S * b + S], bank(bk, 0, S), ACT.Identity,
                                    bias=cols[:, C_B2:C_B2 + 1], scale=cols[:, C_G2:C_G2 + 1])

            def lat_read(n):
                kind, c = LCH[n]
                if kind == "v" and c // 2 % 2 == 1:
                    return
                act.wait_ge(s_lch, n + 1)
                bk = lat_bank(n)
                if kind == "q":
                    if c == 1:
                        act.wait_ge(s_OtT, 2)
                    if c == 3:
                        act.wait_ge(s_pj, 2)
                    A.activation(qh[:, S * c:S * c + S], bank(bk, 0, S), ACT.Copy, scale=XD ** -0.5).then_inc(s_lhi, 1)
                elif kind == "k":
                    A.activation(klh[:, :].rearrange("p (b c t) -> p b c t", b=B, c=NP)[:, :, c, :],
                                 bank(bk).rearrange("p (b t) -> p b t", b=B), ACT.Copy).then_inc(s_lhi, 1)
                else:
                    t, half = c // 2, c % 2
                    if t % 2 == 0:
                        A.activation(vl[:, 1024 * t + 512 * half:1024 * t + 512 * half + 512], bank(bk),
                                     ACT.Copy).then_inc(s_lhi, 1)

            k_hi(1)
            o_copy(0, 4)
            k_hi(1)
            ln_rstd(0, 0, 2)
            act_exp(act, a1, 5)
            ln_rstd(1, 0, 2)
            k_hi(1)
            ln_gain(0, 3).then_inc(s_lnTs, 1)
            k_hi(1)
            lat_read(0)
            lat_read(1)
            o_copy(1, 0)
            lat_read(2)
            lat_read(3)
            k_hi(1)
            ln_rstd(2, 2, 4)
            lat_read(4)
            lat_read(5)
            k_hi(1)
            lat_read(6)
            ln_rstd(3, 2, 4)
            k_hi(1)
            act.wait_ge(s_kch, 16)
            A.activation(lnTh[:, 0:S], lnT[:, 0:S], ACT.Copy).then_inc(s_lnTs, 1)
            link(ln_gain(1, 2))
            act.wait_ge(s_lnTs, 3)
            A.activation(lnTh[:, S:2 * S], lnT[:, S:2 * S], ACT.Copy).then_inc(s_lnTs, 1)

            def x_exp(s, heads=(0, 1)):
                for u in heads:
                    b, c, i = STEPS[s]
                    k = 32 * b + 16 * i + 2 * c + u
                    slot = (2 * s + u) % 4
                    act.wait_ge(s_mx, 2 * s + u + 1)
                    if s <= 1:
                        act.wait_ge(s_lch, (16, 20, 24, 24)[2 * s + u])
                    if s >= 2:
                        act.wait_ge(s_tr, 3 * (s - 1))
                    A.activation(pr[:, slot * 768:slot * 768 + 768],
                                 ps[:, 2 * u:2 * u + 2, :].rearrange("p a b -> p (a b)")[:, 0:768],
                                 ACT.Exp, bias=negmax[:, (2 * s + u) % 8:(2 * s + u) % 8 + 1],
                                 accum_out=psums[:, k:k + 1]).then_inc(s_ex, 1)

            def x_copy(s):
                act.wait_ge(s_tr, 3 * s + 2)
                if s >= 2:
                    act.wait_ge(s_pv, s - 1)
                p0 = (s % 2) * 1536 + 512
                A.activation(pT[:, p0:p0 + 512], bank(5), ACT.Copy).then_inc(s_cpA, 1)

            def act_recip_rows(b, n, bk):
                act.wait_ge(s_rcT, 4 * b + n + 1)
                A.activation(recT[0:4, :], ps[0:4, bk, 0:256], ACT.Copy).then_inc(s_rcS, 1)

            def x_slot(s):
                what = SLOT.get(s, ("",))
                if what[0] == "q":
                    c = what[1]
                    act.wait_ge(s_S, 4 * c + 4)
                    act.wait_ge(s_q1, c + 1)
                    A.activation(qh[:, S * c:S * c + S], bank(7, 0, S), ACT.Copy,
                                 scale=XD ** -0.5).then_inc(s_q1h, 1)
                elif what[0] == "x2T":
                    f_x2T(0, 7)
                elif what[0] == "rc":
                    if 4 * what[1] + what[2] > 0:
                        act.wait_ge(s_R, 4 * what[1] + what[2])
                    act_recip_rows(what[1], what[2], 7)

            g = s_g

            def squares(b, x, scratch):
                for i in range(2):
                    t = 2 * b + i
                    last = A.activation(scratch[:, P * i:P * i + P], x[:, P * t:P * t + P], ACT.Square,
                                        accum_out=st[:, 36 + t:37 + t])
                link(last)

            def f_rms(b):
                act.wait_ge(s_xn, 2 * NT + 2 * b + 2)
                squares(b, xs, rq[:, 320 * b:320 * b + 256])
                rstd(st[:, 40 + 2 * b:42 + 2 * b], st[:, 36 + 2 * b:38 + 2 * b], 1.0 / D, e6).then_inc(g["rstd"], 1)

            def f_x2T(b, bk):
                act.wait_ge(g["x2T"], b + 1)
                act.wait_ge(s_w2l, 4)
                A.activation(x2T[:, S * b:S * b + S], bank(bk, 0, S), ACT.Copy,
                             scale=cols[:, C_L1:C_L1 + 1]).then_inc(g["x2Tsb"], 1)

            def f_head_squares(b):
                act.wait_ge(g["rot"], b + 1)
                w = slice(320 * b, 320 * b + 320)
                A.activation(rq[:, w], rp[:, w], ACT.Square).then_inc(g["hsq"], 1)

            def f_head_rms(b):
                act.wait_ge(g["sq"], b + 1)
                rstd(rq[:, 320 * b:320 * b + 40], rq[:, 320 * b + 40:320 * b + 80], 1.0 / HD,
                     e6).then_inc(g["rms"], 1)

            hq = rp[:, :].rearrange("p (t n d) -> p t n d", t=NT, n=20)
            qs2 = a2.qs[:, :].rearrange("p (t n r d) -> p t n r d", t=NT, n=16, r=4)
            ks2 = a2.ks[:, :].rearrange("p (t n r d) -> p t n r d", t=NT, n=4, r=4)

            def f_hi(b):
                act.wait_ge(g["ss"], b + 1)
                m = slice(2 * b, 2 * b + 2)
                A.activation(qs2[:, m, :, 0, :].bitcast(R), hq[:, m, 0:16, :], ACT.Copy,
                             scale=HD ** -0.5).then_inc(g["hi"], 1)
                A.activation(ks2[:, m, :, 0, :].bitcast(R), hq[:, m, 16:20, :], ACT.Copy).then_inc(g["hi"], 1)
                act.wait_ge(s_zero, 6)
                A.activation(a2.vp[:, :].rearrange("p (t n c) -> p t n c", t=NT, c=32)[:, m, :, 0:HD],
                             a2.h[:, :].rearrange("p (t n d) -> p t n d", t=NT, d=HD)[:, m, 20:24, :],
                             ACT.Copy).then_inc(a2.s_vp, 1)

            def f_qst(b, bk):
                act.wait_ge(a2.s_T, 10 * b + 8)
                A.activation(a2.qst[:, :].rearrange("p (g t) -> p g t", g=4)[:, :, 256 * b:256 * b + 256],
                             ps[:, bk:bk + 2, :].rearrange("p a (g t) -> p (a g) t", g=2),
                             ACT.Copy).then_inc(a2.s_q_ev, 1)
                act.wait_ge(a2.s_T, 10 * b + 10)
                act.wait_ge(s_zero, 7)
                for j in range(4):
                    s = slice(32 * j, 32 * j + 32)
                    k0 = 1024 * b + 256 * j
                    A.activation(a2.kst[s, k0:k0 + 256], ps[s, bk + 2, 0:256], ACT.Copy).then_inc(a2.s_k_ev, 1)

            def f_copy(b, s_in, dst, bk, s_out, **kw):
                act.wait_ge(s_in, b + 1)
                return A.activation(dst[:, S * b:S * b + S], bank(bk, 0, S), ACT.Copy, **kw).then_inc(s_out, 1)

            def f_gate(b):
                act.wait_ge(g["gpre"], b + 1)
                A.activation(gat[:, S * b:S * b + S], gat[:, S * b:S * b + S], ACT.Exp,
                             scale=-1.0).then_inc(g["e"], 1)

            def f_rms3(b):
                act.wait_ge(g["x3"], b + 1)
                squares(b, x3, gat[:, S * b:S * b + S])
                rstd(st[:, 84 + 2 * b:86 + 2 * b], st[:, 36 + 2 * b:38 + 2 * b], 1.0 / D,
                     e6).then_inc(g["rstd3"], 1)

            def f_h2T(b):
                act.wait_ge(g["h2T"], b + 1)
                link(A.activation(h2T[:, S * b:S * b + S], bank(6, 0, S), ACT.Copy, scale=cols[:, C_L2:C_L2 + 1]))
                A.activation(h2h[:, S * b:S * b + S], h2T[:, S * b:S * b + S], ACT.Copy).then_inc(g["h2Ts"], 1)

            def f_mkT(b):
                act.wait_ge(g["mkT"], b + 1)
                A.activation(mkR[0:NE, S * b:S * b + S], ps[0:NE, 6, 0:S], ACT.Copy).then_inc(g["mkTs"], 1)
                A.activation(mkT[0:NE, S * b:S * b + S], ps[0:NE, 6, 0:S], ACT.Copy).then_inc(g["mkTs"], 1)

            def gate_u(t):
                act.wait_ge(g["u"], t + 1)
                A.activation(sg[:, HID * t:HID * t + HID], bank(t, 256, 512), ACT.Exp, scale=-1.0).then_inc(g["eu"], 1)

            def act_hi(t):
                act.wait_ge(g["actT"], t + 1)
                A.activation(acTh[:, HID * t:HID * t + HID], bank((2 if t < 2 else 6) + t % 2, 0, 256),
                             ACT.Copy).then_inc(g["acTh"], 1)

            def mask_rows(b, j):
                act.wait_ge(g["bc"], 4 * b + j + 1)
                if 4 * b + j >= 2:
                    act.wait_ge(g["xm"], 4 * b + j - 1)
                    act.wait_ge(g["xml"], 4 * b + j - 1)
                A.activation(mkB[:, 512 * (j % 2):512 * (j % 2) + 512], bank((2 if b == 0 else 6) + j % 2),
                             ACT.Copy).then_inc(g["mb"], 1)

            def mask_y(t, halves):
                if t >= 2:
                    act.wait_ge(g["sum"], t - 1)
                for e in (e for e in range(NE) if e // 4 in halves):
                    if e % 4 == 0:
                        act.wait_ge(g["y"], 2 * t + e // 4 + 1)
                    k = 1024 * (t % 2) + P * e
                    last = A.activation(prod[:, k:k + P], bank(4 - 4 * (t % 2) + e // 4, P * (e % 4), P * (e % 4) + P),
                                        ACT.Copy, scale=mk[:, NE * t + e:NE * t + e + 1])
                    if e % 4 == 3:
                        last.then_inc(g["yr"], 1)

            for n in range(7, len(LCH) - 3):
                lat_read(n)
            x_exp(0, (0,))
            for n in range(len(LCH) - 3, len(LCH)):
                lat_read(n)
            x_exp(0, (1,))
            for s in range(1, NS):
                x_slot(s)
                x_exp(s)
                x_copy(s - 1)
                if s == 19:
                    ln_rstd(4, 0, 2)
                if s == 27:
                    act.wait_ge(s_w1l, NE)
                    f_rms(0)
                if s == 28:
                    f_head_squares(0)
                if s == 29:
                    f_head_rms(0)
                if s == 30:
                    f_hi(0)
            x_copy(NS - 1)
            act_recip_rows(1, 3, 0)
            f_qst(0, 4)
            ln_rstd(5, 2, 4)
            f_rms(1)
            f_x2T(1, 6)
            act_maxrows(act, a2, 0, 4)
            act_exp(act, a2, 0)
            f_head_squares(1)
            f_head_rms(1)
            act_exp(act, a2, 1)
            f_hi(1)
            act_exp(act, a2, 2)
            f_qst(1, 0)
            f_copy(0, g["OtT"], a2.ott, 6, g["ott"])
            act_maxrows(act, a2, 1, 4)
            f_gate(0)
            act_exp(act, a2, 3)
            f_copy(0, g["gT"], fT, 6, g["gTs"])
            act_exp(act, a2, 4)
            f_rms3(0)
            act_exp(act, a2, 5)
            f_h2T(0)
            act.wait_ge(s_ldb, 16)
            A.activation(beh[0:NE, :], wbe[0:NE, 0:512], ACT.Copy).then_inc(g["be"], 1)
            f_mkT(0)
            for j in range(3):
                mask_rows(0, j)
            f_copy(1, g["OtT"], a2.ott, 6, g["ott"])
            mask_rows(0, 3)
            f_gate(1)
            gate_u(0)
            gate_u(1)
            f_copy(1, g["gT"], fT, 6, g["gTs"])
            act_hi(0)
            f_rms3(1)
            f_h2T(1)
            mask_y(0, (0, 1))
            act_hi(1)
            f_mkT(1)
            mask_rows(1, 0)
            mask_rows(1, 1)
            mask_y(1, (0,))
            mask_rows(1, 2)
            mask_y(1, (1,))
            mask_rows(1, 3)
            ln_rstd(6, 0, 2)
            gate_u(2)
            act_hi(2)
            gate_u(3)
            mask_y(2, (0,))
            act_hi(3)
            mask_y(2, (1,))
            ln_rstd(7, 2, 4)

        @block.vector
        def _(dve):
            V = nc.vector
            n_dv = [0]

            def v(ins):
                n_dv[0] += 1
                ins.then_inc(s_dv, 1)
                return n_dv[0]

            def need(n):
                dve.wait_ge(s_dv, n)

            mv = st[:, 0:32].rearrange("p (t c) -> p t c", c=2)
            bn = bnst

            def stats(src, tiles, s_done, raw):
                need(n_dv[0])
                for k, t in enumerate(tiles):
                    n = v(V.bn_stats(bn[:, 6 * k:6 * k + 6], src[:, P * t:P * t + P]))
                for k, t in enumerate(tiles):
                    need(n - len(tiles) + 1 + k)
                    last = V.bn_aggr(raw[:, t, :], bn[:, 6 * k:6 * k + 6])
                    if k < len(tiles) - 1:
                        v(last)
                last.then_inc(s_done, 1)

            def ctx_stats(b):
                if b > 0:
                    dve.wait_ge(s_cst, b)
                stats(cx, range(4 * b, 4 * b + 4), s_cst, mv)

            def ctx_low(b):
                dve.wait_ge(s_cTh, b + 1)
                if b == 1:
                    dve.wait_ge(s_cTl, 1)
                n = v(V.tensor_scalar(cX[:, :], bank(4 + b), cols[:, C_G1:C_G1 + 1], cols[:, C_B1:C_B1 + 1],
                                      ALU.mult, ALU.add))
                need(n)
                V.tensor_tensor(cTl[:, SC * b:SC * b + SC], cX[:, :], cTh[:, SC * b:SC * b + SC].bitcast(F),
                                ALU.subtract).then_inc(s_cTl, 1)

            hv = a1.h[:, :].rearrange("p (n c d) -> p n c d", c=3, d=HD)
            qs = a1.qs[:, :].rearrange("p (n r d) -> p n r d", r=4, d=HD)
            ks = a1.ks[:, :].rearrange("p (n r d) -> p n r d", r=4, d=HD)

            def sa_h(t):
                dve.wait_ge(s_qkv, t + 1)
                V.tensor_tensor(a1.h[:, 384 * t:384 * t + 384], bank(4 + t, 0, 384), wA[:, A_B1:A_B1 + 384],
                                ALU.add).then_inc(s_h, 1)

            def sa_low(b):
                m = slice(32 * b, 32 * b + 32)
                dve.wait_ge(s_kev, 2 * b + 1)
                dve.wait_ge(s_h, 2 * b + 2)
                n = v(V.scalar_tensor_tensor(out=qs[:, m, 1, :], in0=hv[:, m, 0, :], scalar=HD ** -0.5,
                                             in1=qs[:, m, 0, :], op0=ALU.mult, op1=ALU.subtract))
                dve.wait_ge(s_kev, 2 * b + 2)
                n2 = v(V.tensor_tensor(ks[:, m, 2, :], hv[:, m, 1, :], ks[:, m, 0, :], ALU.subtract))
                need(n)
                V.tensor_copy(qs[:, m, 2, :], qs[:, m, 0, :]).then_inc(a1.s_qsplit, 1)
                need(n2)
                V.tensor_copy(ks[:, m, 1, :], ks[:, m, 0, :]).then_inc(a1.s_ksplit, 1)

            dve.wait_ge(s_ldA, 16)
            sa_h(0)
            dve.wait_ge(s_const, 3)
            V.tensor_copy(cR[:, 0:P], ident[:, :]).then_inc(s_constR, 1)
            V.tensor_copy(cR[:, P:3 * P], cS[:, :]).then_inc(s_constR, 1)
            sa_h(1)
            sa_low(0)
            sa_h(2)
            sa_h(3)
            sa_low(1)

            def k_stack_ev(a, b, bk):
                kg = a.kg
                dve.wait_ge(a.s_T, (8 + 2 * kg) * (b + 1))
                V.tensor_copy(a.kst[:, :].rearrange("p (g t) -> p g t", g=kg)[:, :, 256 * b:256 * b + 256],
                              ps[:, bk:bk + 2, :].rearrange("p a (g t) -> p (a g) t", g=2)).then_inc(a.s_k_ev, 1)

            dve.wait_ge(s_ldc, 32)
            ctx_stats(0)
            k_stack_ev(a1, 0, 2)
            ctx_stats(1)
            k_stack_ev(a1, 1, 6)
            for r in range(6):
                dve_max(dve, a1, r, v, need)
                if r == 1:
                    ctx_low(0)
                    ctx_low(1)
            dve_maxrows(dve, a1, 0, 4)
            dve_maxrows(dve, a1, 1, 6)

            kn = 0

            def k_lo(m):
                nonlocal kn
                for _ in range(m):
                    c, b = kn // 2, kn % 2
                    dve.wait_ge(s_khi, kn + 2)
                    kk = slice((b * NP + c) * SC, (b * NP + c + 1) * SC)
                    V.tensor_tensor(kcl[:, kk], bank(6 + kn % 2), kch[:, kk].bitcast(F),
                                    ALU.subtract).then_inc(s_kdn, 1)
                    kn += 1

            def ots(a, b, half):
                dve.wait_ge(a.s_PV, 2 * b + half + 1)
                if b > 0:
                    dve.wait_ge(a.s_OT, 2 * b)
                V.tensor_copy(a.ots[:, 512 * half:512 * half + 512], bank(4 + half)).then_inc(a.s_ots, 1)

            dve.wait_ge(s_ldx, 16)
            n_xb = v(V.tensor_tensor(xs[:, :].rearrange("p (t d) -> p t d", t=NT),
                                  xs[:, :].rearrange("p (t d) -> p t d", t=NT),
                                  wA[:, A_BP:A_BP + P].unsqueeze(1).to_broadcast([P, NT, P]), ALU.add))
            k_lo(6)
            ots(a1, 0, 0)
            ots(a1, 0, 1)
            k_lo(2)
            dve_norm(dve, a1, 0, v, need)
            def ln_stats(k, src, t0=0, t1=NT):
                dve.wait_ge(s_st, k) if k else dve.wait_ge(s_cst, 2)
                stats(src, range(t0, t1), s_st, mv)

            def ln_apply(k, src, dst, s_done, t0=0, t1=NT):
                dve.wait_ge(s_rs, k + 1)
                for t in range(t0, t1):
                    V.tensor_scalar(dst[:, P * t:P * t + P], src[:, P * t:P * t + P], mv[:, t, 0:1],
                                    st[:, 32 + t:33 + t], ALU.subtract, ALU.mult).then_inc(s_done, 1)

            def x_plus_attention(b, bk):
                dve.wait_ge(s_pj, b + 1)
                n = v(V.tensor_tensor(xs[:, S * b:S * b + S], bank(bk, 0, S), xs[:, S * b:S * b + S], ALU.add))
                need(n)

            def lat_low(n):
                kind, c = LCH[n]
                bk = lat_bank(n)
                if kind == "v":
                    t, half = c // 2, c % 2
                    if t % 2 == 1:
                        dve.wait_ge(s_lch, n + 1)
                        V.tensor_copy(vl[:, 1024 * t + 512 * half:1024 * t + 512 * half + 512],
                                      bank(bk)).then_inc(s_llo, 1)
                    return
                dve.wait_ge(s_lhi, n + 1)
                if kind == "q":
                    if c == 7:
                        dve.wait_ge(s_lnT, 2)
                    V.scalar_tensor_tensor(out=ql[:, S * c:S * c + S], in0=bank(bk, 0, S), scalar=XD ** -0.5,
                                           in1=qh[:, S * c:S * c + S].bitcast(F), op0=ALU.mult,
                                           op1=ALU.subtract).then_inc(s_llo, 1)
                else:
                    vv = lambda z: z[:, :].rearrange("p (b c t) -> p b c t", b=B, c=NP)[:, :, c, :]
                    V.tensor_tensor(vv(kll), bank(bk).rearrange("p (b t) -> p b t", b=B), vv(klh).bitcast(F),
                                    ALU.subtract).then_inc(s_llo, 1)

            k_lo(1)
            need(n_xb)
            x_plus_attention(0, 5)
            ln_stats(0, xs, 0, 2)
            k_lo(2)
            ln_apply(0, xs, xs, s_xn, 0, 2)
            dve.wait_ge(s_xn, 2)
            ln_stats(1, xs, 0, 2)
            ots(a1, 1, 0)
            ln_apply(1, xs, ln, s_xn, 0, 2)
            k_lo(1)
            ots(a1, 1, 1)
            dve_norm(dve, a1, 1, v, need)
            lat_low(0)
            lat_low(1)
            k_lo(1)
            x_plus_attention(1, 1)
            ln_stats(2, xs, 2, 4)
            lat_low(2)
            lat_low(3)
            k_lo(1)
            ln_apply(2, xs, xs, s_xn, 2, 4)
            dve.wait_ge(s_xn, 6)
            ln_stats(3, xs, 2, 4)
            lat_low(4)
            lat_low(5)
            ln_apply(3, xs, ln, s_xn, 2, 4)
            k_lo(1)

            def ln_low(b):
                dve.wait_ge(s_lnTs, 2 * b + 2)
                w = slice(S * b, S * b + S)
                V.tensor_tensor(lnTl[:, w], lnT[:, w], lnTh[:, w].bitcast(F), ALU.subtract).then_inc(s_lnTs, 1)

            ln_low(0)
            lat_low(6)
            k_lo(1)
            ln_low(1)

            def x_max(s):
                for u in range(2):
                    dve.wait_ge(s_S, 2 * s + u + 1)
                    if s >= 4:
                        dve.wait_ge(s_ex, 2 * (s - 4) + u + 1)
                    k = (2 * s + u) % 8
                    V.tensor_reduce(negmax[:, k:k + 1],
                                    ps[:, 2 * u:2 * u + 2, :].rearrange("p a b -> p (a b)")[:, 0:768],
                                    X, ALU.max, negate=True).then_inc(s_mx, 1)

            def x_copies(s):
                if s >= 2:
                    dve.wait_ge(s_pv, s - 1)
                for m in (0, 2):
                    dve.wait_ge(s_tr, 3 * s + m + 1)
                    p0 = (s % 2) * 1536 + 512 * m
                    V.tensor_copy(pT[:, p0:p0 + 512], bank(4 + m)).then_inc(s_cpD, 1)

            def x_out(s):
                b, c, i = STEPS[s]
                dve.wait_ge(s_pv, s + 1)
                V.tensor_copy(ot[:, S * c + P * i:S * c + P * i + P], bank(7, 0, P)).then_inc(s_oev, 1)

            def x_recip(b, n):
                dve.wait_ge(s_ex, 2 * (16 * b + 4 * n + 4))
                w = slice(32 * b, 32 * b + 32)
                pick = lambda z: z.rearrange("p (i h) -> p i h", i=2)[:, :, 4 * n:4 * n + 4]
                V.reciprocal(pick(rc[:, w]), pick(psums[:, w])).then_inc(s_rc, 1)

            def x_norm(b, n, bk):
                dve.wait_ge(s_R, 4 * b + n + 1)
                dve.wait_ge(s_oev, 16 * b + 4 * n + 4)
                V.tensor_tensor(ot[:, 512 * n:512 * n + 512], bank(bk), ot[:, 512 * n:512 * n + 512],
                                       ALU.mult).then_inc(s_on, 1)

            def x_add(b, bk):
                dve.wait_ge(s_xo, b + 1)
                V.tensor_tensor(xs[:, S * b:S * b + S], bank(bk, 0, S), xs[:, S * b:S * b + S],
                                ALU.add).then_inc(s_xadd, 1)

            def x_slot(s):
                what = SLOT.get(s, ("",))
                if what[0] == "q":
                    c = what[1]
                    dve.wait_ge(s_q1h, c + 1)
                    V.scalar_tensor_tensor(out=ql[:, S * c:S * c + S], in0=bank(7, 0, S), scalar=XD ** -0.5,
                                           in1=qh[:, S * c:S * c + S].bitcast(F), op0=ALU.mult,
                                           op1=ALU.subtract).then_inc(s_q1l, 1)
                elif what[0] == "R":
                    x_norm(what[1], what[2], 7)
                elif what[0] == "qkv":
                    f_h(0, 7)

            g = s_g

            def f_h(b, bk):
                dve.wait_ge(g["rstd"], b + 1)
                dve.wait_ge(s_ldg, 16)
                dve.wait_ge(g["qkv"], b + 1)
                for i in range(2):
                    t = 2 * b + i
                    V.scalar_tensor_tensor(out=a2.h[:, 192 * t:192 * t + 192], in0=bank(bk, 192 * i, 192 * i + 192),
                                           scalar=st[:, 40 + t:41 + t], in1=wG[:, G_BQKV:G_BQKV + 192],
                                           op0=ALU.mult, op1=ALU.add).then_inc(g["h"], 1)

            hh = a2.h[:, :].rearrange("p (t n d) -> p t n d", t=NT, d=HD)
            rope = wG[:, G_ROPE:G_ROPE + 32].rearrange("p (t k d) -> p t k d", t=2, k=2)
            rpv = rp[:, :].rearrange("p (t n d) -> p t n d", t=NT, d=HD)
            qn = wG[:, G_QN:G_QN + 160]

            def f_rope(b):
                dve.wait_ge(g["h"], 2 * b + 2)
                for i in range(2):
                    t = 2 * b + i
                    n = v(V.tensor_tensor(rpv[:, t, :, :], hh[:, t, 0:20, :],
                                          rope[:, i, 0:1, :].to_broadcast([P, 20, HD]), ALU.mult))
                need(n)
                dve.wait_ge(g["swap"], 4 * b + 4)
                w = slice(320 * b, 320 * b + 320)
                V.tensor_tensor(rp[:, w], rp[:, w], rq[:, w], ALU.add).then_inc(g["rot"], 1)

            def f_squares(b):
                w = slice(320 * b, 320 * b + 320)
                dve.wait_ge(g["hsq"], b + 1)
                ssq = st[:, 44:84]
                n = v(V.tensor_reduce(ssq, rq[:, w].rearrange("p (n d) -> p n d", d=HD), X, ALU.add))
                need(n)
                V.tensor_copy(rq[:, 320 * b + 40:320 * b + 80], ssq).then_inc(g["sq"], 1)

            def f_scale(b):
                w = slice(320 * b, 320 * b + 320)
                dve.wait_ge(g["rms"], b + 1)
                n = v(V.tensor_tensor(rp[:, w].rearrange("p (n d) -> p n d", d=HD),
                                      rp[:, w].rearrange("p (n d) -> p n d", d=HD),
                                      rq[:, 320 * b:320 * b + 40].unsqueeze(2).to_broadcast([P, 40, HD]), ALU.mult))
                need(n)
                V.tensor_tensor(rp[:, w].rearrange("p (t c) -> p t c", t=2),
                                rp[:, w].rearrange("p (t c) -> p t c", t=2),
                                qn.unsqueeze(1).to_broadcast([P, 2, 160]), ALU.mult).then_inc(g["ss"], 1)

            qs2 = a2.qs[:, :].rearrange("p (t n r d) -> p t n r d", t=NT, n=16, r=4)

            def f_low(b):
                m = slice(2 * b, 2 * b + 2)
                dve.wait_ge(g["ss"], b + 1)
                dve.wait_ge(g["hi"], 2 * b + 1)
                n = v(V.scalar_tensor_tensor(out=qs2[:, m, :, 1, :], in0=rpv[:, m, 0:16, :], scalar=HD ** -0.5,
                                             in1=qs2[:, m, :, 0, :], op0=ALU.mult, op1=ALU.subtract))
                need(n)
                q3 = a2.qs[:, 1024 * b:1024 * b + 1024].rearrange("p (n r d) -> p n r d", r=4, d=HD)
                V.tensor_copy(q3[:, :, 2, :], q3[:, :, 0, :]).then_inc(a2.s_qsplit, 1)

            pair = lambda z, b: z[:, S * b:S * b + S].rearrange("p (t d) -> p t d", t=2)
            both = lambda ap: ap.unsqueeze(1).to_broadcast([P, 2, P])

            def f_gate_in(b):
                dve.wait_ge(g["gl"], b + 1)
                V.tensor_tensor(pair(gat, b), bank(7, 0, S).rearrange("p (t d) -> p t d", t=2),
                                both(wG[:, G_BG:G_BG + P]), ALU.add).then_inc(g["gpre"], 1)

            def f_gated(b):
                w = slice(S * b, S * b + S)
                dve.wait_ge(g["e"], b + 1)
                n = v(V.tensor_scalar(gat[:, w], gat[:, w], 1.0, None, ALU.add))
                need(n)
                n = v(V.reciprocal(gat[:, w], gat[:, w]))
                need(n)
                V.tensor_tensor(a2.otok[:, w], a2.otok[:, w], gat[:, w], ALU.mult).then_inc(g["gated"], 1)
                return v(V.tensor_tensor(pair(x3, b), pair(xs, b), both(wG[:, G_BO:G_BO + P]), ALU.add))

            def f_x3(b, n):
                w = slice(S * b, S * b + S)
                need(n)
                dve.wait_ge(g["wo"], b + 1)
                V.tensor_tensor(x3[:, w], bank(7, 0, S), x3[:, w], ALU.add).then_inc(g["x3"], 1)

            def f_h2(b):
                w = slice(S * b, S * b + S)
                dve.wait_ge(g["rstd3"], b + 1)
                for t in (2 * b, 2 * b + 1):
                    V.tensor_scalar(h2[:, P * t:P * t + P], x3[:, P * t:P * t + P], st[:, 84 + t:85 + t], None,
                                    ALU.mult).then_inc(g["h2"], 1)
                v(V.tensor_tensor(xs[:, w], xs[:, w], x3[:, w], ALU.add))

            def f_router(b):
                l3 = lg[:, 16 * b:16 * b + 16].rearrange("p (t e) -> p t e", t=2)
                l4 = lg[:, 32 + 16 * b:48 + 16 * b].rearrange("p (t e) -> p t e", t=2)
                top, pick = st[:, 88 + 2 * b:90 + 2 * b], st[:, 92 + 2 * b:94 + 2 * b]
                dve.wait_ge(g["lg"], b + 1)
                V.tensor_tensor(l3, bank(7, 0, 16).rearrange("p (t e) -> p t e", t=2),
                                wG[:, G_BR:G_BR + NE].unsqueeze(1).to_broadcast([P, 2, NE]), ALU.add
                                ).then_inc(g["lgr"], 1)
                dve.wait_ge(g["lgr"], b + 1)
                n = v(V.tensor_reduce(top, l3, X, ALU.max))
                need(n)
                n = v(V.tensor_tensor(l4, l3, top.unsqueeze(2).to_broadcast([P, 2, NE]), ALU.is_equal))
                need(n)
                n = v(V.tensor_tensor(l3, l4, wG[:, G_RK:G_RK + NE].unsqueeze(1).to_broadcast([P, 2, NE]), ALU.mult))
                need(n)
                n = v(V.tensor_reduce(pick, l3, X, ALU.max))
                need(n)
                V.tensor_tensor(mk[:, 16 * b:16 * b + 16].rearrange("p (t e) -> p t e", t=2), l3,
                                pick.unsqueeze(2).to_broadcast([P, 2, NE]), ALU.is_equal).then_inc(g["mk"], 1)
                w = slice(S * b, S * b + S)
                dve.wait_ge(g["h2Ts"], b + 1)
                V.tensor_tensor(h2l[:, w], h2T[:, w], h2h[:, w].bitcast(F), ALU.subtract).then_inc(g["low"], 1)

            def f_masked(b, j):
                dve.wait_ge(g["mb"], 4 * b + j + 1)
                src = mkB[:, 512 * (j % 2):512 * (j % 2) + 512].rearrange("p (e t) -> p e t", e=2)
                V.tensor_tensor(xmh[b][:, 512 * j:512 * j + 512].rearrange("p (e t) -> p e t", e=2), src,
                                h2h[:, S * b:S * b + S].bitcast(F).unsqueeze(1).to_broadcast([P, 2, S]),
                                ALU.mult).then_inc(g["xm"], 1)

            def gated_u(t):
                w = slice(HID * t, HID * t + HID)
                dve.wait_ge(g["eu"], t + 1)
                n = v(V.tensor_scalar(sg[:, w], sg[:, w], 1.0, None, ALU.add))
                need(n)
                n = v(V.reciprocal(sg[:, w], sg[:, w]))
                need(n)
                V.tensor_tensor(actf[:, w], bank(t, 0, 256), sg[:, w], ALU.mult).then_inc(g["act"], 1)

            def act_low(t):
                w = slice(HID * t, HID * t + HID)
                dve.wait_ge(g["acTh"], t + 1)
                V.tensor_tensor(acTl[:, w], bank((2 if t < 2 else 6) + t % 2, 0, 256), acTh[:, w].bitcast(F),
                                ALU.subtract).then_inc(g["acTl"], 1)

            def f_b2(b):
                w = slice(S * b, S * b + S)
                dve.wait_ge(g["b2"], b + 1)
                V.tensor_tensor(xs[:, w], bank(5, 0, S), xs[:, w], ALU.add).then_inc(g["b2r"], 1)

            def choose(t):
                dve.wait_ge(g["yr"], 2 * t + 2)
                V.tensor_reduce(yv[:, P * t:P * t + P],
                                prod[:, 1024 * (t % 2):1024 * (t % 2) + 1024].rearrange("p (e d) -> p d e", e=NE),
                                X, ALU.add).then_inc(g["sum"], 1)
                dve.wait_ge(g["sum"], t + 1)
                dve.wait_ge(g["b2r"], t // 2 + 1)
                return v(V.tensor_tensor(xs[:, P * t:P * t + P], xs[:, P * t:P * t + P], yv[:, P * t:P * t + P],
                                         ALU.add))

            def choose_last(t, n):
                w = slice(P * t, P * t + P)
                sums = (xs[:, w], yv[:, w])
                done = [n, 0]
                for e in range(NE):
                    if e % 4 == 0:
                        dve.wait_ge(g["y"], 2 * t + e // 4 + 1)
                    src = bank(e // 4, P * (e % 4), P * (e % 4) + P)
                    m = mk[:, NE * t + e:NE * t + e + 1]
                    acc = sums[e % 2]
                    if e == 1:
                        done[1] = v(V.tensor_scalar(acc, src, m, None, ALU.mult))
                    else:
                        need(done[e % 2])
                        done[e % 2] = v(V.scalar_tensor_tensor(out=acc, in0=src, scalar=m, in1=acc,
                                                               op0=ALU.mult, op1=ALU.add))
                need(done[1])
                return v(V.tensor_tensor(sums[0], sums[0], sums[1], ALU.add))

            for n in range(7, len(LCH) - 4):
                lat_low(n)
            for s in range(NS):
                if SLOT.get(s, ("",))[0] == "rc":
                    x_recip(*SLOT[s][1:])
                x_slot(s)
                x_max(s)
                if s == 0:
                    for n in range(len(LCH) - 4, len(LCH)):
                        lat_low(n)
                if s > 0:
                    x_copies(s - 1)
                if s == 18:
                    x_add(0, 7)
                if s > 1:
                    x_out(s - 2)
                if s == 19:
                    dve.wait_ge(s_xadd, 1)
                    ln_stats(4, xs, 0, 2)
                if s == 20:
                    ln_apply(4, xs, xs, s_xn, 0, 2)
                if s == 28:
                    f_rope(0)
                if s == 29:
                    f_squares(0)
                if s == 30:
                    f_scale(0)
                if s == 31:
                    f_low(0)
            x_copies(NS - 1)
            x_recip(1, 3)
            x_out(NS - 2)
            x_out(NS - 1)
            x_norm(1, 3, 1)
            x_add(1, 7)
            dve.wait_ge(s_xadd, 2)
            ln_stats(5, xs, 2, 4)
            dve_max(dve, a2, 0, v, need)
            ln_apply(5, xs, xs, s_xn, 2, 4)
            dve_max(dve, a2, 1, v, need)
            dve_max(dve, a2, 2, v, need)
            dve_maxrows(dve, a2, 0, 4)
            f_h(1, 7)
            f_rope(1)
            f_squares(1)
            f_scale(1)
            f_low(1)
            ots(a2, 0, 0)
            dve_max(dve, a2, 3, v, need)
            ots(a2, 0, 1)
            dve_max(dve, a2, 4, v, need)
            dve_norm(dve, a2, 0, v, need)
            dve_max(dve, a2, 5, v, need)
            dve_maxrows(dve, a2, 1, 4)
            f_gate_in(0)
            n = f_gated(0)
            f_x3(0, n)
            f_h2(0)
            f_router(0)
            ots(a2, 1, 0)
            ots(a2, 1, 1)
            f_masked(0, 0)
            dve_norm(dve, a2, 1, v, need)
            f_masked(0, 1)
            dve.wait_ge(g["be"], 1)
            V.tensor_tensor(bel[0:NE, :], wbe[0:NE, 0:512], beh[0:NE, :].bitcast(F), ALU.subtract).then_inc(g["be"], 1)
            f_masked(0, 2)
            f_masked(0, 3)
            f_gate_in(1)
            n = f_gated(1)
            gated_u(0)
            f_b2(0)
            f_x3(1, n)
            act_low(0)
            f_h2(1)
            gated_u(1)
            f_router(1)
            act_low(1)
            choose(0)
            f_masked(1, 0)
            f_masked(1, 1)
            f_masked(1, 2)
            f_masked(1, 3)
            n = choose(1)
            need(n)
            ln_stats(6, xs, 0, 2)
            gated_u(2)
            f_b2(1)
            ln_apply(6, xs, xs, g["v"], 0, 2)
            act_low(2)
            gated_u(3)
            act_low(3)
            n = choose(2)
            need(n)
            n = v(V.bn_stats(bn[:, 0:6], xs[:, 2 * P:3 * P]))
            need(n)
            n = v(V.bn_aggr(mv[:, 2, :], bn[:, 0:6]))
            n = choose_last(3, n)
            need(n)
            n = v(V.bn_stats(bn[:, 6:12], xs[:, 3 * P:4 * P]))
            need(n)
            V.bn_aggr(mv[:, 3, :], bn[:, 6:12]).then_inc(s_st, 1)
            ln_apply(7, xs, xs, g["v"], 2, 4)


def kernel(**inputs):
    import numpy as np
    import concourse.bacc as bacc
    from concourse import mybir as mb
    from concourse.bass_utils import run_bass_kernel_spmd

    a = {k: np.asarray(v) for k, v in inputs.items()}
    f32 = np.float32

    def rows(v):
        return np.broadcast_to(v.reshape(1, -1), (P, v.size))

    def tiles(m):
        t = m.shape[0] // P
        return m.reshape(t, P, -1).transpose(1, 0, 2).reshape(P, -1)

    x = a["x"].reshape(B * S, D)
    d_a = np.concatenate([x.T, a["L0_attn_W1"], rows(a["L0_attn_b1"]), a["L0_attn_Wp"], rows(a["L0_attn_bp"])], 1)
    def gm(m):
        return m.reshape(-1, KV, H // KV, HD).transpose(0, 2, 1, 3).reshape(m.shape[0], -1)
    wq, bq = gm(a["L0_ffn_Wq"]), gm(a["L0_ffn_bq"].reshape(1, -1))
    wo = gm(a["L0_ffn_Wo"].T).T
    pos = np.arange(S, dtype=f32).reshape(2, P)
    inv = (1.0 / 10000.0 ** (np.arange(0, HD, 2, dtype=f32) / HD)).astype(f32)
    ang = (pos[:, :, None] * inv).astype(f32)
    cos, sin = np.cos(ang).astype(f32), np.sin(ang).astype(f32)
    rope = np.stack([np.concatenate([cos, cos], -1), np.concatenate([-sin, sin], -1)], 1)
    rope = rope.transpose(2, 0, 1, 3).reshape(P, -1)
    wg = np.zeros((P, P), f32)
    for h in range(H):
        wg[HD * h:HD * h + HD, HD * h:HD * h + HD] = a["L0_ffn_Wg"]
    d_g = np.concatenate([
        wq, a["L0_ffn_Wk"], a["L0_ffn_Wv"], rows(bq), rows(a["L0_ffn_bk"]), rows(a["L0_ffn_bv"]), rope,
        rows(np.concatenate([np.tile(a["L0_ffn_qn_w"], 16), np.tile(a["L0_ffn_kn_w"], 4)])),
        wg, rows(np.tile(a["L0_ffn_bg"], H)), wo, rows(a["L0_ffn_bo"]), a["L0_ffn_Wr"], rows(a["L0_ffn_br"]),
        rows(np.arange(NE, 0, -1).astype(f32))], 1)
    col = np.stack([a["L0_xattn_g1"], a["L0_xattn_b1"], a["L0_xattn_g2"], a["L0_xattn_b2"], a["L0_ffn_ln1_w"],
                    a["L0_ffn_ln2_w"], np.full(P, 1e-5, f32), np.full(P, 1e-6, f32)], 1)
    arrays = {
        "d_a": d_a, "d_x": tiles(x), "d_ctx": tiles(a["ctx_1024"].reshape(B * SC, D)), "d_cols": col,
        "d_wkv": a["L0_xattn_Wkv"], "d_wq": a["L0_xattn_Wq"], "d_wout": tiles(a["L0_xattn_Wout"]), "d_g": d_g,
        "d_we1": a["L0_ffn_W1"].transpose(1, 0, 2).reshape(D, -1),
        "d_we2": a["L0_ffn_W2"].reshape(NE, 2, P, D).transpose(2, 1, 0, 3).reshape(P, -1),
        "d_be": np.concatenate([a["L0_ffn_b1"], a["L0_ffn_b2"]], 1),
    }
    arrays = {k: np.ascontiguousarray(v) for k, v in arrays.items()}
    nc = bacc.Bacc("TRN2", target_bir_lowering=False, num_devices=1)
    args = [nc.dram_tensor(k, v.shape, mb.dt.from_np(v.dtype), kind="ExternalInput").ap() for k, v in arrays.items()]
    out = nc.dram_tensor("d_out", (P, NT * D), mb.dt.from_np(np.dtype(f32)), kind="ExternalOutput").ap()
    decoder_layer(nc, *args, out)
    r = run_bass_kernel_spmd(nc, [arrays], core_ids=[0])
    y = r.results[0]["d_out"]
    return y.reshape(P, NT, D).transpose(1, 0, 2).reshape(B, S, D)
```
